# Optimizing a Trainium2 kernel written in Bass

```python
import numpy as np
import jax
import jax.numpy as jnp

def _softmax(x, axis=-1):
    return jax.nn.softmax(x, axis=axis)

def _gelu(x):
    return jax.nn.gelu(x, approximate=True)

def _silu(x):
    return jax.nn.silu(x)

def _sigmoid(x):
    return jax.nn.sigmoid(x)

def _layernorm(x, axis=-1, eps=1e-05):
    m = jnp.mean(x, axis=axis, keepdims=True)
    v = jnp.var(x, axis=axis, keepdims=True)
    return (x - m) / jnp.sqrt(v + eps)

def _scatter_add(tgt, idx, src, axis=0):
    return tgt.at[idx].add(src)

def _segment_sum(src, seg, n):
    return jax.ops.segment_sum(src, seg, n)
kernel_name = 'mk_hybrid_d2_jaxref_r8_d5caa0'

def setup_inputs(seed: int=0):
    np.random.seed(seed)
    _w = jnp.asarray

    def _L0_attn_a_setup():
        import jax, jax.numpy as jnp
        import numpy as np
        D_MODEL = 128
        N_HEADS = 16
        HEAD_DIM = D_MODEL // N_HEADS
        D_LATENT = 32
        LAMBDA_DECAY = 0.01
        TIME_STEP = 0.01
        CLAMP = 10000.0

        def _reference_tuple_inner(x, Wq, Wk, Wv, Wo, W_down_kv, W_up_k, W_up_v):
            B, S, _ = x.shape
            q = x @ Wq
            k = x @ Wk
            v = x @ Wv
            latent_kv = (k + v) @ W_down_kv
            k_rec = latent_kv @ W_up_k
            v_rec = latent_kv @ W_up_v

            def heads(t):
                return t.reshape(B, S, N_HEADS, HEAD_DIM).transpose(0, 2, 1, 3)
            qh, kh, vh = (heads(q), heads(k_rec), heads(v_rec))
            scale = 1.0 / (jnp.sqrt(jnp.float32(D_MODEL)) + 1e-08)
            scores = jnp.einsum('bhqd,bhkd->bhqk', qh, kh) * scale
            scores = jnp.clip(jnp.nan_to_num(scores, nan=-1000000000.0), -CLAMP, CLAMP)
            idx = jnp.arange(S, dtype=jnp.float32)
            decay = jnp.exp(-LAMBDA_DECAY * TIME_STEP * jnp.abs(idx[:, None] - idx[None, :]))
            scores = scores * decay[None, None, :, :]
            scores = jnp.clip(jnp.nan_to_num(scores, nan=-1000000000.0), -CLAMP, CLAMP)
            attn = jax.nn.softmax(scores, axis=-1)
            out = jnp.einsum('bhqk,bhkd->bhqd', attn, vh)
            out = out.transpose(0, 2, 1, 3).reshape(B, S, D_MODEL)
            return (out @ Wo, latent_kv)
        key = jax.random.key(seed)
        ks = jax.random.split(key, 8)
        B, S = (2, 256)

        def w(k, i, o):
            return jax.random.normal(k, (i, o), dtype=jnp.float32) * 0.02
        return {'x': jax.random.normal(ks[0], (B, S, D_MODEL), dtype=jnp.float32), 'Wq': w(ks[1], D_MODEL, D_MODEL), 'Wk': w(ks[2], D_MODEL, D_MODEL), 'Wv': w(ks[3], D_MODEL, D_MODEL), 'Wo': w(ks[4], D_MODEL, D_MODEL), 'W_down_kv': w(ks[5], D_MODEL, D_LATENT), 'W_up_k': w(ks[6], D_LATENT, D_MODEL), 'W_up_v': w(ks[7], D_LATENT, D_MODEL)}
    _L0_attn_a_in = _L0_attn_a_setup()

    def _L0_attn_b_setup():
        import jax, jax.numpy as jnp
        import numpy as np
        HEADS = 32
        DIM_HEAD = 32
        EPS = 1e-06
        key = jax.random.key(seed)
        k1, k2, k3 = jax.random.split(key, 3)
        b, n, dim = (2, 256, 128)
        x = jax.random.normal(k1, (b, n, dim), dtype=jnp.float32)
        w_qkv = jax.random.normal(k2, (dim, 3 * HEADS * DIM_HEAD), dtype=jnp.float32) * dim ** (-0.5)
        w_out = jax.random.normal(k3, (HEADS * DIM_HEAD, dim), dtype=jnp.float32) * dim ** (-0.5)
        b_out = jnp.zeros((dim,), dtype=jnp.float32)
        ln_gamma = jnp.ones((dim,), dtype=jnp.float32)
        ln_beta = jnp.zeros((dim,), dtype=jnp.float32)
        return {'x': x, 'w_qkv': w_qkv, 'w_out': w_out, 'b_out': b_out, 'ln_gamma': ln_gamma, 'ln_beta': ln_beta}
    _L0_attn_b_in = _L0_attn_b_setup()

    def _L0_ffn_setup():
        import jax, jax.numpy as jnp
        import numpy as np
        H = 128
        DFF = 512
        E_ROUTED = 7
        TOP_K = 2

        def _swiglu(flat, gate_w, up_w, down_w):
            g = flat @ gate_w.T
            up = flat @ up_w.T
            return jax.nn.silu(g) * up @ down_w.T
        key = jax.random.key(seed)
        ks = jax.random.split(key, 8)
        s = 0.02
        return {'x': jax.random.normal(ks[0], (4, 256, H), jnp.float32), 'shared_up': jax.random.normal(ks[1], (DFF, H), jnp.float32) * s, 'shared_gate': jax.random.normal(ks[2], (DFF, H), jnp.float32) * s, 'shared_down': jax.random.normal(ks[3], (H, DFF), jnp.float32) * s, 'routed_up': jax.random.normal(ks[4], (E_ROUTED, DFF, H), jnp.float32) * s, 'routed_gate': jax.random.normal(ks[5], (E_ROUTED, DFF, H), jnp.float32) * s, 'routed_down': jax.random.normal(ks[6], (E_ROUTED, H, DFF), jnp.float32) * s, 'router_w': jax.random.normal(ks[7], (E_ROUTED, H), jnp.float32) * 0.02}
    _L0_ffn_in = _L0_ffn_setup()

    def _L1_attn_a_setup():
        import jax, jax.numpy as jnp
        import numpy as np
        DIM = 128
        HEADS = 16
        HEAD_DIM = DIM // HEADS
        NUM_FILTERS = 4
        NUM_TAPS = 101
        RES = 64

        def _fir_fft(c, sig):
            R = sig.shape[0]
            L = R + c.shape[0] - 1
            out = jnp.fft.ifft(jnp.fft.fft(sig, n=L) * jnp.fft.fft(c, n=L)).real
            return out[:R]
        key = jax.random.key(seed)
        ks = jax.random.split(key, 5)
        B, S = (2, 256)
        x = jax.random.normal(ks[0], (B, S, DIM), dtype=jnp.float32)
        Wqkv = jax.random.normal(ks[1], (3 * DIM, DIM), dtype=jnp.float32) * DIM ** (-0.5)
        Wout = jax.random.normal(ks[2], (DIM, DIM), dtype=jnp.float32) * DIM ** (-0.5)
        Wpos = jax.random.normal(ks[3], (HEADS, NUM_FILTERS), dtype=jnp.float32) * 0.5
        coeffs = jax.random.normal(ks[4], (NUM_FILTERS, NUM_TAPS), dtype=jnp.float32) * 0.05
        return {'x': x, 'Wqkv': Wqkv, 'Wout': Wout, 'Wpos': Wpos, 'coeffs': coeffs}
    _L1_attn_a_in = _L1_attn_a_setup()

    def _L1_attn_b_setup():
        import jax, jax.numpy as jnp
        import numpy as np
        H = 128
        NH = 32
        D = H // NH
        M = 2
        BMIN, BMAX = (0.85, 0.9995)
        EPS = 1e-06
        ROPE_BASE = 10000.0
        LN_EPS = 1e-05

        def _rope(u, cos, sin):
            half = D // 2
            u1, u2 = (u[..., :half], u[..., half:])
            return jnp.concatenate([u1 * cos - u2 * sin, u1 * sin + u2 * cos], axis=-1)

        def _forward(x, Wq, Wk, Wv, Wbeta, bbeta, Wmix, bmix, Wout, bout, ln_g, ln_b):
            b, t, _ = x.shape
            q = (x @ Wq.T).reshape(b, t, NH, D)
            k = (x @ Wk.T).reshape(b, t, NH, D)
            v = (x @ Wv.T).reshape(b, t, NH, D)
            half = D // 2
            inv_freq = 1.0 / ROPE_BASE ** (jnp.arange(half, dtype=jnp.float32) / half)
            freqs = jnp.arange(t, dtype=jnp.float32)[:, None] * inv_freq
            cos = jnp.cos(freqs)[None, :, None, :]
            sin = jnp.sin(freqs)[None, :, None, :]
            q = _rope(q, cos, sin)
            k = _rope(k, cos, sin)
            phi_q = jax.nn.elu(q) + 1.0
            phi_k = jax.nn.elu(k) + 1.0
            beta = jnp.clip(jax.nn.sigmoid((x @ Wbeta.T + bbeta).reshape(b, t, NH, M)), BMIN, BMAX)
            mix = jax.nn.softmax((x @ Wmix.T + bmix).reshape(b, t, NH, M), axis=-1)

            def step(carry, xs):
                S, K = carry
                pq, pk, vt, bt, mt = xs
                K = K * bt[..., None] + pk[:, :, None, :]
                S = S * bt[..., None, None] + pk[:, :, None, :, None] * vt[:, :, None, None, :]
                num = jnp.einsum('bhd,bhmdc->bhmc', pq, S)
                den = jnp.einsum('bhd,bhmd->bhm', pq, K) + EPS
                y = jnp.sum(num / den[..., None] * mt[..., None], axis=2)
                return ((S, K), y)
            S0 = jnp.zeros((b, NH, M, D, D), x.dtype)
            K0 = jnp.zeros((b, NH, M, D), x.dtype)
            tf = lambda a: jnp.moveaxis(a, 1, 0)
            _, ys = jax.lax.scan(step, (S0, K0), (tf(phi_q), tf(phi_k), tf(v), tf(beta), tf(mix)))
            y = jnp.moveaxis(ys, 0, 1).reshape(b, t, H) @ Wout.T + bout
            z = x + y
            mu = z.mean(-1, keepdims=True)
            var = ((z - mu) ** 2).mean(-1, keepdims=True)
            return (z - mu) / jnp.sqrt(var + LN_EPS) * ln_g + ln_b
        key = jax.random.key(seed)
        ks = jax.random.split(key, 8)
        b, t = (4, 128)
        x = jax.random.normal(ks[0], (b, t, H), jnp.float32)
        sc = (6.0 / (H + H)) ** 0.5
        Wq = jax.random.uniform(ks[1], (H, H), jnp.float32, -sc, sc)
        Wk = jax.random.uniform(ks[2], (H, H), jnp.float32, -sc, sc)
        Wv = jax.random.uniform(ks[3], (H, H), jnp.float32, -sc, sc)
        Wout = jax.random.uniform(ks[4], (H, H), jnp.float32, -sc, sc)
        bout = jnp.zeros((H,), jnp.float32)
        scb = (6.0 / (H + NH * M)) ** 0.5
        Wbeta = jax.random.uniform(ks[5], (NH * M, H), jnp.float32, -scb, scb)
        targets = jnp.linspace(BMIN, BMAX, M)
        bbeta = jnp.tile(jnp.log(targets / (1.0 - targets)), NH)
        Wmix = jnp.zeros((NH * M, H), jnp.float32)
        bmix = jnp.zeros((NH * M,), jnp.float32)
        ln_g = jnp.ones((H,), jnp.float32)
        ln_b = jnp.zeros((H,), jnp.float32)
        return dict(x=x, Wq=Wq, Wk=Wk, Wv=Wv, Wbeta=Wbeta, bbeta=bbeta, Wmix=Wmix, bmix=bmix, Wout=Wout, bout=bout, ln_g=ln_g, ln_b=ln_b)
    _L1_attn_b_in = _L1_attn_b_setup()

    def _L1_ffn_setup():
        import jax, jax.numpy as jnp
        import numpy as np
        DIM = 128
        HIDDEN = 384
        SCALE = 1.0 / 127.0

        def _dequant(w_int, dtype):
            return w_int.astype(dtype) * jnp.asarray(SCALE, dtype)
        key = jax.random.key(seed)
        k_x, k_g, k_u, k_d = jax.random.split(key, 4)
        x = jax.random.normal(k_x, (4, 256, DIM), dtype=jnp.float32)
        w_gate = jax.random.randint(k_g, (HIDDEN, DIM), -127, 128, dtype=jnp.int32)
        w_up = jax.random.randint(k_u, (HIDDEN, DIM), -127, 128, dtype=jnp.int32)
        w_down = jax.random.randint(k_d, (DIM, HIDDEN), -127, 128, dtype=jnp.int32)
        return {'x': x, 'w_gate': w_gate, 'w_up': w_up, 'w_down': w_down}
    _L1_ffn_in = _L1_ffn_setup()
    _d = {'L0_attn_a_x': _L0_attn_a_in['x'], 'L0_attn_a_Wq': _L0_attn_a_in['Wq'], 'L0_attn_a_Wk': _L0_attn_a_in['Wk'], 'L0_attn_a_Wv': _L0_attn_a_in['Wv'], 'L0_attn_a_Wo': _L0_attn_a_in['Wo'], 'L0_attn_a_W_down_kv': _L0_attn_a_in['W_down_kv'], 'L0_attn_a_W_up_k': _L0_attn_a_in['W_up_k'], 'L0_attn_a_W_up_v': _L0_attn_a_in['W_up_v'], 'L0_attn_b_w_qkv': _L0_attn_b_in['w_qkv'], 'L0_attn_b_w_out': _L0_attn_b_in['w_out'], 'L0_attn_b_b_out': _L0_attn_b_in['b_out'], 'L0_attn_b_ln_gamma': _L0_attn_b_in['ln_gamma'], 'L0_attn_b_ln_beta': _L0_attn_b_in['ln_beta'], 'L0_ffn_shared_up': _L0_ffn_in['shared_up'], 'L0_ffn_shared_gate': _L0_ffn_in['shared_gate'], 'L0_ffn_shared_down': _L0_ffn_in['shared_down'], 'L0_ffn_routed_up': _L0_ffn_in['routed_up'], 'L0_ffn_routed_gate': _L0_ffn_in['routed_gate'], 'L0_ffn_routed_down': _L0_ffn_in['routed_down'], 'L0_ffn_router_w': _L0_ffn_in['router_w'], 'L1_attn_a_Wqkv': _L1_attn_a_in['Wqkv'], 'L1_attn_a_Wout': _L1_attn_a_in['Wout'], 'L1_attn_a_Wpos': _L1_attn_a_in['Wpos'], 'L1_attn_a_coeffs': _L1_attn_a_in['coeffs'], 'L1_attn_b_Wq': _L1_attn_b_in['Wq'], 'L1_attn_b_Wk': _L1_attn_b_in['Wk'], 'L1_attn_b_Wv': _L1_attn_b_in['Wv'], 'L1_attn_b_Wbeta': _L1_attn_b_in['Wbeta'], 'L1_attn_b_bbeta': _L1_attn_b_in['bbeta'], 'L1_attn_b_Wmix': _L1_attn_b_in['Wmix'], 'L1_attn_b_bmix': _L1_attn_b_in['bmix'], 'L1_attn_b_Wout': _L1_attn_b_in['Wout'], 'L1_attn_b_bout': _L1_attn_b_in['bout'], 'L1_attn_b_ln_g': _L1_attn_b_in['ln_g'], 'L1_attn_b_ln_b': _L1_attn_b_in['ln_b'], 'L1_ffn_w_gate': _L1_ffn_in['w_gate'], 'L1_ffn_w_up': _L1_ffn_in['w_up'], 'L1_ffn_w_down': _L1_ffn_in['w_down']}
    _x0 = _d['L0_attn_a_x']
    _d['L0_attn_a_x'] = jax.random.normal(jax.random.fold_in(jax.random.key(seed), 1), (8, 512, 128), dtype=_x0.dtype)
    del _x0
    return _d

def reference(L0_attn_a_x, L0_attn_a_Wq, L0_attn_a_Wk, L0_attn_a_Wv, L0_attn_a_Wo, L0_attn_a_W_down_kv, L0_attn_a_W_up_k, L0_attn_a_W_up_v, L0_attn_b_w_qkv, L0_attn_b_w_out, L0_attn_b_b_out, L0_attn_b_ln_gamma, L0_attn_b_ln_beta, L0_ffn_shared_up, L0_ffn_shared_gate, L0_ffn_shared_down, L0_ffn_routed_up, L0_ffn_routed_gate, L0_ffn_routed_down, L0_ffn_router_w, L1_attn_a_Wqkv, L1_attn_a_Wout, L1_attn_a_Wpos, L1_attn_a_coeffs, L1_attn_b_Wq, L1_attn_b_Wk, L1_attn_b_Wv, L1_attn_b_Wbeta, L1_attn_b_bbeta, L1_attn_b_Wmix, L1_attn_b_bmix, L1_attn_b_Wout, L1_attn_b_bout, L1_attn_b_ln_g, L1_attn_b_ln_b, L1_ffn_w_gate, L1_ffn_w_up, L1_ffn_w_down):

    def _L0_attn_a_ref(x, Wq, Wk, Wv, Wo, W_down_kv, W_up_k, W_up_v):
        import jax, jax.numpy as jnp
        import numpy as np
        D_MODEL = 128
        N_HEADS = 16
        HEAD_DIM = D_MODEL // N_HEADS
        D_LATENT = 32
        LAMBDA_DECAY = 0.01
        TIME_STEP = 0.01
        CLAMP = 10000.0

        def _reference_tuple_inner(x, Wq, Wk, Wv, Wo, W_down_kv, W_up_k, W_up_v):
            B, S, _ = x.shape
            q = x @ Wq
            k = x @ Wk
            v = x @ Wv
            latent_kv = (k + v) @ W_down_kv
            k_rec = latent_kv @ W_up_k
            v_rec = latent_kv @ W_up_v

            def heads(t):
                return t.reshape(B, S, N_HEADS, HEAD_DIM).transpose(0, 2, 1, 3)
            qh, kh, vh = (heads(q), heads(k_rec), heads(v_rec))
            scale = 1.0 / (jnp.sqrt(jnp.float32(D_MODEL)) + 1e-08)
            scores = jnp.einsum('bhqd,bhkd->bhqk', qh, kh) * scale
            scores = jnp.clip(jnp.nan_to_num(scores, nan=-1000000000.0), -CLAMP, CLAMP)
            idx = jnp.arange(S, dtype=jnp.float32)
            decay = jnp.exp(-LAMBDA_DECAY * TIME_STEP * jnp.abs(idx[:, None] - idx[None, :]))
            scores = scores * decay[None, None, :, :]
            scores = jnp.clip(jnp.nan_to_num(scores, nan=-1000000000.0), -CLAMP, CLAMP)
            attn = jax.nn.softmax(scores, axis=-1)
            out = jnp.einsum('bhqk,bhkd->bhqd', attn, vh)
            out = out.transpose(0, 2, 1, 3).reshape(B, S, D_MODEL)
            return (out @ Wo, latent_kv)
        return _reference_tuple_inner(x, Wq, Wk, Wv, Wo, W_down_kv, W_up_k, W_up_v)[0]

    def _L0_attn_b_ref(x, w_qkv, w_out, b_out, ln_gamma, ln_beta):
        import jax, jax.numpy as jnp
        import numpy as np
        HEADS = 32
        DIM_HEAD = 32
        EPS = 1e-06
        b, n, dim = x.shape
        scale = DIM_HEAD ** (-0.5)
        qkv = x @ w_qkv
        qkv = qkv.reshape(b, n, 3, HEADS, DIM_HEAD)
        qkv = jnp.transpose(qkv, (2, 0, 3, 1, 4))
        q, k, v = (qkv[0], qkv[1], qkv[2])
        dots = jnp.einsum('bhnd,bhmd->bhnm', q, k) * scale
        attn = jax.nn.softmax(dots, axis=-1)
        out = jnp.einsum('bhnm,bhmd->bhnd', attn, v)
        out = jnp.transpose(out, (0, 2, 1, 3)).reshape(b, n, HEADS * DIM_HEAD)
        out = out @ w_out + b_out
        mu = jnp.mean(out, axis=-1, keepdims=True)
        var = jnp.mean((out - mu) ** 2, axis=-1, keepdims=True)
        out = (out - mu) / jnp.sqrt(var + EPS) * ln_gamma + ln_beta
        return out

    def _L0_ffn_ref(x, shared_up, shared_gate, shared_down, routed_up, routed_gate, routed_down, router_w):
        import jax, jax.numpy as jnp
        import numpy as np
        H = 128
        DFF = 512
        E_ROUTED = 7
        TOP_K = 2

        def _swiglu(flat, gate_w, up_w, down_w):
            g = flat @ gate_w.T
            up = flat @ up_w.T
            return jax.nn.silu(g) * up @ down_w.T
        orig_shape = x.shape
        flat = x.reshape(-1, H)
        out = _swiglu(flat, shared_gate, shared_up, shared_down)
        logits = flat @ router_w.T
        probs = jax.nn.softmax(logits, axis=-1)
        top_vals, top_idx = jax.lax.top_k(probs, TOP_K)
        top_vals = top_vals / (top_vals.sum(-1, keepdims=True) + 1e-09)
        combine = jnp.sum(jax.nn.one_hot(top_idx, E_ROUTED, dtype=flat.dtype) * top_vals[..., None], axis=1)
        routed = jnp.zeros_like(flat)
        for e in range(E_ROUTED):
            eo = _swiglu(flat, routed_gate[e], routed_up[e], routed_down[e])
            routed = routed + combine[:, e:e + 1] * eo
        return (out + routed).reshape(orig_shape)

    def _L1_attn_a_ref(x, Wqkv, Wout, Wpos, coeffs):
        import jax, jax.numpy as jnp
        import numpy as np
        DIM = 128
        HEADS = 16
        HEAD_DIM = DIM // HEADS
        NUM_FILTERS = 4
        NUM_TAPS = 101
        RES = 64

        def _fir_fft(c, sig):
            R = sig.shape[0]
            L = R + c.shape[0] - 1
            out = jnp.fft.ifft(jnp.fft.fft(sig, n=L) * jnp.fft.fft(c, n=L)).real
            return out[:R]
        B, S, D = x.shape
        scale = HEAD_DIM ** (-0.5)
        proto = jnp.linspace(0.0, 1.0, RES).astype(x.dtype)
        table = jax.vmap(_fir_fft, in_axes=(0, None))(coeffs, proto).T
        r = jnp.arange(S)
        rel = jnp.abs(r[None, :] - r[:, None]).astype(jnp.float32) / max(S - 1, 1)
        idx = jnp.clip(jnp.round(rel * (RES - 1)).astype(jnp.int32), 0, RES - 1)
        pos_feat = table[idx]
        pos_bias = jnp.einsum('ijf,hf->hij', pos_feat, Wpos)
        qkv = jnp.einsum('bsd,ed->bse', x, Wqkv)
        q, k, v = jnp.split(qkv, 3, axis=-1)
        q = q.reshape(B, S, HEADS, HEAD_DIM)
        k = k.reshape(B, S, HEADS, HEAD_DIM)
        v = v.reshape(B, S, HEADS, HEAD_DIM)
        logits = jnp.einsum('bihd,bjhd->bhij', q, k) * scale + pos_bias[None]
        attn = jax.nn.softmax(logits, axis=-1)
        out = jnp.einsum('bhij,bjhd->bihd', attn, v).reshape(B, S, D)
        return jnp.einsum('bsd,ed->bse', out, Wout)

    def _L1_attn_b_ref(x, Wq, Wk, Wv, Wbeta, bbeta, Wmix, bmix, Wout, bout, ln_g, ln_b):
        import jax, jax.numpy as jnp
        import numpy as np
        H = 128
        NH = 32
        D = H // NH
        M = 2
        BMIN, BMAX = (0.85, 0.9995)
        EPS = 1e-06
        ROPE_BASE = 10000.0
        LN_EPS = 1e-05

        def _rope(u, cos, sin):
            half = D // 2
            u1, u2 = (u[..., :half], u[..., half:])
            return jnp.concatenate([u1 * cos - u2 * sin, u1 * sin + u2 * cos], axis=-1)

        def _forward(x, Wq, Wk, Wv, Wbeta, bbeta, Wmix, bmix, Wout, bout, ln_g, ln_b):
            b, t, _ = x.shape
            q = (x @ Wq.T).reshape(b, t, NH, D)
            k = (x @ Wk.T).reshape(b, t, NH, D)
            v = (x @ Wv.T).reshape(b, t, NH, D)
            half = D // 2
            inv_freq = 1.0 / ROPE_BASE ** (jnp.arange(half, dtype=jnp.float32) / half)
            freqs = jnp.arange(t, dtype=jnp.float32)[:, None] * inv_freq
            cos = jnp.cos(freqs)[None, :, None, :]
            sin = jnp.sin(freqs)[None, :, None, :]
            q = _rope(q, cos, sin)
            k = _rope(k, cos, sin)
            phi_q = jax.nn.elu(q) + 1.0
            phi_k = jax.nn.elu(k) + 1.0
            beta = jnp.clip(jax.nn.sigmoid((x @ Wbeta.T + bbeta).reshape(b, t, NH, M)), BMIN, BMAX)
            mix = jax.nn.softmax((x @ Wmix.T + bmix).reshape(b, t, NH, M), axis=-1)

            def step(carry, xs):
                S, K = carry
                pq, pk, vt, bt, mt = xs
                K = K * bt[..., None] + pk[:, :, None, :]
                S = S * bt[..., None, None] + pk[:, :, None, :, None] * vt[:, :, None, None, :]
                num = jnp.einsum('bhd,bhmdc->bhmc', pq, S)
                den = jnp.einsum('bhd,bhmd->bhm', pq, K) + EPS
                y = jnp.sum(num / den[..., None] * mt[..., None], axis=2)
                return ((S, K), y)
            S0 = jnp.zeros((b, NH, M, D, D), x.dtype)
            K0 = jnp.zeros((b, NH, M, D), x.dtype)
            tf = lambda a: jnp.moveaxis(a, 1, 0)
            _, ys = jax.lax.scan(step, (S0, K0), (tf(phi_q), tf(phi_k), tf(v), tf(beta), tf(mix)))
            y = jnp.moveaxis(ys, 0, 1).reshape(b, t, H) @ Wout.T + bout
            z = x + y
            mu = z.mean(-1, keepdims=True)
            var = ((z - mu) ** 2).mean(-1, keepdims=True)
            return (z - mu) / jnp.sqrt(var + LN_EPS) * ln_g + ln_b
        return _forward(x, Wq, Wk, Wv, Wbeta, bbeta, Wmix, bmix, Wout, bout, ln_g, ln_b)

    def _L1_ffn_ref(x, w_gate, w_up, w_down):
        import jax, jax.numpy as jnp
        import numpy as np
        DIM = 128
        HIDDEN = 384
        SCALE = 1.0 / 127.0

        def _dequant(w_int, dtype):
            return w_int.astype(dtype) * jnp.asarray(SCALE, dtype)
        wg = _dequant(w_gate, x.dtype)
        wu = _dequant(w_up, x.dtype)
        wd = _dequant(w_down, x.dtype)
        gate = jnp.einsum('bsd,hd->bsh', x, wg)
        up = jnp.einsum('bsd,hd->bsh', x, wu)
        h = jax.nn.silu(gate) * up
        return jnp.einsum('bsh,dh->bsd', h, wd)
    x = L0_attn_a_x
    x = x + _L0_attn_a_ref(_layernorm(x, axis=-1), L0_attn_a_Wq, L0_attn_a_Wk, L0_attn_a_Wv, L0_attn_a_Wo, L0_attn_a_W_down_kv, L0_attn_a_W_up_k, L0_attn_a_W_up_v)
    x = x + _L0_ffn_ref(_layernorm(x, axis=-1), L0_ffn_shared_up, L0_ffn_shared_gate, L0_ffn_shared_down, L0_ffn_routed_up, L0_ffn_routed_gate, L0_ffn_routed_down, L0_ffn_router_w)
    x = x + _L0_attn_b_ref(_layernorm(x, axis=-1), L0_attn_b_w_qkv, L0_attn_b_w_out, L0_attn_b_b_out, L0_attn_b_ln_gamma, L0_attn_b_ln_beta)
    x = x + _L0_ffn_ref(_layernorm(x, axis=-1), L0_ffn_shared_up, L0_ffn_shared_gate, L0_ffn_shared_down, L0_ffn_routed_up, L0_ffn_routed_gate, L0_ffn_routed_down, L0_ffn_router_w)
    x = x + _L1_attn_a_ref(_layernorm(x, axis=-1), L1_attn_a_Wqkv, L1_attn_a_Wout, L1_attn_a_Wpos, L1_attn_a_coeffs)
    x = x + _L1_ffn_ref(_layernorm(x, axis=-1), L1_ffn_w_gate, L1_ffn_w_up, L1_ffn_w_down)
    x = x + _L1_attn_b_ref(_layernorm(x, axis=-1), L1_attn_b_Wq, L1_attn_b_Wk, L1_attn_b_Wv, L1_attn_b_Wbeta, L1_attn_b_bbeta, L1_attn_b_Wmix, L1_attn_b_bmix, L1_attn_b_Wout, L1_attn_b_bout, L1_attn_b_ln_g, L1_attn_b_ln_b)
    x = x + _L1_ffn_ref(_layernorm(x, axis=-1), L1_ffn_w_gate, L1_ffn_w_up, L1_ffn_w_down)
    return x

_drawn_inputs = setup_inputs


def setup_inputs(seed=0):
    import zlib

    import numpy as np

    out = dict(_drawn_inputs(seed))
    spreads = {'L0_attn_b_b_out': (0.0, 0.1),
     'L0_attn_b_ln_gamma': (1.0, 0.2),
     'L0_attn_b_ln_beta': (0.0, 0.1),
     'L1_attn_b_Wmix': (0.0, 2.0),
     'L1_attn_b_bmix': (0.0, 2.0),
     'L1_attn_b_bout': (0.0, 2.0),
     'L1_attn_b_ln_g': (1.0, 0.6),
     'L1_attn_b_ln_b': (0.0, 2.0)}
    factors = {'L0_attn_a_Wq': 8.0,
     'L0_attn_a_Wk': 8.0,
     'L0_attn_a_Wv': 8.0,
     'L0_attn_a_Wo': 8.0,
     'L0_attn_a_W_down_kv': 8.0,
     'L0_attn_a_W_up_k': 8.0,
     'L0_attn_a_W_up_v': 8.0,
     'L0_ffn_router_w': 25.952,
     'L1_attn_a_Wpos': 8.0,
     'L1_attn_a_coeffs': 23.931,
     'L1_attn_b_Wq': 200.0,
     'L1_attn_b_Wk': 200.0,
     'L1_attn_b_Wv': 200.0,
     'L1_attn_b_Wbeta': 200.0,
     'L1_attn_b_Wout': 200.0,
     'L0_ffn_shared_up': 4.738,
     'L0_ffn_shared_gate': 4.769,
     'L0_ffn_shared_down': 4.723,
     'L0_ffn_routed_up': 6.69,
     'L0_ffn_routed_gate': 6.698,
     'L0_ffn_routed_down': 6.669}
    for name, (base, spread) in spreads.items():
        noise = np.random.default_rng([zlib.crc32(name.encode()), seed]).standard_normal(out[name].shape)
        drawn = base * np.exp(spread * noise) if base else spread * noise
        out[name] = jnp.asarray(drawn.astype(out[name].dtype))
    for name, factor in factors.items():
        out[name] = (out[name] * factor).astype(out[name].dtype)
    return out
```

```python
from contextlib import ExitStack

import concourse.bass as bass
import numpy as np
from concourse import mybir

ALU = mybir.AluOpType
ACT = mybir.ActivationFunctionType
F32 = mybir.dt.float32
F32R = mybir.dt.float32r
I32 = mybir.dt.int32
AX_X = mybir.AxisListType.X

P = 128
B, S, DM = 8, 512, 128
TB = S // P
TILES = B * TB
HG = 4
KROWS = 96
CLAMP = 10000.0
STRIP = S + (TB - 1) * P
STRIP0 = (TB - 1) * P
EXPERTS, DFF = 8, 512
HID = 384


class Phase:

    def __init__(self, nc, name):
        self.nc, self.name = nc, name

    def __enter__(self):
        self.stack = ExitStack().__enter__()
        self.sems = []
        return self

    def sb(self, name, shape, dt=F32):
        return self.stack.enter_context(self.nc.sbuf_tensor(f"{self.name}_{name}", shape, dt))

    def sem(self, name):
        s = self.stack.enter_context(self.nc.semaphore(f"{self.name}_{name}"))
        self.sems.append(s)
        return s

    def __exit__(self, *exc):
        if exc[0] is None:
            for s in self.sems:
                self.nc.sync.sem_clear(s)
            self.nc.all_engine_barrier()
        return self.stack.__exit__(*exc)


def wait(eng, sem, value):
    if isinstance(value, int) and value <= 0:
        return
    eng.wait_ge(sem, value)


def settle(eng, sem):
    eng.sem_inc(sem, 1)


class Link:

    def __init__(self, eng, sem, n, k):
        self.eng, self.sem, self.n, self.k, self.done = eng, sem, n, k, 0

    def __call__(self, ins):
        self.done += 1
        assert self.done <= self.k
        ins.then_inc(self.sem, 1)
        self.eng.wait_ge(self.sem, self.k * (self.n - 1) + self.done)


class Step:

    def __init__(self, i, c, count, U=4):
        self.i, self.c, self.count, self.U = i, c, count, U

    def has(self, k):
        return not isinstance(self.i, int) or 1 <= self.U * self.i + self.c - k <= self.count

    def n(self, k):
        return self.U * self.i + (self.c - k)

    def slot(self, k, ring):
        return (self.c - k) % ring

    def use(self, k, ring):
        return self.U // ring * self.i + (self.c - k + ring - 1) // ring


def run_steps(eng, count, extra, step, U=4):
    peeled = max(1, -(-extra // U))
    for i in range(peeled):
        for c in range(1, U + 1):
            step(Step(i, c, count, U))
    with eng.Fori(peeled, count // U) as i:
        for c in range(1, U + 1):
            step(Step(i, c, count, U))
    for c in range(1, extra + 1):
        step(Step(count // U, c, count, U))


RSQRT_LINKS = 12


def rsqrt(dve, link, var, eps, y, t):
    y_bits, t_bits = y.bitcast(I32), t.bitcast(I32)
    link(dve.tensor_scalar(var, var, eps, None, ALU.add))
    link(dve.tensor_scalar(t_bits, var.bitcast(I32), 1, None, ALU.logical_shift_right))
    link(dve.tensor_scalar(y_bits, t_bits, -1.0, float(0x5F3759DF), ALU.mult, ALU.add))
    for _ in range(3):
        link(dve.tensor_tensor(t, y, y, ALU.mult))
        link(dve.scalar_tensor_tensor(t, t, -0.5, var, ALU.mult, ALU.mult))
        link(dve.scalar_tensor_tensor(y, t, 1.5, y, ALU.add, ALU.mult))


def row_stats(nc, name, x_all, mean_var, rstd, eps):
    with Phase(nc, name) as ph:
        stats = ph.sb("stats", [P, TILES, 6])
        t = ph.sb("t", [P, TILES])
        var = ph.sb("var", [P, TILES])
        stats_done, aggr_done, chain = ph.sem("stats_done"), ph.sem("aggr_done"), ph.sem("chain")
        with nc.Block() as block:
            @block.vector
            def _(dve):
                with dve.Fori(0, B) as b:
                    for tb in range(TB):
                        tile = b * TB + tb
                        dve.bn_stats(stats[:, bass.ds(tile, 1), :].rearrange("p a n -> p (a n)"),
                                     x_all[:, bass.ds(tile, 1), :].rearrange("p a n -> p (a n)")
                                     ).then_inc(stats_done, 1)
                dve.wait_ge(stats_done, TILES)
                for tile in range(TILES):
                    dve.bn_aggr(mean_var[:, tile, :], stats[:, tile, :]).then_inc(aggr_done, 1)
                dve.wait_ge(aggr_done, TILES)
                link = Link(dve, chain, 1, RSQRT_LINKS + 1)
                link(dve.tensor_copy(var[:], mean_var[:, :, 1]))
                rsqrt(dve, link, var[:], eps, rstd[:], t[:])


def normalise(dve, x_all, mean_var, rstd, n, xn, done):
    for tb in range(TB):
        tile = (n - 1) * TB + tb
        if isinstance(tile, int):
            x, m, r = x_all[:, tile, :], mean_var[:, tile, 0:1], rstd[:, tile:tile + 1]
        else:
            x = x_all[:, bass.ds(tile, 1), :].rearrange("p a n -> p (a n)")
            m = mean_var[:, bass.ds(tile, 1), 0:1].rearrange("p a n -> p (a n)")
            r = rstd[:, bass.ds(tile, 1)]
        dve.tensor_scalar(xn[:, tb, :], x, m, r, ALU.subtract, ALU.mult).then_inc(done, 1)


def batch_of(x_all, n):
    return x_all[:, bass.ds((n - 1) * TB, TB), :]


def item(dram, n):
    return dram[bass.ds(n - 1, 1)]


def project_small(nc, g, name, scale, latent, weights):
    with Phase(nc, name) as ph:
        n_w = len(weights)
        w = ph.sb("w", [P, n_w, DM])
        wd, wu = (ph.sb("wd", [P, 32]), ph.sb("wu", [32, 2, DM])) if latent else (None, None)
        xn = ph.sb("xn", [P, TB, DM])
        xT = ph.sb("xT", [P, S])
        kv = ph.sb("kv", [P, S])
        lat = ph.sb("lat", [32, S])
        hi = ph.sb("hi", [P, 2, S], F32R)
        lo = ph.sb("lo", [P, 2, S], F32R)
        va = ph.sb("va", [P, TB, 16, 32])
        w_loaded = ph.sem("w_loaded")
        ones_set = ph.sem("ones_set")
        xn_done, xn_free, xp_ready, xT_done, xT_free = (ph.sem(k) for k in ("xn_done", "xn_free", "xp_ready", "xT_done", "xT_free"))
        proj_done, hi_done, lo_done, v_done = (ph.sem(k) for k in ("proj_done", "hi_done", "lo_done", "v_done"))
        kv_ready, kv_done, lat_ready, lat_done = (ph.sem(k) for k in ("kv_ready", "kv_done", "lat_ready", "lat_done"))
        stored = ph.sem("stored")
        bank_x, bank_q, bank_k, bank_kv, bank_lat, bank_v = (g.ps[:, k, :] for k in range(6))
        n_loads = n_w + (3 if latent else 0)
        q_w = w[:, 0, :]

        with nc.Block() as block:
            @block.sync
            def _(sp):
                for k, src in enumerate(weights):
                    sp.dma_start(w[:, k, :], src).then_inc(w_loaded, 16)
                if latent:
                    for dst, src in zip((wd[:], wu[:, 0, :], wu[:, 1, :]), latent):
                        sp.dma_start(dst, src).then_inc(w_loaded, 16)
                with sp.Fori(1, B + 1) as n:
                    sp.wait_ge(lo_done, 2 * n)
                    for k, (dh, dl) in enumerate(((g.q_hi8, g.q_lo8), (g.k_hi8, g.k_lo8))):
                        sp.dma_start(dh[bass.ds((n - 1) * P, P), :], hi[:, k, :].bitcast(F32)).then_inc(stored, 16)
                        sp.dma_start(dl[bass.ds((n - 1) * P, P), :], lo[:, k, :].bitcast(F32)).then_inc(stored, 16)
                    sp.wait_ge(v_done, n)
                    for hg in range(4):
                        sp.dma_start(g.v8[bass.ds((n - 1) * 4 + hg, 1)].rearrange("a (t p) n -> p (a t) n", p=P),
                                     va[:, :, hg * HG:(hg + 1) * HG, :].rearrange("p t h d -> p t (h d)")
                                     ).then_inc(stored, 16)
                sp.wait_ge(stored, 16 * 8 * (B + 1))

            @block.vector
            def _(dve):
                dve.memset(va[:], 0.0).then_inc(ones_set, 1)
                dve.wait_ge(ones_set, 1)
                dve.memset(va[:, :, :, 8:9], 1.0).then_inc(ones_set, 1)
                dve.wait_ge(ones_set, 2)
                dve.sem_inc(xn_free, 1)
                dve.sem_inc(stored, 16 * 8)
                with dve.Fori(1, B + 1) as n:
                    dve.wait_ge(xn_free, n)
                    normalise(dve, g.x_all, g.mean_var, g.rstd, n, xn, xn_done)
                    for k, bank in enumerate((bank_q, bank_k)):
                        dve.wait_ge(hi_done, 2 * (n - 1) + k + 1)
                        dve.scalar_tensor_tensor(lo[:, k, :], bank, scale if k == 0 else 1.0, hi[:, k, :].bitcast(F32),
                                                 ALU.mult, ALU.subtract).then_inc(lo_done, 1)
                    dve.wait_ge(proj_done, 3 * n)
                    dve.wait_ge(stored, 16 * 8 * n)
                    dve.tensor_copy(va[:, :, :, 0:8], bank_v.rearrange("p (t h d) -> p t h d", t=TB, d=8)
                                    ).then_inc(v_done, 1)

            @block.scalar
            def _(act):
                act.sem_inc(xT_free, 1)
                with act.Fori(1, B + 1) as n:
                    act.wait_ge(xT_free, n)
                    act.wait_ge(xp_ready, n)
                    act.activation(xT[:], bank_x, ACT.Copy).then_inc(xT_done, 1)
                    if latent:
                        act.wait_ge(kv_ready, n)
                        act.activation(kv[:], bank_kv, ACT.Copy).then_inc(kv_done, 1)
                        act.wait_ge(lat_ready, n)
                        act.activation(lat[:], bank_lat[0:32, :], ACT.Copy).then_inc(lat_done, 1)
                    act.wait_ge(stored, 16 * 8 * n)
                    for k, bank in enumerate((bank_q, bank_k)):
                        act.wait_ge(proj_done, 3 * (n - 1) + k + 1)
                        act.activation(hi[:, k, :], bank, ACT.Copy,
                                       scale=scale if k == 0 else 1.0).then_inc(hi_done, 1)

            @block.tensor
            def _(pe):
                pe.wait_ge(w_loaded, 16 * n_loads)
                with pe.Fori(1, B + 1) as n:
                    pe.wait_ge(xn_done, TB * n)
                    for tb in range(TB):
                        ins = pe.transpose(bank_x[:, tb * P:(tb + 1) * P], xn[:, tb, :], g.ident[:])
                    ins.then_inc(xp_ready, 1)
                    pe.wait_ge(xT_done, n)
                    pe.sem_inc(xn_free, 1)
                    pe.matmul(bank_q, q_w, xT[:], start=True, stop=True).then_inc(proj_done, 1)
                    if latent:
                        pe.matmul(bank_kv, w[:, 1, :], xT[:], start=True, stop=False)
                        pe.matmul(bank_kv, w[:, 2, :], xT[:], start=False, stop=True).then_inc(kv_ready, 1)
                        pe.wait_ge(kv_done, n)
                        pe.matmul(bank_lat[0:32, :], wd[:], kv[:], start=True, stop=True).then_inc(lat_ready, 1)
                        pe.wait_ge(lat_done, n)
                        pe.matmul(bank_k, wu[:, 0, :], lat[:], start=True, stop=True).then_inc(proj_done, 1)
                        for tb in range(TB):
                            ins = pe.matmul(bank_v[:, tb * P:(tb + 1) * P], lat[:, tb * P:(tb + 1) * P],
                                            wu[:, 1, :], start=True, stop=True)
                    else:
                        pe.matmul(bank_k, w[:, 1, :], xT[:], start=True, stop=True).then_inc(proj_done, 1)
                        for tb in range(TB):
                            ins = pe.matmul(bank_v[:, tb * P:(tb + 1) * P], xT[:, tb * P:(tb + 1) * P],
                                            w[:, 2, :], start=True, stop=True)
                    ins.then_inc(proj_done, 1)
                    pe.wait_ge(v_done, n)
                    pe.wait_ge(lo_done, 2 * n)
                    pe.sem_inc(xT_free, 1)


def attend_small(nc, g, name, decay):
    NG = B * 4
    with Phase(nc, name) as ph:
        q4 = [ph.sb(f"q4_{r}", [P, HG, S], F32R) for r in range(2)]
        k4 = [ph.sb(f"k4_{r}", [P, HG, S], F32R) for r in range(2)]
        v4 = [ph.sb(f"v4_{r}", [P, TB, P]) for r in range(4)]
        strip = None if decay else [ph.sb(f"strip{r}", [P, HG, STRIP]) for r in range(2)]
        clipped = ph.sb("clipped", [P, 2, S]) if decay else None
        logits = ph.sb("logits", [P, 2, TB, S])
        top = ph.sb("top", [P, 2, TB])
        neg_top = ph.sb("neg_top", [P, 2, TB])
        e = ph.sb("e", [P, HG, TB, S])
        eT = [ph.sb(f"eT_{r}", [P, HG, TB, S]) for r in range(2)]
        o_sb = ph.sb("o_sb", [P, S])
        r16 = ph.sb("r16", [P, TB, HG])
        o_tok = [ph.sb(f"o_tok{r}", [P, TB, HG, 8]) for r in range(2)]
        zeroed = ph.sem("zeroed")
        loaded = [ph.sem(f"loaded{r}") for r in range(2)]
        v_loaded = [ph.sem(f"v_loaded{r}") for r in range(4)]
        s_ready, logits_done, top_done = ph.sem("s_ready"), ph.sem("logits_done"), ph.sem("top_done")
        clip_done = ph.sem("clip_done")
        dve_settled, sp_settled = ph.sem("dve_settled"), ph.sem("sp_settled")
        s_read = clip_done if decay else logits_done
        exp_done, tr_ready = ph.sem("exp_done"), ph.sem("tr_ready")
        tr_read = [ph.sem(f"tr_read{kb}") for kb in range(TB)]
        pv_done, o_copied, oT_ready, recip_done, o_done = (
            ph.sem(k) for k in ("pv_done", "o_copied", "oT_ready", "recip_done", "o_done"))
        stored = [ph.sem(f"stored{r}") for r in range(2)]
        S_BANK, TR_BANK, PV_BANK, OT_BANK = 0, 2, 6, 7
        on_dve = () if decay else (3,)
        n_loads = 6 * 16 + (0 if decay else 16)

        with nc.Block() as block:
            @block.gpsimd
            def _(pool):
                for r in range(2):
                    pool.memset(q4[r][:].bitcast(F32), 0.0).then_inc(zeroed, 1)
                    pool.memset(k4[r][:].bitcast(F32), 0.0).then_inc(zeroed, 1)

            @block.sync
            def _(sp):
                sp.wait_ge(zeroed, 4)

                def step(st):
                    if st.has(0):
                        n, r, rv = st.n(0), st.slot(0, 2), st.slot(0, 4)
                        wait(sp, s_ready, 16 * (n - 2))
                        if not decay:
                            wait(sp, logits_done, 16 * (n - 2))
                        settle(sp, sp_settled)
                        for row, dq, dk in ((0, g.q_hi8, g.k_hi8), (32, g.q_hi8, g.k_lo8), (64, g.q_lo8, g.k_hi8)):
                            for dst, src in ((q4[r], dq), (k4[r], dk)):
                                sp.dma_start(dst[row:row + 8].bitcast(F32),
                                             src[bass.ds((n - 1) * 32, 32), :].rearrange("(j d) n -> d j n", d=8)
                                             ).then_inc(loaded[r], 16)
                        if not decay:
                            hg = (st.c - 1) % 4
                            sp.dma_start(strip[r][:], g.strips[hg * HG:(hg + 1) * HG].rearrange("h p n -> p h n")
                                         ).then_inc(loaded[r], 16)
                        wait(sp, pv_done, n - 4)
                        settle(sp, sp_settled)
                        sp.dma_start(v4[rv][:], item(g.v8, n).rearrange("a (t p) n -> p (a t) n", p=P)
                                     ).then_inc(v_loaded[rv], 16)
                    if st.has(4):
                        sp.wait_ge(o_done, st.n(4))
                        settle(sp, sp_settled)
                        r = st.slot(4, 2)
                        sp.dma_start(item(g.o8, st.n(4)).rearrange("a t p c -> p (a t) c"),
                                     o_tok[r][:].rearrange("p t j d -> p t (j d)")).then_inc(stored[r], 16)

                run_steps(sp, NG, 4, step)
                for r in range(2):
                    sp.wait_ge(stored[r], 16 * NG // 2)

            @block.tensor
            def _(pe):
                def scores(n, r, j, blocks):
                    for qb in blocks:
                        wait(pe, s_read, 16 * (n - 1) + 4 * j + qb - 1)
                        pe.matmul(g.ps[:, S_BANK + qb % 2, :], q4[r][0:KROWS, j, qb * P:(qb + 1) * P],
                                  k4[r][0:KROWS, j, :], start=True, stop=True).then_inc(s_ready, 1)

                def transposes(n, j, blocks):
                    pe.wait_ge(exp_done, 16 * (n - 1) + 4 * j + 4)
                    for kb in blocks:
                        wait(pe, tr_read[kb], 4 * (n - 1) + j)
                        for qb in range(TB):
                            ins = pe.transpose(g.ps[:, TR_BANK + kb, qb * P:(qb + 1) * P],
                                               e[:, j, qb, kb * P:(kb + 1) * P], g.ident[:])
                        ins.then_inc(tr_ready, 1)

                def product(n, r, rv, kb):
                    if kb == 0:
                        for k in range(TB):
                            pe.wait_ge(tr_read[k], 4 * n)
                        wait(pe, o_copied, n - 1)
                    for j in range(HG):
                        ins = pe.matmul(g.ps[32 * j:32 * j + 32, PV_BANK, :], v4[rv][:, kb, 32 * j:32 * j + 32],
                                        eT[r][:, j, kb, :], start=(kb == 0), stop=(kb == TB - 1))
                    if kb == TB - 1:
                        ins.then_inc(pv_done, 1)

                def turn(n):
                    pe.wait_ge(o_copied, n)
                    wait(pe, o_done, n - 1)
                    for tb in range(TB):
                        ins = pe.transpose(g.ps[:, OT_BANK, tb * P:(tb + 1) * P], o_sb[:, tb * P:(tb + 1) * P],
                                           g.ident[:])
                    ins.then_inc(oT_ready, 1)

                def step(st):
                    now, before = st.has(0), st.has(1)
                    if now:
                        pe.wait_ge(loaded[st.slot(0, 2)], n_loads * st.use(0, 2))
                    for j in range(HG):
                        k, jt = (0, j - 2) if j >= 2 else (1, j + 2)
                        for blocks, turned in (((0, 1), (0, 1)), ((2,), (2,)), ((3,), (3,))):
                            if now:
                                scores(st.n(0), st.slot(0, 2), j, blocks)
                            if st.has(k):
                                transposes(st.n(k), jt, turned)
                        if before and j >= 2:
                            if j == 2:
                                pe.wait_ge(v_loaded[st.slot(1, 4)], 16 * st.use(1, 4))
                            for kb in (2 * j - 4, 2 * j - 3):
                                product(st.n(1), st.slot(1, 2), st.slot(1, 4), kb)
                        if j == 1 and st.has(2):
                            turn(st.n(2))

                run_steps(pe, NG, 2, step)

            @block.scalar
            def _(act):
                def copies(n, r, j):
                    for kb in range(TB):
                        if kb in on_dve:
                            continue
                        act.wait_ge(tr_ready, 16 * (n - 1) + 4 * j + kb + 1)
                        if kb == 0 and j == 0:
                            wait(act, pv_done, n - 2)
                        act.activation(eT[r][:, j, kb, :], g.ps[:, TR_BANK + kb, :], ACT.Copy).then_inc(tr_read[kb], 1)

                def exps(n, j):
                    act.wait_ge(top_done, 4 * (n - 1) + j + 1)
                    wait(act, tr_ready, 16 * (n - 1) + 4 * j - 12)
                    for qb in range(TB):
                        act.activation(e[:, j, qb, :], logits[:, j % 2, qb, :], ACT.Exp,
                                       bias=neg_top[:, j % 2, qb:qb + 1]).then_inc(exp_done, 1)

                def copy_out(n):
                    act.wait_ge(pv_done, n)
                    wait(act, oT_ready, n - 1)
                    act.activation(o_sb[:], g.ps[:, PV_BANK, :], ACT.Copy).then_inc(o_copied, 1)

                def step(st):
                    for j in range(HG):
                        k, jt = (0, j - 2) if j >= 2 else (1, j + 2)
                        if st.has(k):
                            copies(st.n(k), st.slot(k, 2), jt)
                        if j == 0 and st.has(2):
                            copy_out(st.n(2))
                        if st.has(0):
                            exps(st.n(0), j)

                run_steps(act, NG, 2, step)

            @block.vector
            def _(dve):
                def head(n, r, j):
                    for qb in range(TB):
                        k = 16 * (n - 1) + 4 * j + qb + 1
                        bank = g.ps[:, S_BANK + qb % 2, :]
                        cols = slice(STRIP0 - qb * P, STRIP0 - qb * P + S)
                        dve.wait_ge(s_ready, k)
                        wait(dve, exp_done, k - 8)
                        if decay:
                            dve.tensor_scalar(clipped[:, qb % 2, :], bank, -CLAMP, CLAMP, ALU.max, ALU.min
                                              ).then_inc(clip_done, 1)
                            dve.wait_ge(clip_done, k)
                        settle(dve, dve_settled)
                        if decay:
                            dve.tensor_tensor_reduce(logits[:, j % 2, qb, :], clipped[:, qb % 2, :], g.decay_strip[:, cols],
                                                     1.0, -3e38, ALU.mult, ALU.max, top[:, j % 2, qb:qb + 1]
                                                     ).then_inc(logits_done, 1)
                        else:
                            dve.tensor_tensor_reduce(logits[:, j % 2, qb, :], bank, strip[r][:, j, cols],
                                                     1.0, -3e38, ALU.add, ALU.max, top[:, j % 2, qb:qb + 1]
                                                     ).then_inc(logits_done, 1)
                    dve.wait_ge(logits_done, 16 * (n - 1) + 4 * j + 4)
                    dve.tensor_scalar(neg_top[:, j % 2, :], top[:, j % 2, :], -1.0, None, ALU.mult).then_inc(top_done, 1)

                def copies(n, r, j):
                    for kb in on_dve:
                        dve.wait_ge(tr_ready, 16 * (n - 1) + 4 * j + kb + 1)
                        if j == 0:
                            wait(dve, pv_done, n - 2)
                        dve.tensor_copy(eT[r][:, j, kb, :], g.ps[:, TR_BANK + kb, :]).then_inc(tr_read[kb], 1)

                def finish(st):
                    n, r = st.n(2), st.slot(2, 2)
                    o = g.ps[:, OT_BANK, :].rearrange("p (t j d) -> p t j d", t=TB, j=HG)
                    dve.wait_ge(oT_ready, n)
                    dve.reciprocal(r16[:], o[:, :, :, 8]).then_inc(recip_done, 1)
                    dve.wait_ge(recip_done, n)
                    wait(dve, stored[r], 16 * (st.use(2, 2) - 1))
                    dve.tensor_tensor(o_tok[r][:], o[:, :, :, 0:8], r16[:, :, :, None].to_broadcast([P, TB, HG, 8]),
                                      ALU.mult).then_inc(o_done, 1)

                def step(st):
                    if not decay and st.has(0):
                        dve.wait_ge(loaded[st.slot(0, 2)], n_loads * st.use(0, 2))
                    for j in range(HG):
                        if st.has(0):
                            head(st.n(0), st.slot(0, 2), j)
                        k, jt = (0, j - 2) if j >= 2 else (1, j + 2)
                        if st.has(k):
                            copies(st.n(k), st.slot(k, 2), jt)
                        if j == 2 and st.has(2):
                            finish(st)

                run_steps(dve, NG, 2, step)


def project_wide(nc, g, name, scale):
    NQ = 8
    M = 3 * NQ
    R = 4
    with Phase(nc, name) as ph:
        w = ph.sb("w", [P, 3 * NQ * P])
        xn = ph.sb("xn", [P, TB, DM])
        xT = ph.sb("xT", [P, S])
        hi = ph.sb("hi", [P, R, S], F32R)
        lo = ph.sb("lo", [P, R, S], F32R)
        vs = ph.sb("vs", [P, R, S])
        w_loaded = ph.sem("w_loaded")
        xn_done, xn_free, xp_ready, xT_done, xT_free = (
            ph.sem(k) for k in ("xn_done", "xn_free", "xp_ready", "xT_done", "xT_free"))
        proj_ready, hi_done, piece_done = ph.sem("proj_ready"), ph.sem("hi_done"), ph.sem("piece_done")
        stored = [ph.sem(f"stored{r}") for r in range(R)]
        X_BANK, R_BANK = 0, 1
        USES = 3 * NQ // R

        def before(n, m):
            return 32 * (USES * (n - 1) + m // R + 1)

        with nc.Block() as block:
            @block.sync
            def _(sp):
                sp.dma_start(w[:], g.w_qkv).then_inc(w_loaded, 16)
                with sp.Fori(1, B + 1) as n:
                    for m in range(M):
                        r = m % R
                        sp.wait_ge(piece_done, M * (n - 1) + m + 1)
                        k = m % NQ
                        if m < 2 * NQ:
                            for dst, src in ((g.q_hi if m < NQ else g.k_hi, hi), (g.q_lo if m < NQ else g.k_lo, lo)):
                                sp.dma_start(item(dst, (n - 1) * NQ + k + 1).rearrange("a p n -> (a p) n"),
                                             src[:, r, :].bitcast(F32)).then_inc(stored[r], 16)
                        else:
                            tb, half = divmod(k, 2)
                            for t in range(2):
                                group = (n - 1) * NQ + half * 4 + 2 * t + 1
                                sp.dma_start(g.v32[bass.ds(group - 1, 2), tb * P:(tb + 1) * P, :]
                                             .rearrange("a p c -> p a c"),
                                             vs[:, r, t * 256:(t + 1) * 256].rearrange("p (a c) -> p a c", a=2)
                                             ).then_inc(stored[r], 16)
                for r in range(R):
                    sp.wait_ge(stored[r], 32 * (USES * B + 1))

            @block.vector
            def _(dve):
                dve.sem_inc(xn_free, 1)
                for r in range(R):
                    dve.sem_inc(stored[r], 32)
                with dve.Fori(1, B + 1) as n:
                    dve.wait_ge(xn_free, n)
                    normalise(dve, g.x_all, g.mean_var, g.rstd, n, xn, xn_done)
                    for m in range(M):
                        r = m % R
                        bank = g.ps[:, R_BANK + r, :]
                        if m < 2 * NQ:
                            dve.wait_ge(hi_done, 2 * NQ * (n - 1) + m + 1)
                            dve.scalar_tensor_tensor(lo[:, r, :], bank, scale if m < NQ else 1.0,
                                                     hi[:, r, :].bitcast(F32), ALU.mult, ALU.subtract
                                                     ).then_inc(piece_done, 1)
                        else:
                            dve.wait_ge(proj_ready, M * (n - 1) + m + 1)
                            dve.wait_ge(stored[r], before(n, m))
                            dve.tensor_copy(vs[:, r, :], bank).then_inc(piece_done, 1)

            @block.scalar
            def _(act):
                act.sem_inc(xT_free, 1)
                with act.Fori(1, B + 1) as n:
                    act.wait_ge(xT_free, n)
                    act.wait_ge(xp_ready, n)
                    act.activation(xT[:], g.ps[:, X_BANK, :], ACT.Copy).then_inc(xT_done, 1)
                    for m in range(2 * NQ):
                        r = m % R
                        act.wait_ge(proj_ready, M * (n - 1) + m + 1)
                        act.wait_ge(stored[r], before(n, m))
                        act.activation(hi[:, r, :], g.ps[:, R_BANK + r, :], ACT.Copy, scale=scale if m < NQ else 1.0
                                       ).then_inc(hi_done, 1)

            @block.tensor
            def _(pe):
                pe.wait_ge(w_loaded, 16)
                with pe.Fori(1, B + 1) as n:
                    pe.wait_ge(xn_done, TB * n)
                    for tb in range(TB):
                        ins = pe.transpose(g.ps[:, X_BANK, tb * P:(tb + 1) * P], xn[:, tb, :], g.ident[:])
                    ins.then_inc(xp_ready, 1)
                    pe.wait_ge(xT_done, n)
                    pe.sem_inc(xn_free, 1)
                    for m in range(M):
                        r = m % R
                        if m >= R:
                            pe.wait_ge(piece_done, M * (n - 1) + m + 1 - R)
                        bank = g.ps[:, R_BANK + r, :]
                        if m < 2 * NQ:
                            ins = pe.matmul(bank, w[:, m * P:(m + 1) * P], xT[:], start=True, stop=True)
                        else:
                            tb, half = divmod(m - 2 * NQ, 2)
                            ins = pe.matmul(bank, xT[:, tb * P:(tb + 1) * P],
                                            w[:, 2 * NQ * P + half * 512:2 * NQ * P + (half + 1) * 512],
                                            start=True, stop=True)
                        ins.then_inc(proj_ready, 1)
                    pe.wait_ge(piece_done, M * n)
                    pe.sem_inc(xT_free, 1)


def attend_wide(nc, g, name):
    NG = B * 8
    RQ = 4
    with Phase(nc, name) as ph:
        q4 = [ph.sb(f"q4_{r}", [P, HG, S], F32R) for r in range(RQ)]
        k4 = [ph.sb(f"k4_{r}", [P, HG, S], F32R) for r in range(RQ)]
        v4 = [ph.sb(f"v4_{r}", [P, TB, P]) for r in range(4)]
        top = ph.sb("top", [P, 2, TB, HG])
        top_row = ph.sb("top_row", [HG, 2, S], F32R)
        e = [ph.sb(f"e{r}", [P, HG, TB, S]) for r in range(2)]
        ones = ph.sb("ones", [P, 32])
        pick = ph.sb("pick", [P, HG])
        o_sb, l_sb = ph.sb("o_sb", [P, S]), ph.sb("l_sb", [P, S])
        r16 = ph.sb("r16", [P, TB, HG])
        o_tok = [ph.sb(f"o_tok{r}", [P, TB, HG, 32]) for r in range(2)]
        set_up, pick_loaded = ph.sem("set_up"), ph.sem("pick_loaded")
        loaded = [ph.sem(f"loaded{r}") for r in range(RQ)]
        v_loaded = [ph.sem(f"v_loaded{r}") for r in range(RQ)]
        row_loaded = [ph.sem(f"row_loaded{r}") for r in range(RQ)]
        s_ready, max_done, tt_ready, row_done, st_ready, exp_done, pv_done, o_copied, l_copied, l_ready, oT_ready, \
            recip_done, o_done = (ph.sem(k) for k in (
                "s_ready", "max_done", "tt_ready", "row_done", "st_ready", "exp_done", "pv_done", "o_copied",
                "l_copied", "l_ready", "oT_ready", "recip_done", "o_done"))
        stored = [ph.sem(f"stored{r}") for r in range(2)]
        S_BANK, ST_BANK, T_BANK, PV_BANK, SUM_BANK, OT_BANK = 0, 2, 4, 5, 6, 7

        with nc.Block() as block:
            @block.gpsimd
            def _(pool):
                for r in range(RQ):
                    pool.memset(k4[r][96:97].bitcast(F32), 1.0).then_inc(set_up, 1)

            @block.sync
            def _(sp):
                sp.dma_start(pick[:], g.pick).then_inc(pick_loaded, 16)

                def step(st):
                    if st.has(0):
                        n, r = st.n(0), st.slot(0, RQ)
                        wait(sp, st_ready, 16 * (n - 4))
                        for row, dq, dk in ((0, g.q_hi, g.k_hi), (32, g.q_hi, g.k_lo), (64, g.q_lo, g.k_hi)):
                            for dst, src in ((q4[r], dq), (k4[r], dk)):
                                sp.dma_start(dst[row:row + 32].bitcast(F32),
                                             item(src, n).rearrange("a (j d) n -> (a d) j n", d=32)
                                             ).then_inc(loaded[r], 16)
                    if st.has(2):
                        k = st.slot(2, RQ)
                        sp.wait_ge(row_done, st.n(2))
                        for j in range(HG):
                            sp.dma_start(q4[k][96:97, j, :].bitcast(F32),
                                         top_row[j:j + 1, st.slot(2, 2), :].bitcast(F32)).then_inc(row_loaded[k], 16)
                    if st.has(0):
                        wait(sp, pv_done, n - 4)
                        sp.dma_start(v4[r][:], item(g.v32, n).rearrange("a (t p) n -> p (a t) n", p=P)
                                     ).then_inc(v_loaded[r], 16)
                    if st.has(4):
                        r = st.slot(4, 2)
                        sp.wait_ge(o_done, st.n(4))
                        sp.dma_start(item(g.o32, st.n(4)).rearrange("a t p c -> p (a t) c"),
                                     o_tok[r][:].rearrange("p t j d -> p t (j d)")).then_inc(stored[r], 16)

                run_steps(sp, NG, 4, step)
                for r in range(2):
                    sp.wait_ge(stored[r], 16 * NG // 2)

            @block.tensor
            def _(pe):
                pe.wait_ge(set_up, RQ + 1)
                pe.wait_ge(pick_loaded, 16)

                def scores(n, r, j):
                    for qb in range(TB):
                        wait(pe, max_done, 16 * (n - 1) + 4 * j + qb - 1)
                        pe.matmul(g.ps[:, S_BANK + qb % 2, :], q4[r][0:KROWS, j, qb * P:(qb + 1) * P],
                                  k4[r][0:KROWS, j, :], start=True, stop=True).then_inc(s_ready, 1)

                def turn_tops(n, t):
                    pe.wait_ge(max_done, 16 * n)
                    wait(pe, row_done, n - 1)
                    for qb in range(TB):
                        ins = pe.transpose(g.ps[0:HG, T_BANK, qb * P:(qb + 1) * P], top[:, t, qb, :], g.ident[:])
                    ins.then_inc(tt_ready, 1)

                def shifted_scores(n, r, j):
                    for kb in range(TB):
                        wait(pe, exp_done, 16 * (n - 1) + 4 * j + kb - 1)
                        pe.matmul(g.ps[:, ST_BANK + kb % 2, :], k4[r][0:KROWS + 1, j, kb * P:(kb + 1) * P],
                                  q4[r][0:KROWS + 1, j, :], start=True, stop=True).then_inc(st_ready, 1)

                def product(n, r, rv, kb):
                    if kb == 0:
                        pe.wait_ge(exp_done, 16 * n)
                        wait(pe, o_copied, n - 1)
                        wait(pe, recip_done, n - 1)
                    for j in range(HG):
                        pe.matmul(g.ps[32 * j:32 * j + 32, PV_BANK, :], v4[rv][:, kb, 32 * j:32 * j + 32],
                                  e[r][:, j, kb, :], start=(kb == 0), stop=(kb == TB - 1))
                    for j in range(HG):
                        ins = pe.matmul(g.ps[32 * j:32 * j + 32, SUM_BANK, :], ones[:], e[r][:, j, kb, :],
                                        start=(kb == 0), stop=(kb == TB - 1))
                    if kb == TB - 1:
                        ins.then_inc(pv_done, 1)

                def turn(n):
                    pe.wait_ge(l_copied, n)
                    for tb in range(TB):
                        ins = pe.matmul(g.ps[:, SUM_BANK, tb * HG:(tb + 1) * HG], l_sb[:, tb * P:(tb + 1) * P],
                                        pick[:], start=True, stop=True)
                    ins.then_inc(l_ready, 1)
                    pe.wait_ge(o_copied, n)
                    wait(pe, o_done, n - 1)
                    for tb in range(TB):
                        ins = pe.transpose(g.ps[:, OT_BANK, tb * P:(tb + 1) * P], o_sb[:, tb * P:(tb + 1) * P],
                                           g.ident[:])
                    ins.then_inc(oT_ready, 1)

                def step(st):
                    if st.has(0):
                        pe.wait_ge(loaded[st.slot(0, RQ)], 16 * 6 * st.use(0, RQ))
                    for j in range(HG):
                        if st.has(0):
                            scores(st.n(0), st.slot(0, RQ), j)
                        if j == 0 and st.has(1):
                            turn_tops(st.n(1), st.slot(1, 2))
                        if j == 0 and st.has(4):
                            turn(st.n(4))
                        if st.has(2):
                            if j == 0:
                                pe.wait_ge(row_loaded[st.slot(2, RQ)], 16 * HG * st.use(2, RQ))
                            shifted_scores(st.n(2), st.slot(2, RQ), j)
                        if st.has(3):
                            if j == 0:
                                pe.wait_ge(v_loaded[st.slot(3, RQ)], 16 * st.use(3, RQ))
                            product(st.n(3), st.slot(3, 2), st.slot(3, RQ), j)

                run_steps(pe, NG, 4, step)

            @block.scalar
            def _(act):
                def step(st):
                    if st.has(4):
                        n = st.n(4)
                        act.wait_ge(pv_done, n)
                        wait(act, oT_ready, n - 1)
                        act.activation(l_sb[:], g.ps[:, SUM_BANK, :], ACT.Copy).then_inc(l_copied, 1)
                        act.activation(o_sb[:], g.ps[:, PV_BANK, :], ACT.Copy).then_inc(o_copied, 1)
                    if st.has(1):
                        n = st.n(1)
                        act.wait_ge(tt_ready, n)
                        if st.has(3):
                            act.wait_ge(row_loaded[st.slot(3, RQ)], 16 * HG * st.use(3, RQ))
                        act.activation(top_row[:, st.slot(1, 2), :], g.ps[0:HG, T_BANK, :], ACT.Copy, scale=-1.0
                                       ).then_inc(row_done, 1)
                    if st.has(2):
                        n, r = st.n(2), st.slot(2, 2)
                        for j in range(HG):
                            for kb in range(TB):
                                act.wait_ge(st_ready, 16 * (n - 1) + 4 * j + kb + 1)
                                if j == 0 and kb == 0:
                                    wait(act, pv_done, n - 2)
                                act.activation(e[r][:, j, kb, :], g.ps[:, ST_BANK + kb % 2, :], ACT.Exp
                                               ).then_inc(exp_done, 1)

                run_steps(act, NG, 4, step)

            @block.vector
            def _(dve):
                def finish(st):
                    n, r = st.n(4), st.slot(4, 2)
                    dve.wait_ge(l_ready, n)
                    wait(dve, o_done, n - 1)
                    dve.reciprocal(r16[:], g.ps[:, SUM_BANK, 0:TB * HG].rearrange("p (t j) -> p t j", t=TB)
                                   ).then_inc(recip_done, 1)
                    dve.wait_ge(recip_done, n)
                    dve.wait_ge(oT_ready, n)
                    wait(dve, stored[r], 16 * (st.use(4, 2) - 1))
                    dve.tensor_tensor(o_tok[r][:], g.ps[:, OT_BANK, :].rearrange("p (t j d) -> p t j d", t=TB, j=HG),
                                      r16[:, :, :, None].to_broadcast([P, TB, HG, 32]), ALU.mult).then_inc(o_done, 1)

                dve.memset(ones[:], 1.0).then_inc(set_up, 1)

                def step(st):
                    for j in range(HG):
                        if st.has(0):
                            n, t = st.n(0), st.slot(0, 2)
                            if j == 0:
                                wait(dve, tt_ready, n - 2)
                            for qb in range(TB):
                                dve.wait_ge(s_ready, 16 * (n - 1) + 4 * j + qb + 1)
                                dve.tensor_reduce(top[:, t, qb, j:j + 1], g.ps[:, S_BANK + qb % 2, :], AX_X, ALU.max
                                                  ).then_inc(max_done, 1)
                        if j == 0 and st.has(4):
                            finish(st)

                run_steps(dve, NG, 4, step)


def bias_strips(nc, g, name, coeffs_t, line_table, wpos_t, flip):
    LINE = 1024
    with Phase(nc, name) as ph:
        taps = ph.sb("taps", [101, 4])
        table = ph.sb("table", [101, LINE])
        wp = ph.sb("wp", [4, 16])
        fl = ph.sb("fl", [P, P])
        resp = ph.sb("resp", [4, LINE])
        lines = ph.sb("lines", [16, LINE])
        hank = ph.sb("hank", [P, 2, STRIP])
        strip = ph.sb("strip", [P, 2, STRIP])
        loaded, mm, copied, line_stored = (ph.sem(k) for k in ("loaded", "mm", "copied", "line_stored"))
        h_loaded = [ph.sem(f"h_loaded{r}") for r in range(2)]
        s_stored = [ph.sem(f"s_stored{r}") for r in range(2)]
        flipped, s_copied = ph.sem("flipped"), ph.sem("s_copied")
        HALF = STRIP // 2
        with nc.Block() as block:
            @block.sync
            def _(sp):
                for dst, src in ((taps, coeffs_t), (table, line_table), (wp, wpos_t), (fl, flip)):
                    sp.dma_start(dst[:], src).then_inc(loaded, 16)
                sp.wait_ge(copied, 4)
                sp.dma_start(g.lines, lines[:]).then_inc(line_stored, 16)
                sp.wait_ge(line_stored, 16)
                for h in range(16):
                    r = h % 2
                    wait(sp, flipped, h - 1)
                    src = bass.AP(g.lines.tensor, h * LINE, [[1, P], [1, STRIP]])
                    sp.dma_start(hank[:, r, :], src).then_inc(h_loaded[r], 16)
                    if h:
                        sp.wait_ge(s_copied, h)
                        sp.dma_start(g.strips[h - 1], strip[:, (h - 1) % 2, :]).then_inc(s_stored[(h - 1) % 2], 16)
                sp.wait_ge(s_copied, 16)
                sp.dma_start(g.strips[15], strip[:, 1, :]).then_inc(s_stored[1], 16)
                for r in range(2):
                    sp.wait_ge(s_stored[r], 16 * 8)

            @block.tensor
            def _(pe):
                pe.wait_ge(loaded, 64)
                for k in range(2):
                    pe.matmul(g.ps[0:4, k, :], taps[:], table[:, k * 512:(k + 1) * 512], start=True, stop=True
                              ).then_inc(mm, 1)
                for k in range(2):
                    pe.wait_ge(copied, k + 1)
                    pe.matmul(g.ps[0:16, 2 + k, :], wp[:], resp[:, k * 512:(k + 1) * 512], start=True, stop=True
                              ).then_inc(mm, 1)
                for h in range(16):
                    r = h % 2
                    pe.wait_ge(h_loaded[r], 16 * (h // 2 + 1))
                    wait(pe, s_copied, h - 1)
                    for k in range(2):
                        ins = pe.matmul(g.ps[:, 4 + 2 * r + k, 0:HALF], fl[:], hank[:, r, k * HALF:(k + 1) * HALF],
                                        start=True, stop=True)
                    ins.then_inc(flipped, 1)

            @block.vector
            def _(dve):
                for k in range(2):
                    dve.wait_ge(mm, k + 1)
                    dve.tensor_copy(resp[:, k * 512:(k + 1) * 512], g.ps[0:4, k, :]).then_inc(copied, 1)
                for k in range(2):
                    dve.wait_ge(mm, 2 + k + 1)
                    dve.tensor_copy(lines[:, k * 512:(k + 1) * 512], g.ps[0:16, 2 + k, :]).then_inc(copied, 1)
                for h in range(16):
                    r = h % 2
                    dve.wait_ge(flipped, h + 1)
                    wait(dve, s_stored[r], 16 * (h // 2))
                    dve.tensor_copy(strip[:, r, :].rearrange("p (k n) -> p k n", k=2),
                                    g.ps[:, 4 + 2 * r:6 + 2 * r, 0:HALF]).then_inc(s_copied, 1)


class Marks:

    def __init__(self, ph, name, steps):
        self.sem, self.steps = ph.sem(name), steps.split()

    def at(self, n, step):
        return len(self.steps) * (n - 1) + self.steps.index(step) + 1


def linear_attention(nc, g, name, d):
    NP = 12
    Q, QS, K, KS, B0, B1, ZA, ZB, V0 = range(9)
    HM = 64
    with Phase(nc, name) as ph:
        w = ph.sb("w", [P, NP, P])
        w_out = ph.sb("w_out", [P, DM])
        bout = ph.sb("bout", [P, DM])
        bias = ph.sb("bias", [P, 4])
        rope = ph.sb("rope", [P, 2, S])
        to_c = ph.sb("to_c", [P, 4, P])
        to_m = ph.sb("to_m", [P, 2, HM])
        from_m = ph.sb("from_m", [P, 2, P])
        xn, xn2, xnb = (ph.sb(k, [P, TB, DM]) for k in ("xn", "xn2", "xnb"))
        xT = [ph.sb(f"xT{r}", [P, S]) for r in range(2)]
        u = ph.sb("u", [P, 2, 2, S])
        rot = ph.sb("rot", [P, 2, S])
        low = ph.sb("low", [P, 2, S])
        phi = ph.sb("phi", [P, 2, S])
        beta = ph.sb("beta", [P, 2, S])
        kv = ph.sb("kv", [P, 4, S])
        z = ph.sb("z", [HM, 2, S])
        zmax = ph.sb("zmax", [HM, S])
        zexp = [ph.sb(f"zexp{r}", [HM, 2, S]) for r in range(2)]
        zsum = [ph.sb(f"zsum{r}", [HM, S]) for r in range(2)]
        state = ph.sb("state", [P, 10, S])
        prod = ph.sb("prod", [P, 10, S])
        den = ph.sb("den", [HM, S])
        coef = ph.sb("coef", [P, S])
        cb = ph.sb("cb", [P, 2, S])
        y2 = ph.sb("y2", [P, 2, S])
        yT = ph.sb("yT", [P, S])
        loaded, zeroed = ph.sem("loaded"), ph.sem("zeroed")
        xn_done, xp_ready, xT_done = ph.sem("xn_done"), ph.sem("xp_ready"), ph.sem("xT_done")
        proj_ready = ph.sem("proj_ready")
        va = Marks(ph, "vec_rotate_scan", "cq sq ck sk rq rk lq lk tq tk phi_q phi_k kv0 kv1 kv2 kv3 beta0 beta1 zmax "
                                          "s0 s1 s2 s3 s4 s5 s6 s7 s8 s9")
        vb = Marks(ph, "vec_finish", "den recip coef y0 y1 y z")
        xn2_done = ph.sem("xn2_done")
        aa = Marks(ph, "act_features", "eq ek beta0 beta1 za zb zexp")
        ab = Marks(ph, "act_coef", "cb0 cb1")
        pa = Marks(ph, "pool_products", "zsub p0 p1 zsum p2 p3 p4 p5 p6 p7 p8 p9")
        pool_xnb = ph.sem("pool_xnb")
        ta = Marks(ph, "pe_sums", "m0 m1 m2 m3 m4 m5 m6 m7 m8 m9")
        tb_ = Marks(ph, "pe_finish", "cb0 cb1 out")
        T_BANK, R_BANK, NUM_BANK, DEN_BANK = 0, 1, 5, 7
        scans = [(0, None), (1, None)] + [(m, c) for m in range(2) for c in range(4)]

        with nc.Block() as block:
            @block.sync
            def _(sp):
                for dst, src in ((w[:], d["w"]), (w_out[:], d["w_out"]), (bias[:], d["bias"]),
                                 (rope[:], d["rope"]), (to_c[:], d["to_c"]), (to_m[:], d["to_m"]),
                                 (from_m[:], d["from_m"]), (bout[:], d["bout"][None, :].to_broadcast([P, DM]))):
                    sp.dma_start(dst, src).then_inc(loaded, 16)

            @block.tensor
            def _(pe):
                pe.wait_ge(loaded, 16 * 8)
                pe.wait_ge(zeroed, 1)

                def project(st, pieces):
                    n, r = st.n(1), st.slot(1, 2)
                    for m in pieces:
                        if m < 4:
                            wait(pe, va.sem, va.at(n - 1, f"kv{m}"))
                        elif m < 8:
                            pe.wait_ge(va.sem, va.at(n, ("cq", "sq", "ck", "sk")[m - 4]))
                        else:
                            pe.wait_ge(aa.sem, aa.at(n, ("beta0", "beta1", "za", "zb")[m - 8]))
                        rows = HM if m in (ZA, ZB) else P
                        pe.matmul(g.ps[0:rows, R_BANK + m % 4, :], w[:, m, 0:rows], xT[r][:], start=True, stop=True
                                  ).then_inc(proj_ready, 1)

                def step(st):
                    if st.has(1):
                        pe.wait_ge(xT_done, st.n(1))
                        project(st, range(Q, KS + 1))
                    if st.has(0):
                        n = st.n(0)
                        pe.wait_ge(xn_done, TB * n)
                        if st.has(3):
                            wait(pe, vb.sem, vb.at(st.n(3), "z"))
                        for tb in range(TB):
                            ins = pe.transpose(g.ps[:, T_BANK, tb * P:(tb + 1) * P], xn[:, tb, :], g.ident[:])
                        ins.then_inc(xp_ready, 1)
                    if st.has(2):
                        pe.wait_ge(vb.sem, vb.at(st.n(2), "coef"))
                        pe.matmul(g.ps[:, DEN_BANK, :], from_m[:, 0, :], coef[:], start=True, stop=True
                                  ).then_inc(tb_.sem, 1)
                    if st.has(1):
                        project(st, (B0, B1))
                    if st.has(2):
                        pe.wait_ge(ab.sem, ab.at(st.n(2), "cb0"))
                        pe.matmul(g.ps[:, DEN_BANK, :], from_m[:, 1, :], coef[:], start=True, stop=True
                                  ).then_inc(tb_.sem, 1)
                    if st.has(1):
                        project(st, range(ZA, NP))
                    if st.has(2):
                        n = st.n(2)
                        pe.wait_ge(vb.sem, vb.at(n, "y"))
                        pe.wait_ge(xT_done, st.n(0) if st.has(0) else B)
                        wait(pe, vb.sem, vb.at(n - 1, "z"))
                        for tb in range(TB):
                            ins = pe.matmul(g.ps[:, T_BANK, tb * P:(tb + 1) * P], yT[:, tb * P:(tb + 1) * P], w_out[:],
                                            start=True, stop=True)
                        ins.then_inc(tb_.sem, 1)
                    if st.has(1):
                        n = st.n(1)
                        for i, (m, c) in enumerate(scans):
                            pe.wait_ge(pa.sem, pa.at(n, f"p{i}"))
                            if i == 0 and st.has(2):
                                pe.wait_ge(ab.sem, ab.at(st.n(2), "cb1"))
                            if i == 2 and st.has(2):
                                pe.wait_ge(vb.sem, vb.at(st.n(2), "y1"))
                            if c is None:
                                pe.matmul(g.ps[0:HM, DEN_BANK, :], to_m[:, m, :], prod[:, i, :], start=(m == 0),
                                          stop=(m == 1)).then_inc(ta.sem, 1)
                            else:
                                pe.matmul(g.ps[:, NUM_BANK + m, :], to_c[:, c, :], prod[:, i, :], start=(c == 0),
                                          stop=(c == 3)).then_inc(ta.sem, 1)

                run_steps(pe, B, 3, step, U=2)

            @block.scalar
            def _(act):
                act.wait_ge(loaded, 16 * 8)

                def bank(m):
                    return g.ps[0:HM if m in (ZA, ZB) else P, R_BANK + m % 4, :]

                def step(st):
                    if st.has(1):
                        n = st.n(1)
                        for k in range(2):
                            act.wait_ge(va.sem, va.at(n, ("lq", "lk")[k]))
                            act.activation(low[:, k, :], low[:, k, :], ACT.Exp).then_inc(aa.sem, 1)
                    if st.has(0):
                        n = st.n(0)
                        act.wait_ge(xp_ready, n)
                        wait(act, proj_ready, NP * (n - 2))
                        act.activation(xT[st.slot(0, 2)][:], g.ps[:, T_BANK, :], ACT.Copy).then_inc(xT_done, 1)
                    if st.has(2):
                        act.wait_ge(tb_.sem, tb_.at(st.n(2), "cb0"))
                        wait(act, vb.sem, vb.at(st.n(2) - 1, "y0"))
                        act.activation(cb[:, 0, :], g.ps[:, DEN_BANK, :], ACT.Copy).then_inc(ab.sem, 1)
                    if st.has(1):
                        n = st.n(1)
                        wait(act, va.sem, va.at(n - 1, "s9"))
                        for k in range(2):
                            act.wait_ge(proj_ready, NP * (n - 1) + B0 + k + 1)
                            act.activation(beta[:, k, :], bank(B0 + k), ACT.Sigmoid, bias=bias[:, k:k + 1]
                                           ).then_inc(aa.sem, 1)
                    if st.has(2):
                        act.wait_ge(tb_.sem, tb_.at(st.n(2), "cb1"))
                        wait(act, vb.sem, vb.at(st.n(2) - 1, "y1"))
                        act.activation(cb[:, 1, :], g.ps[:, DEN_BANK, :], ACT.Copy).then_inc(ab.sem, 1)
                    if st.has(1):
                        n = st.n(1)
                        for k in range(2):
                            act.wait_ge(proj_ready, NP * (n - 1) + ZA + k + 1)
                            if k == 0:
                                wait(act, aa.sem, aa.at(n - 1, "zexp"))
                            act.activation(z[:, k, :], bank(ZA + k), ACT.Identity, bias=bias[0:HM, 2 + k:3 + k]
                                           ).then_inc(aa.sem, 1)
                        act.wait_ge(pa.sem, pa.at(n, "zsub"))
                        if st.has(3):
                            act.wait_ge(vb.sem, vb.at(st.n(3), "coef"))
                        act.activation(zexp[st.slot(1, 2)][:], z[:], ACT.Exp).then_inc(aa.sem, 1)

                run_steps(act, B, 3, step, U=2)

            @block.gpsimd
            def _(pool):
                pool.wait_ge(loaded, 16 * 8)

                def step(st):
                    if st.has(1):
                        n, r = st.n(1), st.slot(1, 2)
                        pool.wait_ge(va.sem, va.at(n, "zmax"))
                        pool.tensor_tensor(z[:], z[:], zmax[:, None, :].to_broadcast([HM, 2, S]), ALU.subtract
                                           ).then_inc(pa.sem, 1)
                        for i in range(10):
                            if i == 2:
                                pool.wait_ge(aa.sem, aa.at(n, "zexp"))
                                if st.has(3):
                                    pool.wait_ge(vb.sem, vb.at(st.n(3), "den"))
                                pool.tensor_tensor(zsum[r][:], zexp[r][:, 0, :], zexp[r][:, 1, :], ALU.add
                                                   ).then_inc(pa.sem, 1)
                            pool.wait_ge(va.sem, va.at(n, f"s{i}"))
                            wait(pool, ta.sem, ta.at(n - 1, f"m{i}"))
                            pool.tensor_tensor(prod[:, i, :], state[:, i, :], phi[:, 0, :], ALU.mult
                                               ).then_inc(pa.sem, 1)
                    if st.has(2):
                        n = st.n(2)
                        pool.wait_ge(xn2_done, TB * n)
                        wait(pool, vb.sem, vb.at(n - 1, "z"))
                        pool.tensor_tensor(xnb[:], xn2[:], bout[:, None, :].to_broadcast([P, TB, DM]), ALU.add
                                           ).then_inc(pool_xnb, 1)

                run_steps(pool, B, 3, step, U=2)

            @block.vector
            def _(dve):
                dve.memset(coef[:], 0.0).then_inc(zeroed, 1)
                dve.wait_ge(loaded, 16 * 8)
                dve.wait_ge(zeroed, 1)

                def bank(m):
                    return g.ps[:, R_BANK + m % 4, :]

                def done(ins, marks):
                    ins.then_inc(marks.sem, 1)

                def step(st):
                    if st.has(0):
                        wait(dve, xp_ready, st.n(0) - 1)
                        normalise(dve, g.x_all, g.mean_var, g.rstd, st.n(0), xn, xn_done)
                    if st.has(1):
                        n = st.n(1)
                        wait(dve, va.sem, va.at(n - 1, "s9"))
                        for k in range(2):
                            for t in range(2):
                                dve.wait_ge(proj_ready, NP * (n - 1) + 2 * k + t + 1)
                                dve.tensor_tensor(u[:, k, t, :], bank(2 * k + t), rope[:, t, :], ALU.mult
                                                  ).then_inc(va.sem, 1)
                        for k in range(2):
                            dve.wait_ge(va.sem, va.at(n, ("sq", "sk")[k]))
                            dve.tensor_tensor(rot[:, k, :], u[:, k, 0, :], u[:, k, 1, :], ALU.add).then_inc(va.sem, 1)
                        for k in range(2):
                            dve.wait_ge(va.sem, va.at(n, ("rq", "rk")[k]))
                            dve.tensor_scalar(low[:, k, :], rot[:, k, :], 0.0, None, ALU.min).then_inc(va.sem, 1)
                    if st.has(2):
                        n, r = st.n(2), st.slot(2, 2)
                        dve.wait_ge(ta.sem, ta.at(n, "m1"))
                        dve.wait_ge(pa.sem, pa.at(n, "zsum"))
                        wait(dve, tb_.sem, tb_.at(n - 1, "cb1"))
                        dve.scalar_tensor_tensor(den[:], g.ps[0:HM, DEN_BANK, :], 1e-6, zsum[r][:], ALU.add, ALU.mult
                                                 ).then_inc(vb.sem, 1)
                        dve.wait_ge(vb.sem, vb.at(n, "den"))
                        dve.reciprocal(den[:], den[:]).then_inc(vb.sem, 1)
                        dve.wait_ge(vb.sem, vb.at(n, "recip"))
                        dve.tensor_tensor(coef[0:HM, :], den[:], zexp[r][:, 0, :], ALU.mult).then_inc(vb.sem, 1)
                    if st.has(1):
                        n = st.n(1)
                        for k in range(2):
                            dve.wait_ge(aa.sem, aa.at(n, ("eq", "ek")[k]))
                            dve.tensor_scalar(low[:, k, :], low[:, k, :], -1.0, 1.0, ALU.add, ALU.add
                                              ).then_inc(va.sem, 1)
                        wait(dve, pa.sem, pa.at(n - 1, "p9"))
                        for k in range(2):
                            dve.wait_ge(va.sem, va.at(n, ("tq", "tk")[k]))
                            dve.scalar_tensor_tensor(phi[:, k, :], rot[:, k, :], 0.0, low[:, k, :], ALU.max, ALU.add
                                                     ).then_inc(va.sem, 1)
                        dve.wait_ge(va.sem, va.at(n, "phi_k"))
                        for c in range(4):
                            dve.wait_ge(proj_ready, NP * (n - 1) + V0 + c + 1)
                            dve.tensor_tensor(kv[:, c, :], bank(V0 + c), phi[:, 1, :], ALU.mult).then_inc(va.sem, 1)
                        for m in range(2):
                            dve.wait_ge(aa.sem, aa.at(n, ("beta0", "beta1")[m]))
                            dve.tensor_scalar(beta[:, m, :], beta[:, m, :], 0.85, 0.9995, ALU.max, ALU.min
                                              ).then_inc(va.sem, 1)
                        dve.wait_ge(aa.sem, aa.at(n, "zb"))
                        wait(dve, pa.sem, pa.at(n - 1, "zsub"))
                        dve.tensor_tensor(zmax[:], z[:, 0, :], z[:, 1, :], ALU.max).then_inc(va.sem, 1)
                    if st.has(2):
                        n = st.n(2)
                        dve.wait_ge(ta.sem, ta.at(n, "m9"))
                        wait(dve, tb_.sem, tb_.at(n - 1, "out"))
                        for m in range(2):
                            dve.wait_ge(ab.sem, ab.at(n, ("cb0", "cb1")[m]))
                            dve.tensor_tensor(y2[:, m, :], g.ps[:, NUM_BANK + m, :], cb[:, m, :], ALU.mult
                                              ).then_inc(vb.sem, 1)
                        dve.wait_ge(vb.sem, vb.at(n, "y1"))
                        dve.tensor_tensor(yT[:], y2[:, 0, :], y2[:, 1, :], ALU.add).then_inc(vb.sem, 1)
                        wait(dve, pool_xnb, n - 1)
                        normalise(dve, g.x_all, g.mean_var, g.rstd, n, xn2, xn2_done)
                    if st.has(1):
                        n = st.n(1)
                        dve.wait_ge(va.sem, va.at(n, "beta1"))
                        for i, (m, c) in enumerate(scans):
                            dve.tensor_tensor_scan(state[:, i, :], beta[:, m, :],
                                                   phi[:, 1, :] if c is None else kv[:, c, :], 0.0, ALU.mult, ALU.add
                                                   ).then_inc(va.sem, 1)
                    if st.has(2):
                        n = st.n(2)
                        dve.wait_ge(tb_.sem, tb_.at(n, "out"))
                        dve.wait_ge(pool_xnb, n)
                        dve.tensor_tensor(batch_of(g.y_all, n), g.ps[:, T_BANK, :].rearrange("p (t d) -> p t d", t=TB),
                                          xnb[:], ALU.add).then_inc(vb.sem, 1)

                run_steps(dve, B, 3, step, U=2)


def project_out(nc, g, name, wide):
    G = 8 if wide else 1
    src = g.o32 if wide else g.o8
    with Phase(nc, name) as ph:
        w = ph.sb("w", [P, G, DM])
        bias = ph.sb("bias", [P, 3, DM])
        o = [ph.sb(f"o{r}", [P, TB, G * P]) for r in range(2)]
        oT = ph.sb("oT", [P, 2, S])
        yT = ph.sb("yT", [P, S])
        w_loaded = ph.sem("w_loaded")
        loaded = [ph.sem(f"loaded{r}") for r in range(2)]
        t_ready, t_read, mm_done, y_copied, yt_ready, added = (
            ph.sem(k) for k in ("t_ready", "t_read", "mm_done", "y_copied", "yt_ready", "added"))
        T_BANK, Y_BANK, YT_BANK = 0, 2, 4
        pieces = 8 if wide else 4
        width = G * P // pieces
        dest = g.y_all if wide else g.x_all

        with nc.Block() as block:
            @block.sync
            def _(sp):
                for k, part in enumerate(g.w_out32 if wide else (g.w_out8[name],)):
                    sp.dma_start(w[:, k, :], part).then_inc(w_loaded, 16)
                if wide:
                    sp.dma_start(bias[:, 0, :], g.b_out[None, :].to_broadcast([P, DM])).then_inc(w_loaded, 16)

                def step(st):
                    n, r = st.n(0), st.slot(0, 2)
                    wait(sp, t_ready, G * (n - 2))
                    for k in range(pieces):
                        sp.dma_start(o[r][:, :, k * width:(k + 1) * width],
                                     src[bass.ds((n - 1) * pieces + k, 1)].rearrange("a t p c -> p (a t) c")
                                     ).then_inc(loaded[r], 16)

                run_steps(sp, B, 0, step, U=2)

            @block.tensor
            def _(pe):
                pe.wait_ge(w_loaded, 16 * (G + wide))

                def step(st):
                    n, r = st.n(0), st.slot(0, 2)
                    pe.wait_ge(loaded[r], 16 * pieces * st.use(0, 2))

                    def turn(k):
                        m = G * (n - 1) + k + 1
                        wait(pe, t_read, m - 2)
                        slot = k % 2 if wide else r
                        for tb in range(TB):
                            ins = pe.transpose(g.ps[:, T_BANK + slot, tb * P:(tb + 1) * P],
                                               o[r][:, tb, k * P:(k + 1) * P], g.ident[:])
                        ins.then_inc(t_ready, 1)

                    turn(0)
                    wait(pe, y_copied, n - 2)
                    for k in range(G):
                        if k + 1 < G:
                            turn(k + 1)
                        pe.wait_ge(t_read, G * (n - 1) + k + 1)
                        slot = k % 2 if wide else r
                        pe.matmul(g.ps[:, Y_BANK + r, :], w[:, k, :], oT[:, slot, :],
                                  start=(k == 0), stop=(k == G - 1)).then_inc(mm_done, 1)
                    pe.wait_ge(y_copied, n)
                    wait(pe, added, n - 2)
                    for tb in range(TB):
                        ins = pe.transpose(g.ps[:, YT_BANK + r, tb * P:(tb + 1) * P], yT[:, tb * P:(tb + 1) * P],
                                           g.ident[:])
                    ins.then_inc(yt_ready, 1)

                run_steps(pe, B, 0, step, U=2)

            @block.scalar
            def _(act):
                def step(st):
                    n, r = st.n(0), st.slot(0, 2)
                    for k in range(G):
                        m = G * (n - 1) + k + 1
                        slot = k % 2 if wide else r
                        act.wait_ge(t_ready, m)
                        wait(act, mm_done, m - 2)
                        act.activation(oT[:, slot, :], g.ps[:, T_BANK + slot, :], ACT.Copy).then_inc(t_read, 1)
                    act.wait_ge(mm_done, G * n)
                    wait(act, yt_ready, n - 1)
                    act.activation(yT[:], g.ps[:, Y_BANK + r, :], ACT.Copy).then_inc(y_copied, 1)

                run_steps(act, B, 0, step, U=2)

            @block.vector
            def _(dve):
                if wide:
                    dve.wait_ge(w_loaded, 16 * (G + 1))

                def step(st):
                    n, r = st.n(0), st.slot(0, 2)
                    dve.wait_ge(yt_ready, n)
                    y = g.ps[:, YT_BANK + r, :].rearrange("p (t d) -> p t d", t=TB)
                    other = (bias[:, 0:1, :].to_broadcast([P, TB, DM]) if wide else batch_of(g.x_all, n))
                    dve.tensor_tensor(batch_of(dest, n), y, other, ALU.add).then_inc(added, 1)

                run_steps(dve, B, 0, step, U=2)


def add_normalised(nc, g, name, source, gamma, beta):
    with Phase(nc, name) as ph:
        gb = ph.sb("gb", [P, 2, DM])
        yn = ph.sb("yn", [P, TB, DM])
        loaded, done, chain = ph.sem("loaded"), ph.sem("done"), ph.sem("chain")
        with nc.Block() as block:
            @block.sync
            def _(sp):
                for k, src in enumerate((gamma, beta)):
                    sp.dma_start(gb[:, k, :], src[None, :].to_broadcast([P, DM])).then_inc(loaded, 16)

            @block.vector
            def _(dve):
                dve.wait_ge(loaded, 32)
                with dve.Fori(1, B + 1) as n:
                    normalise(dve, source, g.mean_var, g.rstd, n, yn, done)
                    dve.wait_ge(done, TB * n)
                    link = Link(dve, chain, n, 3)
                    link(dve.tensor_tensor(yn[:], yn[:], gb[:, 0:1, :].to_broadcast([P, TB, DM]), ALU.mult))
                    link(dve.tensor_tensor(yn[:], yn[:], gb[:, 1:2, :].to_broadcast([P, TB, DM]), ALU.add))
                    link(dve.tensor_tensor(batch_of(g.x_all, n), batch_of(g.x_all, n), yn[:], ALU.add))


def swiglu(nc, g, name, packed, E, C, router=None):
    EC = E * C
    W = 3 * C * P
    quant = packed.dtype == I32
    routed = E - 1
    OUT_LAG, OUT_AT = (2, 4) if E > 1 else (3, 0)
    X_AT = EC // 3
    with Phase(nc, name) as ph:
        stage = ph.sb("stage", [P, 2, W], I32 if quant else F32)
        stage_f = ph.sb("stage_f", [P, 2, W]) if quant else stage
        w_hi = ph.sb("w_hi", [P, E, W], F32R)
        w_lo = ph.sb("w_lo", [P, E, W], F32R)
        xn = ph.sb("xn", [P, TB, DM])
        xT = ph.sb("xT", [P, S])
        x_hi = [ph.sb(f"x_hi{r}", [P, S], F32R) for r in range(2)]
        x_lo = [ph.sb(f"x_lo{r}", [P, S], F32R) for r in range(2)]
        gate = ph.sb("gate", [P, 2, S])
        h = ph.sb("h", [P, C, S])
        h_hi = ph.sb("h_hi", [P, C, S], F32R)
        h_lo = ph.sb("h_lo", [P, C, S], F32R)
        acc = ph.sb("acc", [P, S])
        stage_loaded = [ph.sem(f"stage_loaded{k}") for k in range(2)]
        dequant_done, w_hi_done, w_done = ph.sem("dequant_done"), ph.sem("w_hi_done"), ph.sem("w_done")
        xn_done, xp_ready, xT_done, x_hi_done, x_lo_done = (
            ph.sem(k) for k in ("xn_done", "xp_ready", "xT_done", "x_hi_done", "x_lo_done"))
        gu_ready, gate_done, h_done, h_hi_done, h_lo_done, down_done, d_ready, d_read, acc_done = (
            ph.sem(k) for k in ("gu_ready", "gate_done", "h_done", "h_hi_done", "h_lo_done", "down_done", "d_ready",
                                "d_read", "acc_done"))
        out_ready, out_added = ph.sem("out_ready"), ph.sem("out_added")
        if routed:
            rw = ph.sb("rw", [P, routed])
            lower = ph.sb("lower", [P, routed, routed])
            comb = [ph.sb(f"comb{r}", [P, TB, routed]) for r in range(2)]
            mx, sm = ph.sb("mx", [P, TB]), ph.sb("sm", [P, TB])
            pr, sel = ph.sb("pr", [P, TB, routed]), ph.sb("sel", [P, TB, routed])
            gt, eq = (ph.sb(k, [P, TB, routed, routed]) for k in ("gt", "eq"))
            cw = ph.sb("cw", [P, 2, S])
            part = ph.sb("part", [P, S])
            small_loaded, lg_ready, shifted, p_exp, comb_done, cw_ready, cw_done, chain = (
                ph.sem(k) for k in ("small_loaded", "lg_ready", "shifted", "p_exp", "comb_done", "cw_ready",
                                    "cw_done", "chain"))
            recip_done = ph.sem("recip_done")
        T_BANK, R_BANK, G_BANK, U_BANK, D_BANK = 0, 1, 2, 4, 6
        LG_AT, COMB_AT = X_AT + 3, X_AT + 4

        def position(st, k, q):
            return EC * (st.n(k) - 1) + q + 1, (EC * (st.c - k - 1) + q) % 2

        with nc.Block() as block:
            @block.sync
            def _(sp):
                if routed:
                    sp.dma_start(rw[:], router[0]).then_inc(small_loaded, 16)
                    sp.dma_start(lower[:], router[1][None, :, :].to_broadcast([P, routed, routed])
                                 ).then_inc(small_loaded, 16)
                for e in range(E):
                    wait(sp, w_done, e - 1)
                    sp.dma_start(stage[:, e % 2, :], packed[e]).then_inc(stage_loaded[e % 2], 16)

            @block.tensor
            def _(pe):
                def three(bank, w0, cols, hi, lo, start, stop):
                    pe.matmul(bank, w_hi[:, w0, cols], hi, start=start, stop=False)
                    pe.matmul(bank, w_lo[:, w0, cols], hi, start=False, stop=False)
                    return pe.matmul(bank, w_hi[:, w0, cols], lo, start=False, stop=stop)

                def gate_up(st, q):
                    e, c = divmod(q, C)
                    m, par = position(st, 1, q)
                    r = st.slot(1, 2)
                    wait(pe, gate_done, m - 2)
                    wait(pe, h_done, m - 2)
                    three(g.ps[:, G_BANK + par, :], e, slice(c * P, (c + 1) * P), x_hi[r][:], x_lo[r][:], True, True)
                    three(g.ps[:, U_BANK + par, :], e, slice((C + c) * P, (C + c + 1) * P), x_hi[r][:], x_lo[r][:],
                          True, True).then_inc(gu_ready, 1)

                def down(st, k, q):
                    e, c = divmod(q, C)
                    m, _ = position(st, k, q)
                    bank = g.ps[:, D_BANK + (E * (st.c - k - 1) + e) % 2, :]
                    pe.wait_ge(h_lo_done, m)
                    if c == 0:
                        wait(pe, d_read, E * (st.n(k) - 1) + e - 1)
                    ins = three(bank, e, slice((2 * C + c) * P, (2 * C + c + 1) * P), h_hi[:, c, :], h_lo[:, c, :],
                                c == 0, c == C - 1)
                    ins.then_inc(down_done, 1)
                    if c == C - 1:
                        pe.wait_ge(down_done, m)
                        pe.sem_inc(d_ready, 1)

                def step(st):
                    if st.has(1):
                        pe.wait_ge(x_lo_done, st.n(1))
                    if routed and st.has(1):
                        pe.wait_ge(comb_done, st.n(1))
                    for q in range(EC):
                        e, c = divmod(q, C)
                        if st.has(1):
                            if isinstance(st.i, int) and st.n(1) == 1 and c == 0:
                                pe.wait_ge(w_done, e + 1)
                            if routed and e and c == 0:
                                k = routed * (st.n(1) - 1) + e
                                wait(pe, cw_done, k - 1)
                                if st.has(0):
                                    wait(pe, shifted, st.n(0) - (0 if q > LG_AT else 1))
                                else:
                                    wait(pe, shifted, st.n(1))
                                for tb in range(TB):
                                    ins = pe.matmul(g.ps[:, R_BANK, tb * P:(tb + 1) * P],
                                                    comb[st.slot(1, 2)][:, tb, e - 1:e].to_broadcast([P, P]),
                                                    g.ident[:], start=True, stop=True)
                                ins.then_inc(cw_ready, 1)
                            gate_up(st, q)
                        if q >= 2 and st.has(1):
                            down(st, 1, q - 2)
                        if q < 2 and st.has(2):
                            down(st, 2, EC - 2 + q)
                        if q == X_AT and st.has(0):
                            pe.wait_ge(xn_done, TB * st.n(0))
                            if st.has(OUT_LAG) or (st.has(OUT_LAG + 1) and OUT_AT >= X_AT):
                                wait(pe, out_added, st.n(OUT_LAG))
                            for tb in range(TB):
                                ins = pe.transpose(g.ps[:, T_BANK, tb * P:(tb + 1) * P], xn[:, tb, :], g.ident[:])
                            ins.then_inc(xp_ready, 1)
                        if routed and q == LG_AT and st.has(0):
                            if st.n(0) == 1 if isinstance(st.i, int) else False:
                                pe.wait_ge(small_loaded, 32)
                            pe.wait_ge(xT_done, st.n(0))
                            if st.has(1):
                                pe.wait_ge(cw_done, routed * (st.n(1) - 1) + q // C)
                            for tb in range(TB):
                                ins = pe.matmul(g.ps[:, R_BANK, tb * 8:tb * 8 + routed], xT[:, tb * P:(tb + 1) * P],
                                                rw[:], start=True, stop=True)
                            ins.then_inc(lg_ready, 1)
                        if q == OUT_AT and st.has(OUT_LAG):
                            if routed:
                                pe.wait_ge(acc_done, routed * st.n(OUT_LAG))
                            else:
                                pe.wait_ge(d_read, st.n(OUT_LAG))
                            if st.has(1):
                                pe.wait_ge(x_lo_done, st.n(1))
                            for tb in range(TB):
                                ins = pe.transpose(g.ps[:, T_BANK, tb * P:(tb + 1) * P], acc[:, tb * P:(tb + 1) * P],
                                                   g.ident[:])
                            ins.then_inc(out_ready, 1)

                run_steps(pe, B, OUT_LAG, step, U=2)

            @block.scalar
            def _(act):
                def step(st):
                    for q in range(EC):
                        e, c = divmod(q, C)
                        if isinstance(st.i, int) and st.c + 2 * st.i == 2 and c == 0:
                            if quant:
                                act.wait_ge(dequant_done, e + 1)
                            else:
                                act.wait_ge(stage_loaded[e % 2], 16 * (e // 2 + 1))
                            act.activation(w_hi[:, e, :], stage_f[:, e % 2, :], ACT.Copy).then_inc(w_hi_done, 1)
                        if st.has(1):
                            m, par = position(st, 1, q)
                            if routed and e and c == 0:
                                k = routed * (st.n(1) - 1) + e
                                act.wait_ge(cw_ready, k)
                                wait(act, d_read, E * (st.n(1) - 1) + (e - 1 if e > 2 else 0))
                                act.activation(cw[:, e % 2, :], g.ps[:, R_BANK, :], ACT.Copy).then_inc(cw_done, 1)
                            act.wait_ge(gu_ready, m)
                            wait(act, h_done, m - 2)
                            act.activation(gate[:, par, :], g.ps[:, G_BANK + par, :], ACT.Silu).then_inc(gate_done, 1)
                        for k, qq in (((1, q - 1),) if q else ((2, EC - 1),)):
                            if st.has(k):
                                m, _ = position(st, k, qq)
                                act.wait_ge(h_done, m)
                                wait(act, down_done, m - C)
                                act.activation(h_hi[:, qq % C, :], h[:, qq % C, :], ACT.Copy).then_inc(h_hi_done, 1)
                        if q == X_AT and st.has(0):
                            act.wait_ge(xp_ready, st.n(0))
                            if routed:
                                wait(act, lg_ready, st.n(0) - 1)
                                act.activation(xT[:], g.ps[:, T_BANK, :], ACT.Copy).then_inc(xT_done, 1)
                            wait(act, gu_ready, EC * (st.n(0) - 2))
                            act.activation(x_hi[st.slot(0, 2)][:], g.ps[:, T_BANK, :], ACT.Copy).then_inc(x_hi_done, 1)
                        if routed and q == COMB_AT and st.has(0):
                            act.wait_ge(shifted, st.n(0))
                            act.activation(pr[:], pr[:], ACT.Exp).then_inc(p_exp, 1)

                run_steps(act, B, OUT_LAG, step, U=2)

            @block.vector
            def _(dve):
                def softmax_top2(st):
                    n, r = st.n(0), st.slot(0, 2)
                    logits = g.ps[:, R_BANK, 0:TB * 8].rearrange("p (t e) -> p t e", t=TB)[:, :, 0:routed]
                    wide = [P, TB, routed]
                    cube = [P, TB, routed, routed]
                    link = Link(dve, chain, n, 12)
                    if isinstance(st.i, int) and n == 1:
                        dve.wait_ge(small_loaded, 32)
                    dve.wait_ge(lg_ready, n)
                    link(dve.tensor_reduce(mx[:], logits, AX_X, ALU.max))
                    dve.tensor_tensor(pr[:], logits, mx[:, :, None].to_broadcast(wide), ALU.subtract
                                      ).then_inc(shifted, 1)
                    dve.wait_ge(p_exp, n)
                    link(dve.tensor_reduce(sm[:], pr[:], AX_X, ALU.add))
                    link(dve.reciprocal(sm[:], sm[:]))
                    link(dve.tensor_tensor(pr[:], pr[:], sm[:, :, None].to_broadcast(wide), ALU.mult))
                    p_e = pr[:, :, :, None].to_broadcast(cube)
                    p_j = pr[:, :, None, :].to_broadcast(cube)
                    link(dve.tensor_tensor(eq[:], p_j, p_e, ALU.is_equal))
                    link(dve.tensor_tensor(eq[:], eq[:], lower[:, None, :, :].to_broadcast(cube), ALU.mult))
                    link(dve.tensor_tensor(gt[:], p_j, p_e, ALU.is_gt))
                    link(dve.tensor_tensor(gt[:], gt[:], eq[:], ALU.add))
                    link(dve.tensor_reduce(sel[:], gt[:], AX_X, ALU.add))
                    link(dve.scalar_tensor_tensor(pr[:], sel[:], 2.0, pr[:], ALU.is_lt, ALU.mult))
                    link(dve.tensor_reduce(sm[:], pr[:], AX_X, ALU.add))
                    link(dve.tensor_scalar(sm[:], sm[:], 1e-9, None, ALU.add))
                    dve.reciprocal(mx[:], sm[:]).then_inc(recip_done, 1)
                    dve.wait_ge(recip_done, n)
                    wait(dve, cw_ready, routed * (n - 2))
                    dve.tensor_tensor(comb[r][:], pr[:], mx[:, :, None].to_broadcast(wide), ALU.mult
                                      ).then_inc(comb_done, 1)

                def add_up(st, k, e):
                    n = st.n(k)
                    bank = g.ps[:, D_BANK + (E * (st.c - k - 1) + e) % 2, :]
                    dve.wait_ge(d_ready, E * (n - 1) + e + 1)
                    if e == 0:
                        wait(dve, out_ready, n - 1)
                        dve.tensor_copy(acc[:], bank).then_inc(d_read, 1)
                        return
                    dve.wait_ge(cw_done, routed * (n - 1) + e)
                    wait(dve, acc_done, routed * (n - 1) + e - 1)
                    dve.tensor_tensor(part[:], bank, cw[:, e % 2, :], ALU.mult).then_inc(d_read, 1)
                    dve.wait_ge(d_read, E * (n - 1) + e + 1)
                    dve.tensor_tensor(acc[:], acc[:], part[:], ALU.add).then_inc(acc_done, 1)

                def step(st):
                    if isinstance(st.i, int) and st.i == 0 and st.c == 1 and quant:
                        dve.wait_ge(stage_loaded[0], 16)
                        dve.tensor_scalar(stage_f[:, 0, :], stage[:, 0, :], float(np.float32(1.0 / 127.0)), None,
                                          ALU.mult).then_inc(dequant_done, 1)
                    for q in range(EC):
                        e, c = divmod(q, C)
                        if isinstance(st.i, int) and st.c + 2 * st.i == 2 and c == 0:
                            dve.wait_ge(w_hi_done, e + 1)
                            dve.tensor_tensor(w_lo[:, e, :], stage_f[:, e % 2, :], w_hi[:, e, :].bitcast(F32),
                                              ALU.subtract).then_inc(w_done, 1)
                        if st.has(1):
                            m, par = position(st, 1, q)
                            dve.wait_ge(gate_done, m)
                            wait(dve, h_lo_done, m - C)
                            dve.tensor_tensor(h[:, c, :], gate[:, par, :], g.ps[:, U_BANK + par, :], ALU.mult
                                              ).then_inc(h_done, 1)
                        for k, qq in (((1, q - 1),) if q else ((2, EC - 1),)):
                            if st.has(k):
                                m, _ = position(st, k, qq)
                                dve.wait_ge(h_hi_done, m)
                                dve.tensor_tensor(h_lo[:, qq % C, :], h[:, qq % C, :],
                                                  h_hi[:, qq % C, :].bitcast(F32), ALU.subtract).then_inc(h_lo_done, 1)
                        for e2 in range(E):
                            at = C * e2 + C + 2
                            if at == q and st.has(1):
                                add_up(st, 1, e2)
                            if at - EC == q and st.has(2):
                                add_up(st, 2, e2)
                        if q == OUT_AT + 1 and st.has(OUT_LAG):
                            dve.wait_ge(out_ready, st.n(OUT_LAG))
                            dst = batch_of(g.x_all, st.n(OUT_LAG))
                            dve.tensor_tensor(dst, g.ps[:, T_BANK, :].rearrange("p (t d) -> p t d", t=TB), dst,
                                              ALU.add).then_inc(out_added, 1)
                        if q == X_AT - 1 and st.has(0):
                            wait(dve, xp_ready, st.n(0) - 1)
                            normalise(dve, g.x_all, g.mean_var, g.rstd, st.n(0), xn, xn_done)
                        if q == X_AT and st.has(0):
                            dve.wait_ge(x_hi_done, st.n(0))
                            dve.tensor_tensor(x_lo[st.slot(0, 2)][:], g.ps[:, T_BANK, :],
                                              x_hi[st.slot(0, 2)][:].bitcast(F32), ALU.subtract).then_inc(x_lo_done, 1)
                        if routed and q == COMB_AT and st.has(0):
                            softmax_top2(st)

                run_steps(dve, B, OUT_LAG, step, U=2)


class Memory:
    pass


def build(nc, a, out, layers=range(8)):
    g = Memory()
    dram = lambda name, shape: nc.dram_tensor(name, shape, F32).ap()
    g.q_hi8, g.q_lo8, g.k_hi8, g.k_lo8 = (dram(k, [B * P, S]) for k in ("q_hi8", "q_lo8", "k_hi8", "k_lo8"))
    g.v8 = dram("v8", [B * 4, S, P])
    g.o8 = dram("o8", [B * 4, TB, P, 32])
    g.q_hi, g.q_lo, g.k_hi, g.k_lo = (dram(k, [B * 8, P, S]) for k in ("q_hi", "q_lo", "k_hi", "k_lo"))
    g.v32 = dram("v32", [B * 8, S, P])
    g.o32 = dram("o32", [B * 8, TB, P, P])
    g.lines = dram("lines", [16, 1024])
    g.strips = dram("strips", [16, P, STRIP])
    g.pick, g.w_qkv, g.b_out = a["pick"], a["b0_wqkv"], a["b0_bout"]
    g.w_out32 = [a["b0_wout"][k * P:(k + 1) * P, :] for k in range(8)]
    with ExitStack() as stack:
        sb = lambda name, shape, dt=F32: stack.enter_context(nc.sbuf_tensor(name, shape, dt))
        g.ps = stack.enter_context(nc.psum_tensor("ps", [P, 8, 512], F32))
        g.x_all = sb("x_all", [P, TILES, DM])
        g.mean_var = sb("mean_var", [P, TILES, 2])
        g.rstd = sb("rstd", [P, TILES])
        g.ident = sb("ident", [P, P])
        g.decay_strip = sb("decay_strip", [P, STRIP])
        x_tiles = a["x"].rearrange("(t p) d -> p t d", p=P)
        g.w_out8 = {"out_a0": a["a0_wo"], "out_a1": a["a1_wo"]}
        with Phase(nc, "begin") as ph:
            loaded = ph.sem("loaded")
            with nc.Block() as block:
                @block.sync
                def _(sp):
                    sp.dma_start(g.x_all[:], x_tiles).then_inc(loaded, 16)
                    sp.dma_start(g.ident[:], a["ident"]).then_inc(loaded, 16)
                    sp.dma_start(g.decay_strip[:], a["decay_strip"]).then_inc(loaded, 16)
                    sp.wait_ge(loaded, 48)

        if 0 in layers:
            row_stats(nc, "st_a0", g.x_all, g.mean_var, g.rstd, 1e-5)
            scale = float(np.float32(1.0) / (np.sqrt(np.float32(DM)) + np.float32(1e-8)))
            project_small(nc, g, "in_a0", scale, (a["a0_wdown"], a["a0_wupk"], a["a0_wupv"]),
                          (a["a0_wq"], a["a0_wk"], a["a0_wv"]))
            attend_small(nc, g, "at_a0", True)
            project_out(nc, g, "out_a0", False)
        def mixture(k):
            row_stats(nc, f"st_moe{k}", g.x_all, g.mean_var, g.rstd, 1e-5)
            swiglu(nc, g, f"moe{k}", a["moe_w"], EXPERTS, DFF // P, (a["router"], a["lower"]))

        def quantised(k):
            row_stats(nc, f"st_ffn{k}", g.x_all, g.mean_var, g.rstd, 1e-5)
            swiglu(nc, g, f"ffn{k}", a["ffn_w"], 1, HID // P)

        if 1 in layers:
            mixture(1)
        if 2 in layers:
            row_stats(nc, "st_b0", g.x_all, g.mean_var, g.rstd, 1e-5)
            project_wide(nc, g, "in_b0", 32 ** -0.5)
            attend_wide(nc, g, "at_b0")
            with nc.sbuf_tensor("y_all", [P, TILES, DM], F32) as g.y_all:
                project_out(nc, g, "out_b0", True)
                row_stats(nc, "st_y", g.y_all, g.mean_var, g.rstd, 1e-6)
                add_normalised(nc, g, "ln_b0", g.y_all, a["b0_gamma"], a["b0_beta"])
        if 3 in layers:
            mixture(3)
        if 4 in layers:
            bias_strips(nc, g, "bias_a1", a["taps"], a["line_table"], a["wpos"], a["flip"])
            row_stats(nc, "st_a1", g.x_all, g.mean_var, g.rstd, 1e-5)
            project_small(nc, g, "in_a1", 8 ** -0.5, None, [a["a1_wqkv"][:, k * P:(k + 1) * P] for k in range(3)])
            attend_small(nc, g, "at_a1", False)
            project_out(nc, g, "out_a1", False)
        if 5 in layers:
            quantised(5)
        if 6 in layers:
            row_stats(nc, "st_lin", g.x_all, g.mean_var, g.rstd, 1e-5)
            with nc.sbuf_tensor("z_all", [P, TILES, DM], F32) as g.y_all:
                linear_attention(nc, g, "lin", {k[4:]: v for k, v in a.items() if k.startswith("lin_")})
                row_stats(nc, "st_z", g.y_all, g.mean_var, g.rstd, 1e-5)
                add_normalised(nc, g, "ln_lin", g.y_all, a["ln_gamma"], a["ln_beta"])
        if 7 in layers:
            quantised(7)
        with Phase(nc, "end") as ph:
            stored = ph.sem("stored")
            with nc.Block() as block:
                @block.sync
                def _(sp):
                    sp.dma_start(out.rearrange("(t p) d -> p t d", p=P), g.x_all[:]).then_inc(stored, 16)
                    sp.wait_ge(stored, 16)


def pack(gate, up, down):
    import numpy as np
    chunks = down.T.reshape(-1, 128, 128)
    return np.concatenate([gate.T, up.T, *chunks], axis=1)


def line_table():
    import numpy as np
    ramp = np.linspace(0.0, 1.0, 64, dtype=np.float32)
    rel = np.abs(np.arange(1024) - 511).astype(np.float32) / np.float32(511)
    point = np.clip(np.round(rel * np.float32(63)).astype(np.int64), 0, 63)
    at = point[None, :] - np.arange(101)[:, None]
    return np.where(at >= 0, ramp[np.maximum(at, 0)], np.float32(0)).astype(np.float32)


def linear_layouts(f):
    import numpy as np
    row = np.arange(128)
    h, d = row // 4, row % 4
    m, hm = np.arange(64) // 32, np.arange(64) % 32
    pad = lambda t: np.concatenate([t, np.zeros_like(t)], axis=0)
    wq, wk, wv, wb, wm = (f[f"L1_attn_b_{k}"] for k in ("Wq", "Wk", "Wv", "Wbeta", "Wmix"))
    bb, bm = f["L1_attn_b_bbeta"], f["L1_attn_b_bmix"]
    swap = 4 * h + (d + 2) % 4
    w = [wq, wq[swap], wk, wk[swap], wb[2 * h], wb[2 * h + 1], pad(wm[2 * hm + m]), pad(wm[2 * hm + 1 - m])]
    w += [wv[4 * h + c] for c in range(4)]
    freq = np.where(d % 2 == 0, np.float32(1.0), np.float32(1.0) / np.float32(10000.0) ** np.float32(0.5))
    angle = np.arange(512, dtype=np.float32)[None, :] * freq.astype(np.float32)[:, None]
    sign = np.where(d < 2, np.float32(-1), np.float32(1))[:, None]
    one = np.float32(1)
    return {
        "lin_w": np.stack(w).transpose(2, 0, 1),
        "lin_w_out": f["L1_attn_b_Wout"].T, "lin_bout": f["L1_attn_b_bout"],
        "lin_bias": np.stack([bb[2 * h], bb[2 * h + 1], pad(bm[2 * hm + m]), pad(bm[2 * hm + 1 - m])], axis=1),
        "lin_rope": np.stack([np.cos(angle), np.sin(angle) * sign], axis=1).astype(np.float32),
        "lin_to_c": ((h[:, None, None] == h) & (np.arange(4)[:, None] == d)) * one,
        "lin_to_m": ((h[:, None, None] == hm) & (np.arange(2)[:, None] == m)) * one,
        "lin_from_m": np.stack([pad(((hm[:, None] == h) & (m[:, None] == k)) * one) for k in range(2)], axis=1),
        "ln_gamma": f["L1_attn_b_ln_g"], "ln_beta": f["L1_attn_b_ln_b"],
    }


def laid_out(i):
    import numpy as np
    f = {k: np.asarray(v) for k, v in i.items()}
    p = np.arange(128)[:, None]
    strip_delta = np.abs(np.arange(896)[None, :] - p - 384).astype(np.float32)
    d = {
        "x": f["L0_attn_a_x"].reshape(-1, 128),
        "ident": np.eye(128, dtype=np.float32),
        "decay_strip": np.exp(np.float32(-0.01 * 0.01) * strip_delta).astype(np.float32),
        "a0_wq": f["L0_attn_a_Wq"], "a0_wk": f["L0_attn_a_Wk"], "a0_wv": f["L0_attn_a_Wv"],
        "a0_wo": f["L0_attn_a_Wo"], "a0_wdown": f["L0_attn_a_W_down_kv"],
        "a0_wupk": f["L0_attn_a_W_up_k"], "a0_wupv": f["L0_attn_a_W_up_v"],
        "a1_wo": f["L1_attn_a_Wout"].T, "a1_wqkv": f["L1_attn_a_Wqkv"].T,
        "taps": f["L1_attn_a_coeffs"].T, "wpos": f["L1_attn_a_Wpos"].T,
        "line_table": line_table(), "flip": np.eye(128, dtype=np.float32)[::-1],
        "pick": np.eye(128, dtype=np.float32)[:, ::32],
        "b0_wqkv": f["L0_attn_b_w_qkv"], "b0_wout": f["L0_attn_b_w_out"], "b0_bout": f["L0_attn_b_b_out"],
        "b0_gamma": f["L0_attn_b_ln_gamma"], "b0_beta": f["L0_attn_b_ln_beta"],
        "moe_w": np.stack([pack(*w) for w in [
            (f["L0_ffn_shared_gate"], f["L0_ffn_shared_up"], f["L0_ffn_shared_down"]),
            *zip(f["L0_ffn_routed_gate"], f["L0_ffn_routed_up"], f["L0_ffn_routed_down"])]]),
        "router": f["L0_ffn_router_w"].T,
        "lower": np.tril(np.ones((7, 7), np.float32), -1),
        "ffn_w": pack(f["L1_ffn_w_gate"], f["L1_ffn_w_up"], f["L1_ffn_w_down"])[None],
    }
    d.update(linear_layouts(f))
    return {k: np.ascontiguousarray(v) for k, v in d.items()}


def kernel(**inputs):
    import concourse.bacc as _bacc
    from concourse import mybir as _mybir
    from concourse.bass_utils import run_bass_kernel_spmd as _run

    nc = _bacc.Bacc("TRN2", target_bir_lowering=False, num_devices=1)
    arrays = laid_out(inputs)
    a = {k: nc.dram_tensor(f"in_{k}", v.shape, _mybir.dt.from_np(v.dtype), kind="ExternalInput").ap()
         for k, v in arrays.items()}
    out = nc.dram_tensor("out", (8 * 512, 128), _mybir.dt.float32, kind="ExternalOutput").ap()
    build(nc, a, out)
    r = _run(nc, [{f"in_{k}": v for k, v in arrays.items()}], core_ids=[0])
    return r.results[0]["out"].reshape(8, 512, 128)
```

```python
from contextlib import ExitStack

import concourse.bass as bass
import numpy as np
from concourse import mybir

ALU = mybir.AluOpType
ACT = mybir.ActivationFunctionType
F32 = mybir.dt.float32
F32R = mybir.dt.float32r
I32 = mybir.dt.int32
AX_X = mybir.AxisListType.X

P = 128
B, S, DM = 8, 512, 128
TB = S // P
TILES = B * TB
HG = 4
KROWS = 96
CLAMP = 10000.0
STRIP = S + (TB - 1) * P
STRIP0 = (TB - 1) * P
EXPERTS, DFF = 8, 512
HID = 384


class Phase:

    def __init__(self, nc, name):
        self.nc, self.name = nc, name

    def __enter__(self):
        self.stack = ExitStack().__enter__()
        self.sems = []
        return self

    def sb(self, name, shape, dt=F32):
        return self.stack.enter_context(self.nc.sbuf_tensor(f"{self.name}_{name}", shape, dt))

    def sem(self, name):
        s = self.stack.enter_context(self.nc.semaphore(f"{self.name}_{name}"))
        self.sems.append(s)
        return s

    def __exit__(self, *exc):
        if exc[0] is None:
            for s in self.sems:
                self.nc.sync.sem_clear(s)
            self.nc.all_engine_barrier()
        return self.stack.__exit__(*exc)


def wait(eng, sem, value):
    if isinstance(value, int) and value <= 0:
        return
    eng.wait_ge(sem, value)


def settle(eng, sem):
    eng.sem_inc(sem, 1)


class Link:

    def __init__(self, eng, sem, n, k, done=0):
        self.eng, self.sem, self.n, self.k, self.done = eng, sem, n, k, done

    def __call__(self, ins):
        self.done += 1
        assert self.done <= self.k
        ins.then_inc(self.sem, 1)
        self.eng.wait_ge(self.sem, self.k * (self.n - 1) + self.done)


class Step:

    def __init__(self, i, c, count, U=4):
        self.i, self.c, self.count, self.U = i, c, count, U

    def has(self, k):
        return not isinstance(self.i, int) or 1 <= self.U * self.i + self.c - k <= self.count

    def n(self, k):
        return self.U * self.i + (self.c - k)

    def slot(self, k, ring):
        return (self.c - k) % ring

    def use(self, k, ring):
        return self.U // ring * self.i + (self.c - k + ring - 1) // ring


def run_steps(eng, count, extra, step, U=4):
    peeled = max(1, -(-extra // U))
    for i in range(peeled):
        for c in range(1, U + 1):
            step(Step(i, c, count, U))
    with eng.Fori(peeled, count // U) as i:
        for c in range(1, U + 1):
            step(Step(i, c, count, U))
    for c in range(1, extra + 1):
        step(Step(count // U, c, count, U))


RSQRT_LINKS = 12


def rsqrt(dve, link, var, eps, y, t):
    y_bits, t_bits = y.bitcast(I32), t.bitcast(I32)
    link(dve.tensor_scalar(var, var, eps, None, ALU.add))
    link(dve.tensor_scalar(t_bits, var.bitcast(I32), 1, None, ALU.logical_shift_right))
    link(dve.tensor_scalar(y_bits, t_bits, -1.0, float(0x5F3759DF), ALU.mult, ALU.add))
    for _ in range(3):
        link(dve.tensor_tensor(t, y, y, ALU.mult))
        link(dve.scalar_tensor_tensor(t, t, -0.5, var, ALU.mult, ALU.mult))
        link(dve.scalar_tensor_tensor(y, t, 1.5, y, ALU.add, ALU.mult))


def row_stats(nc, name, x_all, mean_var, rstd, eps):
    with Phase(nc, name) as ph:
        stats = ph.sb("stats", [P, TILES, 6])
        t = ph.sb("t", [P, TILES])
        var = ph.sb("var", [P, TILES])
        stats_done, aggr_done, chain = ph.sem("stats_done"), ph.sem("aggr_done"), ph.sem("chain")
        with nc.Block() as block:
            @block.vector
            def _(dve):
                for tile in range(TILES):
                    dve.bn_stats(stats[:, tile, :], x_all[:, tile, :]).then_inc(stats_done, 1)
                dve.wait_ge(stats_done, TILES)
                for tile in range(TILES):
                    dve.bn_aggr(mean_var[:, tile, :], stats[:, tile, :]).then_inc(aggr_done, 1)
                dve.wait_ge(aggr_done, TILES)
                link = Link(dve, chain, 1, RSQRT_LINKS + 1)
                link(dve.tensor_copy(var[:], mean_var[:, :, 1]))
                rsqrt(dve, link, var[:], eps, rstd[:], t[:])


def normalise(dve, x_all, mean_var, rstd, n, xn, done):
    for tb in range(TB):
        tile = (n - 1) * TB + tb
        if isinstance(tile, int):
            x, m, r = x_all[:, tile, :], mean_var[:, tile, 0:1], rstd[:, tile:tile + 1]
        else:
            x = x_all[:, bass.ds(tile, 1), :].rearrange("p a n -> p (a n)")
            m = mean_var[:, bass.ds(tile, 1), 0:1].rearrange("p a n -> p (a n)")
            r = rstd[:, bass.ds(tile, 1)]
        dve.tensor_scalar(xn[:, tb, :], x, m, r, ALU.subtract, ALU.mult).then_inc(done, 1)


def batch_of(x_all, n):
    return x_all[:, bass.ds((n - 1) * TB, TB), :]


def item(dram, n):
    return dram[bass.ds(n - 1, 1)]


def project_small(nc, g, name, scale, latent, weights):
    with Phase(nc, name) as ph:
        n_w = len(weights)
        w = ph.sb("w", [P, n_w, DM])
        wd, wu = (ph.sb("wd", [P, 32]), ph.sb("wu", [32, 2, DM])) if latent else (None, None)
        xn = ph.sb("xn", [P, TB, DM])
        xT = ph.sb("xT", [P, S])
        kv = ph.sb("kv", [P, S])
        lat = ph.sb("lat", [32, S])
        hi = ph.sb("hi", [P, 2, S], F32R)
        lo = ph.sb("lo", [P, 2, S], F32R)
        va = ph.sb("va", [P, TB, 16, 32])
        w_loaded = ph.sem("w_loaded")
        ones_set = ph.sem("ones_set")
        xn_done, xn_free, xp_ready, xT_done, xT_free = (ph.sem(k) for k in ("xn_done", "xn_free", "xp_ready", "xT_done", "xT_free"))
        proj_done, hi_done, lo_done, v_done = (ph.sem(k) for k in ("proj_done", "hi_done", "lo_done", "v_done"))
        kv_ready, kv_done, lat_ready, lat_done = (ph.sem(k) for k in ("kv_ready", "kv_done", "lat_ready", "lat_done"))
        stored = ph.sem("stored")
        bank_x, bank_q, bank_k, bank_kv, bank_lat, bank_v = (g.ps[:, k, :] for k in range(6))
        n_loads = n_w + (3 if latent else 0)
        q_w = w[:, 0, :]

        with nc.Block() as block:
            @block.sync
            def _(sp):
                for k, src in enumerate(weights):
                    sp.dma_start(w[:, k, :], src).then_inc(w_loaded, 16)
                if latent:
                    for dst, src in zip((wd[:], wu[:, 0, :], wu[:, 1, :]), latent):
                        sp.dma_start(dst, src).then_inc(w_loaded, 16)
                with sp.Fori(1, B + 1) as n:
                    sp.wait_ge(lo_done, 2 * n)
                    for k, (dh, dl) in enumerate(((g.q_hi8, g.q_lo8), (g.k_hi8, g.k_lo8))):
                        sp.dma_start(dh[bass.ds((n - 1) * P, P), :], hi[:, k, :].bitcast(F32)).then_inc(stored, 16)
                        sp.dma_start(dl[bass.ds((n - 1) * P, P), :], lo[:, k, :].bitcast(F32)).then_inc(stored, 16)
                    sp.wait_ge(v_done, n)
                    for hg in range(4):
                        sp.dma_start(g.v8[bass.ds((n - 1) * 4 + hg, 1)].rearrange("a (t p) n -> p (a t) n", p=P),
                                     va[:, :, hg * HG:(hg + 1) * HG, :].rearrange("p t h d -> p t (h d)")
                                     ).then_inc(stored, 16)
                sp.wait_ge(stored, 16 * 8 * (B + 1))

            @block.vector
            def _(dve):
                dve.memset(va[:], 0.0).then_inc(ones_set, 1)
                dve.wait_ge(ones_set, 1)
                dve.memset(va[:, :, :, 8:9], 1.0).then_inc(ones_set, 1)
                dve.wait_ge(ones_set, 2)
                dve.sem_inc(xn_free, 1)
                dve.sem_inc(stored, 16 * 8)
                with dve.Fori(1, B + 1) as n:
                    dve.wait_ge(xn_free, n)
                    normalise(dve, g.x_all, g.mean_var, g.rstd, n, xn, xn_done)
                    for k, bank in enumerate((bank_q, bank_k)):
                        dve.wait_ge(hi_done, 2 * (n - 1) + k + 1)
                        dve.scalar_tensor_tensor(lo[:, k, :], bank, scale if k == 0 else 1.0, hi[:, k, :].bitcast(F32),
                                                 ALU.mult, ALU.subtract).then_inc(lo_done, 1)
                    dve.wait_ge(proj_done, 3 * n)
                    dve.wait_ge(stored, 16 * 8 * n)
                    dve.tensor_copy(va[:, :, :, 0:8], bank_v.rearrange("p (t h d) -> p t h d", t=TB, d=8)
                                    ).then_inc(v_done, 1)

            @block.scalar
            def _(act):
                act.sem_inc(xT_free, 1)
                with act.Fori(1, B + 1) as n:
                    act.wait_ge(xT_free, n)
                    act.wait_ge(xp_ready, n)
                    act.activation(xT[:], bank_x, ACT.Copy).then_inc(xT_done, 1)
                    if latent:
                        act.wait_ge(kv_ready, n)
                        act.activation(kv[:], bank_kv, ACT.Copy).then_inc(kv_done, 1)
                        act.wait_ge(lat_ready, n)
                        act.activation(lat[:], bank_lat[0:32, :], ACT.Copy).then_inc(lat_done, 1)
                    act.wait_ge(stored, 16 * 8 * n)
                    for k, bank in enumerate((bank_q, bank_k)):
                        act.wait_ge(proj_done, 3 * (n - 1) + k + 1)
                        act.activation(hi[:, k, :], bank, ACT.Copy,
                                       scale=scale if k == 0 else 1.0).then_inc(hi_done, 1)

            @block.tensor
            def _(pe):
                pe.wait_ge(w_loaded, 16 * n_loads)
                with pe.Fori(1, B + 1) as n:
                    pe.wait_ge(xn_done, TB * n)
                    for tb in range(TB):
                        ins = pe.transpose(bank_x[:, tb * P:(tb + 1) * P], xn[:, tb, :], g.ident[:])
                    ins.then_inc(xp_ready, 1)
                    pe.wait_ge(xT_done, n)
                    pe.sem_inc(xn_free, 1)
                    pe.matmul(bank_q, q_w, xT[:], start=True, stop=True).then_inc(proj_done, 1)
                    if latent:
                        pe.matmul(bank_kv, w[:, 1, :], xT[:], start=True, stop=False)
                        pe.matmul(bank_kv, w[:, 2, :], xT[:], start=False, stop=True).then_inc(kv_ready, 1)
                        pe.wait_ge(kv_done, n)
                        pe.matmul(bank_lat[0:32, :], wd[:], kv[:], start=True, stop=True).then_inc(lat_ready, 1)
                        pe.wait_ge(lat_done, n)
                        pe.matmul(bank_k, wu[:, 0, :], lat[:], start=True, stop=True).then_inc(proj_done, 1)
                        for tb in range(TB):
                            ins = pe.matmul(bank_v[:, tb * P:(tb + 1) * P], lat[:, tb * P:(tb + 1) * P],
                                            wu[:, 1, :], start=True, stop=True)
                    else:
                        pe.matmul(bank_k, w[:, 1, :], xT[:], start=True, stop=True).then_inc(proj_done, 1)
                        for tb in range(TB):
                            ins = pe.matmul(bank_v[:, tb * P:(tb + 1) * P], xT[:, tb * P:(tb + 1) * P],
                                            w[:, 2, :], start=True, stop=True)
                    ins.then_inc(proj_done, 1)
                    pe.wait_ge(v_done, n)
                    pe.wait_ge(lo_done, 2 * n)
                    pe.sem_inc(xT_free, 1)


def attend_small(nc, g, name, decay):
    NG = B * 4
    with Phase(nc, name) as ph:
        q4 = [ph.sb(f"q4_{r}", [P, HG, S], F32R) for r in range(2)]
        k4 = [ph.sb(f"k4_{r}", [P, HG, S], F32R) for r in range(2)]
        v4 = [ph.sb(f"v4_{r}", [P, TB, P]) for r in range(4)]
        decay_strip = ph.sb("decay_strip", [P, STRIP]) if decay else None
        strip = None if decay else [ph.sb(f"strip{r}", [P, HG, STRIP]) for r in range(2)]
        clipped = ph.sb("clipped", [P, TB, S]) if decay else None
        logits = ph.sb("logits", [P, 2, TB, S])
        top = ph.sb("top", [P, 2, TB])
        neg_top = ph.sb("neg_top", [P, 2, TB])
        e = ph.sb("e", [P, HG, TB, S])
        eT = [ph.sb(f"eT_{r}", [P, HG, TB, S]) for r in range(2)]
        o_sb = ph.sb("o_sb", [P, S])
        r16 = ph.sb("r16", [P, TB, HG])
        o_tok = [ph.sb(f"o_tok{r}", [P, TB, HG, 8]) for r in range(2)]
        zeroed, decay_loaded = ph.sem("zeroed"), ph.sem("decay_loaded")
        loaded = [ph.sem(f"loaded{r}") for r in range(2)]
        v_loaded = [ph.sem(f"v_loaded{r}") for r in range(4)]
        s_ready, logits_done, top_done = ph.sem("s_ready"), ph.sem("logits_done"), ph.sem("top_done")
        clip_done = ph.sem("clip_done")
        dve_settled, sp_settled = ph.sem("dve_settled"), ph.sem("sp_settled")
        s_read = clip_done if decay else logits_done
        exp_done, tr_ready = ph.sem("exp_done"), ph.sem("tr_ready")
        tr_read = [ph.sem(f"tr_read{kb}") for kb in range(TB)]
        pv_done, o_copied, oT_ready, recip_done, o_done = (
            ph.sem(k) for k in ("pv_done", "o_copied", "oT_ready", "recip_done", "o_done"))
        stored = [ph.sem(f"stored{r}") for r in range(2)]
        S_BANK, TR_BANK, PV_BANK, OT_BANK = 0, 2, 6, 7
        on_dve = () if decay else (3,)
        n_loads = 6 * 16 + (0 if decay else 16)

        with nc.Block() as block:
            @block.gpsimd
            def _(pool):
                for r in range(2):
                    pool.memset(q4[r][:].bitcast(F32), 0.0).then_inc(zeroed, 1)
                    pool.memset(k4[r][:].bitcast(F32), 0.0).then_inc(zeroed, 1)

            @block.sync
            def _(sp):
                if decay:
                    sp.dma_start(decay_strip[:], g.decay).then_inc(decay_loaded, 16)
                sp.wait_ge(zeroed, 4)

                def step(st):
                    if st.has(0):
                        n, r, rv = st.n(0), st.slot(0, 2), st.slot(0, 4)
                        wait(sp, s_ready, 16 * (n - 2))
                        if not decay:
                            wait(sp, logits_done, 16 * (n - 2))
                        settle(sp, sp_settled)
                        for row, dq, dk in ((0, g.q_hi8, g.k_hi8), (32, g.q_hi8, g.k_lo8), (64, g.q_lo8, g.k_hi8)):
                            for dst, src in ((q4[r], dq), (k4[r], dk)):
                                sp.dma_start(dst[row:row + 8].bitcast(F32),
                                             src[bass.ds((n - 1) * 32, 32), :].rearrange("(j d) n -> d j n", d=8)
                                             ).then_inc(loaded[r], 16)
                        if not decay:
                            hg = (st.c - 1) % 4
                            sp.dma_start(strip[r][:], g.strips[hg * HG:(hg + 1) * HG].rearrange("h p n -> p h n")
                                         ).then_inc(loaded[r], 16)
                        wait(sp, pv_done, n - 4)
                        settle(sp, sp_settled)
                        sp.dma_start(v4[rv][:], item(g.v8, n).rearrange("a (t p) n -> p (a t) n", p=P)
                                     ).then_inc(v_loaded[rv], 16)
                    if st.has(4):
                        sp.wait_ge(o_done, st.n(4))
                        settle(sp, sp_settled)
                        r = st.slot(4, 2)
                        sp.dma_start(item(g.o8, st.n(4)).rearrange("a t p c -> p (a t) c"),
                                     o_tok[r][:].rearrange("p t j d -> p t (j d)")).then_inc(stored[r], 16)

                run_steps(sp, NG, 4, step)
                for r in range(2):
                    sp.wait_ge(stored[r], 16 * NG // 2)

            @block.tensor
            def _(pe):
                def scores(n, r, j, blocks):
                    for qb in blocks:
                        wait(pe, s_read, 16 * (n - 1) + 4 * j + qb - 1)
                        pe.matmul(g.ps[:, S_BANK + qb % 2, :], q4[r][0:KROWS, j, qb * P:(qb + 1) * P],
                                  k4[r][0:KROWS, j, :], start=True, stop=True).then_inc(s_ready, 1)

                def transposes(n, j, blocks):
                    pe.wait_ge(exp_done, 16 * (n - 1) + 4 * j + 4)
                    for kb in blocks:
                        wait(pe, tr_read[kb], 4 * (n - 1) + j)
                        for qb in range(TB):
                            ins = pe.transpose(g.ps[:, TR_BANK + kb, qb * P:(qb + 1) * P],
                                               e[:, j, qb, kb * P:(kb + 1) * P], g.ident[:])
                        ins.then_inc(tr_ready, 1)

                def product(n, r, rv, kb):
                    if kb == 0:
                        for k in range(TB):
                            pe.wait_ge(tr_read[k], 4 * n)
                        wait(pe, o_copied, n - 1)
                    for j in range(HG):
                        ins = pe.matmul(g.ps[32 * j:32 * j + 32, PV_BANK, :], v4[rv][:, kb, 32 * j:32 * j + 32],
                                        eT[r][:, j, kb, :], start=(kb == 0), stop=(kb == TB - 1))
                    if kb == TB - 1:
                        ins.then_inc(pv_done, 1)

                def turn(n):
                    pe.wait_ge(o_copied, n)
                    wait(pe, o_done, n - 1)
                    for tb in range(TB):
                        ins = pe.transpose(g.ps[:, OT_BANK, tb * P:(tb + 1) * P], o_sb[:, tb * P:(tb + 1) * P],
                                           g.ident[:])
                    ins.then_inc(oT_ready, 1)

                def step(st):
                    now, before = st.has(0), st.has(1)
                    if now:
                        pe.wait_ge(loaded[st.slot(0, 2)], n_loads * st.use(0, 2))
                    for j in range(HG):
                        k, jt = (0, j - 2) if j >= 2 else (1, j + 2)
                        for blocks, turned in (((0, 1), (0, 1)), ((2,), (2,)), ((3,), (3,))):
                            if now:
                                scores(st.n(0), st.slot(0, 2), j, blocks)
                            if st.has(k):
                                transposes(st.n(k), jt, turned)
                        if before and j >= 2:
                            if j == 2:
                                pe.wait_ge(v_loaded[st.slot(1, 4)], 16 * st.use(1, 4))
                            for kb in (2 * j - 4, 2 * j - 3):
                                product(st.n(1), st.slot(1, 2), st.slot(1, 4), kb)
                        if j == 1 and st.has(2):
                            turn(st.n(2))

                run_steps(pe, NG, 2, step)

            @block.scalar
            def _(act):
                def copies(n, r, j):
                    for kb in range(TB):
                        if kb in on_dve:
                            continue
                        act.wait_ge(tr_ready, 16 * (n - 1) + 4 * j + kb + 1)
                        if kb == 0 and j == 0:
                            wait(act, pv_done, n - 2)
                        act.activation(eT[r][:, j, kb, :], g.ps[:, TR_BANK + kb, :], ACT.Copy).then_inc(tr_read[kb], 1)

                def exps(n, j):
                    act.wait_ge(top_done, 4 * (n - 1) + j + 1)
                    wait(act, tr_ready, 16 * (n - 1) + 4 * j - 12)
                    for qb in range(TB):
                        act.activation(e[:, j, qb, :], logits[:, j % 2, qb, :], ACT.Exp,
                                       bias=neg_top[:, j % 2, qb:qb + 1]).then_inc(exp_done, 1)

                def copy_out(n):
                    act.wait_ge(pv_done, n)
                    wait(act, oT_ready, n - 1)
                    act.activation(o_sb[:], g.ps[:, PV_BANK, :], ACT.Copy).then_inc(o_copied, 1)

                def step(st):
                    for j in range(HG):
                        k, jt = (0, j - 2) if j >= 2 else (1, j + 2)
                        if st.has(k):
                            copies(st.n(k), st.slot(k, 2), jt)
                        if j == 0 and st.has(2):
                            copy_out(st.n(2))
                        if st.has(0):
                            exps(st.n(0), j)

                run_steps(act, NG, 2, step)

            @block.vector
            def _(dve):
                if decay:
                    dve.wait_ge(decay_loaded, 16)

                def clip(n, j, qb):
                    dve.wait_ge(s_ready, 16 * (n - 1) + 4 * j + qb + 1)
                    dve.tensor_scalar(clipped[:, qb, :], g.ps[:, S_BANK + qb % 2, :], -CLAMP, CLAMP,
                                      ALU.max, ALU.min).then_inc(clip_done, 1)

                def head(n, r, j):
                    wait(dve, exp_done, 16 * (n - 1) + 4 * j - 4)
                    if decay:
                        clip(n, j, 0)
                    for qb in range(TB):
                        k = 16 * (n - 1) + 4 * j + qb + 1
                        cols = slice(STRIP0 - qb * P, STRIP0 - qb * P + S)
                        if decay:
                            dve.wait_ge(clip_done, k)
                            if qb + 1 < TB:
                                clip(n, j, qb + 1)
                            else:
                                settle(dve, dve_settled)
                            dve.tensor_tensor_reduce(logits[:, j % 2, qb, :], clipped[:, qb, :], decay_strip[:, cols],
                                                     1.0, -3e38, ALU.mult, ALU.max, top[:, j % 2, qb:qb + 1]
                                                     ).then_inc(logits_done, 1)
                        else:
                            dve.wait_ge(s_ready, k)
                            settle(dve, dve_settled)
                            dve.tensor_tensor_reduce(logits[:, j % 2, qb, :], g.ps[:, S_BANK + qb % 2, :],
                                                     strip[r][:, j, cols], 1.0, -3e38, ALU.add, ALU.max,
                                                     top[:, j % 2, qb:qb + 1]).then_inc(logits_done, 1)
                    dve.wait_ge(logits_done, 16 * (n - 1) + 4 * j + 4)
                    dve.tensor_scalar(neg_top[:, j % 2, :], top[:, j % 2, :], -1.0, None, ALU.mult).then_inc(top_done, 1)

                def copies(n, r, j):
                    for kb in on_dve:
                        dve.wait_ge(tr_ready, 16 * (n - 1) + 4 * j + kb + 1)
                        if j == 0:
                            wait(dve, pv_done, n - 2)
                        dve.tensor_copy(eT[r][:, j, kb, :], g.ps[:, TR_BANK + kb, :]).then_inc(tr_read[kb], 1)

                def finish(st):
                    n, r = st.n(2), st.slot(2, 2)
                    o = g.ps[:, OT_BANK, :].rearrange("p (t j d) -> p t j d", t=TB, j=HG)
                    dve.wait_ge(oT_ready, n)
                    dve.reciprocal(r16[:], o[:, :, :, 8]).then_inc(recip_done, 1)
                    dve.wait_ge(recip_done, n)
                    wait(dve, stored[r], 16 * (st.use(2, 2) - 1))
                    dve.tensor_tensor(o_tok[r][:], o[:, :, :, 0:8], r16[:, :, :, None].to_broadcast([P, TB, HG, 8]),
                                      ALU.mult).then_inc(o_done, 1)

                def step(st):
                    if not decay and st.has(0):
                        dve.wait_ge(loaded[st.slot(0, 2)], n_loads * st.use(0, 2))
                    for j in range(HG):
                        if st.has(0):
                            head(st.n(0), st.slot(0, 2), j)
                        k, jt = (0, j - 2) if j >= 2 else (1, j + 2)
                        if st.has(k):
                            copies(st.n(k), st.slot(k, 2), jt)
                        if j == 2 and st.has(2):
                            finish(st)

                run_steps(dve, NG, 2, step)


def attend_wide(nc, g, name, scale):
    U = 8
    NG = B * U
    RQ = 4
    W = U * P
    with Phase(nc, name) as ph:
        w = ph.sb("w", [P, 3 * W])
        xn = ph.sb("xn", [P, TB, DM])
        xT, xT_v = ph.sb("xT", [P, S]), ph.sb("xT_v", [P, S])
        q_hi, q_lo, k_hi, k_lo = (ph.sb(k, [P, S], F32R) for k in ("q_hi", "q_lo", "k_hi", "k_lo"))
        q4 = [ph.sb(f"q4_{r}", [P, HG, S], F32R) for r in range(RQ)]
        k4 = [ph.sb(f"k4_{r}", [P, HG, S], F32R) for r in range(RQ)]
        v4 = [ph.sb(f"v4_{r}", [P, TB, P]) for r in range(2)]
        top = ph.sb("top", [P, 2, TB, HG])
        top_hi, top_lo = (ph.sb(k, [HG, S], F32R) for k in ("top_hi", "top_lo"))
        e = [ph.sb(f"e{r}", [P, HG, TB, S]) for r in range(2)]
        e_pair = ph.sb("e_pair", [P, HG, 2, S])
        ones = ph.sb("ones", [P, 32])
        pick = ph.sb("pick", [P, HG])
        o_sb, l_sb = ph.sb("o_sb", [P, S]), ph.sb("l_sb", [P, S])
        r16 = ph.sb("r16", [P, TB, HG])
        o_tok = [ph.sb(f"o_tok{r}", [P, TB, HG, 32]) for r in range(2)]
        sp_settled = ph.sem("sp_settled")
        set_up, pick_loaded, w_loaded = ph.sem("set_up"), ph.sem("pick_loaded"), ph.sem("w_loaded")
        xn_done, xp_ready, xT_done, xT_v_done = (ph.sem(k) for k in ("xn_done", "xp_ready", "xT_done", "xT_v_done"))
        q_ready, q_hi_done, q_lo_done, k_ready, k_hi_done, k_lo_done, v_ready, v_done = (
            ph.sem(k) for k in ("q_ready", "q_hi_done", "q_lo_done", "k_ready", "k_hi_done", "k_lo_done", "v_ready",
                                "v_done"))
        loaded = [ph.sem(f"loaded{r}") for r in range(RQ)]
        row_loaded = [ph.sem(f"row_loaded{r}") for r in range(RQ)]
        s_ready, max_done, tt_ready, hi_done, lo_done, st_ready, exp_done, pair_done, pv_done, o_copied, l_ready, \
            oT_ready, recip_done, o_done = (ph.sem(k) for k in (
                "s_ready", "max_done", "tt_ready", "hi_done", "lo_done", "st_ready", "exp_done", "pair_done",
                "pv_done", "o_copied", "l_ready", "oT_ready", "recip_done", "o_done"))
        stored = [ph.sem(f"stored{r}") for r in range(2)]
        S_BANK, ST_BANK, PV_BANK, TURN_BANK, Q_BANK, K_BANK = 0, 2, 4, 5, 6, 7

        with nc.Block() as block:
            @block.gpsimd
            def _(pool):
                for r in range(RQ):
                    pool.memset(k4[r][KROWS:KROWS + 2].bitcast(F32), 1.0).then_inc(set_up, 1)

                def step(st):
                    if st.has(4):
                        n, r = st.n(4), st.slot(4, 2)
                        for j in range(HG):
                            pool.wait_ge(exp_done, 16 * (n - 1) + 4 * j + 4)
                            if j == 0:
                                wait(pool, pv_done, n - 1)
                            pool.tensor_tensor(e_pair[:, j, :, :], e[r][:, j, 0:2, :], e[r][:, j, 2:4, :], ALU.add
                                               ).then_inc(pair_done, 1)

                run_steps(pool, NG, 5, step, U=U)

            @block.sync
            def _(sp):
                sp.dma_start(w[:], g.w_qkv).then_inc(w_loaded, 16)
                sp.dma_start(pick[:], g.pick).then_inc(pick_loaded, 16)

                def step(st):
                    if st.has(5):
                        r = st.slot(5, 2)
                        sp.wait_ge(o_done, st.n(5))
                        settle(sp, sp_settled)
                        sp.dma_start(item(g.o32, st.n(5)).rearrange("a t p c -> p (a t) c"),
                                     o_tok[r][:].rearrange("p t j d -> p t (j d)")).then_inc(stored[r], 16)
                    if st.has(0):
                        n, r = st.n(0), st.slot(0, RQ)
                        wait(sp, st_ready, 16 * (n - 4))
                        settle(sp, sp_settled)
                        sp.wait_ge(q_lo_done, n)
                        for row, src in ((0, q_hi), (32, q_hi), (64, q_lo)):
                            sp.dma_start(q4[r][row:row + 32].bitcast(F32), src[:].bitcast(F32)).then_inc(loaded[r], 16)
                    if st.has(2):
                        k = st.slot(2, RQ)
                        sp.wait_ge(lo_done, st.n(2))
                        for row, part in ((KROWS, top_hi), (KROWS + 1, top_lo)):
                            sp.dma_start(q4[k][row:row + 1].bitcast(F32), part[:].bitcast(F32)
                                         ).then_inc(row_loaded[k], 16)
                    if st.has(0):
                        n, r = st.n(0), st.slot(0, RQ)
                        sp.wait_ge(k_lo_done, n)
                        for row, src in ((0, k_hi), (32, k_lo), (64, k_hi)):
                            sp.dma_start(k4[r][row:row + 32].bitcast(F32), src[:].bitcast(F32)).then_inc(loaded[r], 16)

                run_steps(sp, NG, 5, step, U=U)
                for r in range(2):
                    sp.wait_ge(stored[r], 16 * NG // 2)

            @block.tensor
            def _(pe):
                pe.wait_ge(set_up, RQ + 1)
                pe.wait_ge(pick_loaded, 16)
                pe.wait_ge(w_loaded, 16)

                def turn_x(st):
                    pe.wait_ge(xn_done, TB * (st.i + 1))
                    wait(pe, k_lo_done, st.n(0) - 1)
                    for tb in range(TB):
                        ins = pe.transpose(g.ps[:, K_BANK, tb * P:(tb + 1) * P], xn[:, tb, :], g.ident[:])
                    ins.then_inc(xp_ready, 1)

                def project_q(st):
                    if st.c == 1:
                        pe.wait_ge(xT_done, st.i + 1)
                    if st.has(4):
                        wait(pe, v_done, st.n(4))
                    pe.matmul(g.ps[:, Q_BANK, :], w[:, (st.c - 1) * P:st.c * P], xT[:], start=True, stop=True
                              ).then_inc(q_ready, 1)

                def project_k(st):
                    wait(pe, k_lo_done, st.n(0) - 1)
                    pe.matmul(g.ps[:, K_BANK, :], w[:, W + (st.c - 1) * P:W + st.c * P], xT[:], start=True, stop=True
                              ).then_inc(k_ready, 1)

                def project_v(st):
                    group = (st.c - 4) % U
                    if group == 0:
                        pe.wait_ge(xT_v_done, st.i + 1)
                    if st.has(0):
                        pe.wait_ge(q_lo_done, st.n(0))
                    wait(pe, v_done, st.n(4))
                    for tb in range(TB):
                        ins = pe.matmul(g.ps[:, Q_BANK, tb * P:(tb + 1) * P], xT_v[:, tb * P:(tb + 1) * P],
                                        w[:, 2 * W + group * P:2 * W + (group + 1) * P], start=True, stop=True)
                    ins.then_inc(v_ready, 1)

                def scores(n, r, j, qb):
                    wait(pe, max_done, 16 * (n - 1) + 4 * j + qb - 1)
                    pe.matmul(g.ps[:, S_BANK + qb % 2, :], q4[r][0:KROWS, j, qb * P:(qb + 1) * P],
                              k4[r][0:KROWS, j, :], start=True, stop=True).then_inc(s_ready, 1)

                def turn_tops(n, t):
                    pe.wait_ge(max_done, 16 * n)
                    wait(pe, o_done, n - 3)
                    for qb in range(TB):
                        ins = pe.transpose(g.ps[0:HG, TURN_BANK, qb * P:(qb + 1) * P], top[:, t, qb, :], g.ident[:])
                    ins.then_inc(tt_ready, 1)

                def shifted_scores(n, r, j, kb):
                    wait(pe, exp_done, 16 * (n - 1) + 4 * j + kb - 1)
                    pe.matmul(g.ps[:, ST_BANK + kb % 2, :], k4[r][0:KROWS + 2, j, kb * P:(kb + 1) * P],
                              q4[r][0:KROWS + 2, j, :], start=True, stop=True).then_inc(st_ready, 1)

                def product(n, r, kb):
                    if kb == 0:
                        pe.wait_ge(exp_done, 16 * n)
                        pe.wait_ge(v_done, n)
                        wait(pe, recip_done, n - 1)
                    for j in range(HG):
                        pe.matmul(g.ps[32 * j:32 * j + 32, PV_BANK, :], v4[r][:, kb, 32 * j:32 * j + 32],
                                  e[r][:, j, kb, :], start=(kb == 0), stop=(kb == TB - 1))

                def sums(st):
                    pe.wait_ge(pair_done, HG * st.n(4))
                    if st.has(2):
                        pe.wait_ge(lo_done, st.n(2))
                    wait(pe, o_done, st.n(5))
                    for pair in range(2):
                        for j in range(HG):
                            ins = pe.matmul(g.ps[32 * j:32 * j + 32, TURN_BANK, :], ones[:], e_pair[:, j, pair, :],
                                            start=(pair == 0), stop=(pair == 1))
                    ins.then_inc(pv_done, 1)

                def turn(n):
                    pe.wait_ge(o_copied, n)
                    for tb in range(TB):
                        ins = pe.matmul(g.ps[:, PV_BANK, tb * HG:(tb + 1) * HG], l_sb[:, tb * P:(tb + 1) * P],
                                        pick[:], start=True, stop=True)
                    ins.then_inc(l_ready, 1)
                    for tb in range(TB):
                        ins = pe.transpose(g.ps[:, TURN_BANK, tb * P:(tb + 1) * P], o_sb[:, tb * P:(tb + 1) * P],
                                           g.ident[:])
                    ins.then_inc(oT_ready, 1)

                def step(st):
                    if st.has(1):
                        pe.wait_ge(loaded[st.slot(1, RQ)], 16 * 6 * st.use(1, RQ))
                    if st.has(3):
                        pe.wait_ge(row_loaded[st.slot(3, RQ)], 16 * 2 * st.use(3, RQ))
                    for j in range(HG):
                        for b in range(TB):
                            if st.has(1):
                                scores(st.n(1), st.slot(1, RQ), j, b)
                            if st.has(3):
                                shifted_scores(st.n(3), st.slot(3, RQ), j, b)
                            if (j, b) == (0, 1) and st.has(0) and st.c == 1:
                                turn_x(st)
                            if (j, b) == (0, 2) and st.has(5):
                                turn(st.n(5))
                            if (j, b) == (1, 0) and st.has(0):
                                project_q(st)
                            if (j, b) == (1, 1) and st.has(2):
                                turn_tops(st.n(2), st.slot(2, 2))
                            if (j, b) == (1, 3) and st.has(0):
                                project_k(st)
                            if (j, b) == (2, 3) and st.has(3):
                                project_v(st)
                            if j + b == 3 and st.has(4):
                                product(st.n(4), st.slot(4, 2), j)
                            if (j, b) == (3, 3) and st.has(4):
                                sums(st)

                run_steps(pe, NG, 5, step, U=U)

            @block.scalar
            def _(act):
                def copy_out(n):
                    act.wait_ge(pv_done, n)
                    wait(act, oT_ready, n - 1)
                    act.activation(l_sb[:], g.ps[:, TURN_BANK, :], ACT.Copy)
                    act.activation(o_sb[:], g.ps[:, PV_BANK, :], ACT.Copy).then_inc(o_copied, 1)

                def copy_x(st):
                    act.wait_ge(xp_ready, st.i + 1)
                    wait(act, k_ready, st.n(0) - 1)
                    wait(act, xT_v_done, st.i)
                    act.activation(xT[:], g.ps[:, K_BANK, :], ACT.Copy).then_inc(xT_done, 1)

                def copy_x_for_v(st):
                    act.wait_ge(xT_done, st.i + 1)
                    wait(act, v_ready, st.n(4))
                    act.activation(xT_v[:], xT[:], ACT.Copy).then_inc(xT_v_done, 1)

                def high(st, bank, ready, hi, factor, done):
                    act.wait_ge(ready, st.n(0))
                    if st.has(1):
                        act.wait_ge(loaded[st.slot(1, RQ)], 16 * 6 * st.use(1, RQ))
                    act.activation(hi[:], g.ps[:, bank, :], ACT.Copy, scale=factor).then_inc(done, 1)

                def copy_v(st):
                    n, r = st.n(3), st.slot(3, 2)
                    act.wait_ge(v_ready, n)
                    wait(act, pv_done, n - 2)
                    act.activation(v4[r][:], g.ps[:, Q_BANK, :].rearrange("p (t c) -> p t c", t=TB), ACT.Copy
                                   ).then_inc(v_done, 1)

                def top_row(st):
                    act.wait_ge(tt_ready, st.n(2))
                    if st.has(3):
                        act.wait_ge(row_loaded[st.slot(3, RQ)], 16 * 2 * st.use(3, RQ))
                    act.activation(top_hi[:], g.ps[0:HG, TURN_BANK, :], ACT.Copy, scale=-1.0).then_inc(hi_done, 1)

                def step(st):
                    for j in range(HG):
                        for b in range(TB):
                            if st.has(3):
                                n, r = st.n(3), st.slot(3, 2)
                                act.wait_ge(st_ready, 16 * (n - 1) + 4 * j + b + 1)
                                if j == 0 and b == 0:
                                    wait(act, pv_done, n - 2)
                                act.activation(e[r][:, j, b, :], g.ps[:, ST_BANK + b % 2, :], ACT.Exp
                                               ).then_inc(exp_done, 1)
                            if (j, b) == (0, 0) and st.has(5):
                                copy_out(st.n(5))
                            if (j, b) == (0, 2) and st.has(0) and st.c == 1:
                                copy_x(st)
                            if (j, b) == (0, 2) and st.has(3) and st.c == 4:
                                copy_x_for_v(st)
                            if (j, b) == (1, 1) and st.has(0):
                                high(st, Q_BANK, q_ready, q_hi, scale, q_hi_done)
                            if (j, b) == (1, 2) and st.has(2):
                                top_row(st)
                            if (j, b) == (2, 0) and st.has(0):
                                high(st, K_BANK, k_ready, k_hi, 1.0, k_hi_done)
                            if (j, b) == (3, 0) and st.has(3):
                                copy_v(st)

                run_steps(act, NG, 5, step, U=U)

            @block.vector
            def _(dve):
                def recip(n):
                    dve.wait_ge(l_ready, n)
                    wait(dve, o_done, n - 1)
                    dve.reciprocal(r16[:], g.ps[:, PV_BANK, 0:TB * HG].rearrange("p (t j) -> p t j", t=TB)
                                   ).then_inc(recip_done, 1)

                def divide(st):
                    n, r = st.n(5), st.slot(5, 2)
                    dve.wait_ge(recip_done, n)
                    dve.wait_ge(oT_ready, n)
                    wait(dve, stored[r], 16 * (st.use(5, 2) - 1))
                    dve.tensor_tensor(o_tok[r][:], g.ps[:, TURN_BANK, :].rearrange("p (t j d) -> p t j d", t=TB, j=HG),
                                      r16[:, :, :, None].to_broadcast([P, TB, HG, 32]), ALU.mult).then_inc(o_done, 1)

                def low(st, bank, hi_done, hi, lo, factor, done):
                    dve.wait_ge(hi_done, st.n(0))
                    if st.has(1):
                        dve.wait_ge(loaded[st.slot(1, RQ)], 16 * 6 * st.use(1, RQ))
                    dve.scalar_tensor_tensor(lo[:], g.ps[:, bank, :], factor, hi[:].bitcast(F32), ALU.mult,
                                             ALU.subtract).then_inc(done, 1)

                def low_top(st):
                    dve.wait_ge(hi_done, st.n(2))
                    if st.has(3):
                        dve.wait_ge(row_loaded[st.slot(3, RQ)], 16 * 2 * st.use(3, RQ))
                    dve.scalar_tensor_tensor(top_lo[:], g.ps[0:HG, TURN_BANK, :], -1.0, top_hi[:].bitcast(F32),
                                             ALU.mult, ALU.subtract).then_inc(lo_done, 1)

                dve.memset(ones[:], 1.0).then_inc(set_up, 1)

                def step(st):
                    if st.has(0) and st.c == 1:
                        wait(dve, xp_ready, st.i)
                        normalise(dve, g.x_all, g.mean_var, g.rstd, st.i + 1, xn, xn_done)
                    for j in range(HG):
                        for qb in range(TB):
                            if st.has(1):
                                n, t = st.n(1), st.slot(1, 2)
                                if j == 0 and qb == 0:
                                    wait(dve, tt_ready, n - 2)
                                dve.wait_ge(s_ready, 16 * (n - 1) + 4 * j + qb + 1)
                                dve.tensor_reduce(top[:, t, qb, j:j + 1], g.ps[:, S_BANK + qb % 2, :], AX_X, ALU.max
                                                  ).then_inc(max_done, 1)
                            if (j, qb) == (0, 2) and st.has(5):
                                recip(st.n(5))
                            if (j, qb) == (0, 3) and st.has(5):
                                divide(st)
                            if (j, qb) == (1, 2) and st.has(0):
                                low(st, Q_BANK, q_hi_done, q_hi, q_lo, scale, q_lo_done)
                            if (j, qb) == (1, 3) and st.has(2):
                                low_top(st)
                            if (j, qb) == (2, 1) and st.has(0):
                                low(st, K_BANK, k_hi_done, k_hi, k_lo, 1.0, k_lo_done)

                run_steps(dve, NG, 5, step, U=U)


def bias_strips(nc, g, name, coeffs_t, line_table, wpos_t, flip):
    LINE = 1024
    with Phase(nc, name) as ph:
        taps = ph.sb("taps", [101, 4])
        table = ph.sb("table", [101, LINE])
        wp = ph.sb("wp", [4, 16])
        fl = ph.sb("fl", [P, P])
        resp = ph.sb("resp", [4, LINE])
        lines = ph.sb("lines", [16, LINE])
        hank = ph.sb("hank", [P, 2, STRIP])
        strip = ph.sb("strip", [P, 2, STRIP])
        loaded, mm, copied, line_stored = (ph.sem(k) for k in ("loaded", "mm", "copied", "line_stored"))
        h_loaded = [ph.sem(f"h_loaded{r}") for r in range(2)]
        s_stored = [ph.sem(f"s_stored{r}") for r in range(2)]
        flipped, s_copied = ph.sem("flipped"), ph.sem("s_copied")
        HALF = STRIP // 2
        with nc.Block() as block:
            @block.sync
            def _(sp):
                for dst, src in ((taps, coeffs_t), (table, line_table), (wp, wpos_t), (fl, flip)):
                    sp.dma_start(dst[:], src).then_inc(loaded, 16)
                sp.wait_ge(copied, 4)
                sp.dma_start(g.lines, lines[:]).then_inc(line_stored, 16)
                sp.wait_ge(line_stored, 16)
                for h in range(16):
                    r = h % 2
                    wait(sp, flipped, h - 1)
                    src = bass.AP(g.lines.tensor, h * LINE, [[1, P], [1, STRIP]])
                    sp.dma_start(hank[:, r, :], src).then_inc(h_loaded[r], 16)
                    if h:
                        sp.wait_ge(s_copied, h)
                        sp.dma_start(g.strips[h - 1], strip[:, (h - 1) % 2, :]).then_inc(s_stored[(h - 1) % 2], 16)
                sp.wait_ge(s_copied, 16)
                sp.dma_start(g.strips[15], strip[:, 1, :]).then_inc(s_stored[1], 16)
                for r in range(2):
                    sp.wait_ge(s_stored[r], 16 * 8)

            @block.tensor
            def _(pe):
                pe.wait_ge(loaded, 64)
                for k in range(2):
                    pe.matmul(g.ps[0:4, k, :], taps[:], table[:, k * 512:(k + 1) * 512], start=True, stop=True
                              ).then_inc(mm, 1)
                for k in range(2):
                    pe.wait_ge(copied, k + 1)
                    pe.matmul(g.ps[0:16, 2 + k, :], wp[:], resp[:, k * 512:(k + 1) * 512], start=True, stop=True
                              ).then_inc(mm, 1)
                for h in range(16):
                    r = h % 2
                    pe.wait_ge(h_loaded[r], 16 * (h // 2 + 1))
                    wait(pe, s_copied, h - 1)
                    for k in range(2):
                        ins = pe.matmul(g.ps[:, 4 + 2 * r + k, 0:HALF], fl[:], hank[:, r, k * HALF:(k + 1) * HALF],
                                        start=True, stop=True)
                    ins.then_inc(flipped, 1)

            @block.vector
            def _(dve):
                for k in range(2):
                    dve.wait_ge(mm, k + 1)
                    dve.tensor_copy(resp[:, k * 512:(k + 1) * 512], g.ps[0:4, k, :]).then_inc(copied, 1)
                for k in range(2):
                    dve.wait_ge(mm, 2 + k + 1)
                    dve.tensor_copy(lines[:, k * 512:(k + 1) * 512], g.ps[0:16, 2 + k, :]).then_inc(copied, 1)
                for h in range(16):
                    r = h % 2
                    dve.wait_ge(flipped, h + 1)
                    wait(dve, s_stored[r], 16 * (h // 2))
                    dve.tensor_copy(strip[:, r, :].rearrange("p (k n) -> p k n", k=2),
                                    g.ps[:, 4 + 2 * r:6 + 2 * r, 0:HALF]).then_inc(s_copied, 1)


class Marks:

    def __init__(self, ph, name, steps):
        self.sem, self.steps = ph.sem(name), steps.split()

    def at(self, n, step):
        return len(self.steps) * (n - 1) + self.steps.index(step) + 1


def linear_attention(nc, g, name, d):
    NP = 12
    Q, QS, K, KS, B0, B1, ZA, ZB, V0 = range(9)
    HM = 64
    with Phase(nc, name) as ph:
        w = ph.sb("w", [P, NP, P])
        w_out = ph.sb("w_out", [P, DM])
        bout = ph.sb("bout", [P, DM])
        bias = ph.sb("bias", [P, 4])
        rope = ph.sb("rope", [P, 2, S])
        to_c = ph.sb("to_c", [P, 4, P])
        to_m = ph.sb("to_m", [P, 2, HM])
        from_m = ph.sb("from_m", [P, 2, P])
        xn, xn2, xnb = (ph.sb(k, [P, TB, DM]) for k in ("xn", "xn2", "xnb"))
        xT = [ph.sb(f"xT{r}", [P, S]) for r in range(2)]
        u = ph.sb("u", [P, 2, 2, S])
        rot = ph.sb("rot", [P, 2, S])
        low = ph.sb("low", [P, 2, S])
        phi = ph.sb("phi", [P, 2, S])
        beta = ph.sb("beta", [P, 2, S])
        kv = ph.sb("kv", [P, 4, S])
        z = ph.sb("z", [HM, 2, S])
        zmax = ph.sb("zmax", [HM, S])
        zexp = [ph.sb(f"zexp{r}", [HM, 2, S]) for r in range(2)]
        zsum = [ph.sb(f"zsum{r}", [HM, S]) for r in range(2)]
        state = ph.sb("state", [P, 10, S])
        prod = ph.sb("prod", [P, 10, S])
        den = ph.sb("den", [HM, S])
        coef = ph.sb("coef", [P, S])
        cb = ph.sb("cb", [P, 2, S])
        y2 = ph.sb("y2", [P, 2, S])
        yT = ph.sb("yT", [P, S])
        loaded, zeroed = ph.sem("loaded"), ph.sem("zeroed")
        xn_done, xp_ready, xT_done = ph.sem("xn_done"), ph.sem("xp_ready"), ph.sem("xT_done")
        proj_ready = ph.sem("proj_ready")
        va = Marks(ph, "vec_rotate_scan", "cq sq ck sk rq rk lq lk tq tk phi_q phi_k kv0 kv1 kv2 kv3 beta0 beta1 zmax "
                                          "s0 s1 s2 s3 s4 s5 s6 s7 s8 s9")
        vb = Marks(ph, "vec_finish", "den recip coef y0 y1 y z")
        xn2_done = ph.sem("xn2_done")
        aa = Marks(ph, "act_features", "eq ek beta0 beta1 za zb zexp")
        ab = Marks(ph, "act_coef", "cb0 cb1")
        pa = Marks(ph, "pool_products", "zsub p0 p1 zsum p2 p3 p4 p5 p6 p7 p8 p9")
        pool_xnb = ph.sem("pool_xnb")
        ta = Marks(ph, "pe_sums", "m0 m1 m2 m3 m4 m5 m6 m7 m8 m9")
        tb_ = Marks(ph, "pe_finish", "cb0 cb1 out")
        T_BANK, R_BANK, NUM_BANK, DEN_BANK = 0, 1, 5, 7
        scans = [(0, None), (1, None)] + [(m, c) for m in range(2) for c in range(4)]

        with nc.Block() as block:
            @block.sync
            def _(sp):
                for dst, src in ((w[:], d["w"]), (w_out[:], d["w_out"]), (bias[:], d["bias"]),
                                 (rope[:], d["rope"]), (to_c[:], d["to_c"]), (to_m[:], d["to_m"]),
                                 (from_m[:], d["from_m"]), (bout[:], d["bout"][None, :].to_broadcast([P, DM]))):
                    sp.dma_start(dst, src).then_inc(loaded, 16)

            @block.tensor
            def _(pe):
                pe.wait_ge(loaded, 16 * 8)
                pe.wait_ge(zeroed, 1)

                def project(st, pieces):
                    n, r = st.n(1), st.slot(1, 2)
                    for m in pieces:
                        if m < 4:
                            wait(pe, va.sem, va.at(n - 1, f"kv{m}"))
                        elif m < 8:
                            pe.wait_ge(va.sem, va.at(n, ("cq", "sq", "ck", "sk")[m - 4]))
                        else:
                            pe.wait_ge(aa.sem, aa.at(n, ("beta0", "beta1", "za", "zb")[m - 8]))
                        rows = HM if m in (ZA, ZB) else P
                        pe.matmul(g.ps[0:rows, R_BANK + m % 4, :], w[:, m, 0:rows], xT[r][:], start=True, stop=True
                                  ).then_inc(proj_ready, 1)

                def step(st):
                    if st.has(1):
                        pe.wait_ge(xT_done, st.n(1))
                        project(st, range(Q, KS + 1))
                    if st.has(0):
                        n = st.n(0)
                        pe.wait_ge(xn_done, TB * n)
                        if st.has(3):
                            wait(pe, vb.sem, vb.at(st.n(3), "z"))
                        for tb in range(TB):
                            ins = pe.transpose(g.ps[:, T_BANK, tb * P:(tb + 1) * P], xn[:, tb, :], g.ident[:])
                        ins.then_inc(xp_ready, 1)
                    if st.has(2):
                        pe.wait_ge(vb.sem, vb.at(st.n(2), "coef"))
                        pe.matmul(g.ps[:, DEN_BANK, :], from_m[:, 0, :], coef[:], start=True, stop=True
                                  ).then_inc(tb_.sem, 1)
                    if st.has(1):
                        project(st, (B0, B1))
                    if st.has(2):
                        pe.wait_ge(ab.sem, ab.at(st.n(2), "cb0"))
                        pe.matmul(g.ps[:, DEN_BANK, :], from_m[:, 1, :], coef[:], start=True, stop=True
                                  ).then_inc(tb_.sem, 1)
                    if st.has(1):
                        project(st, range(ZA, NP))
                    if st.has(2):
                        n = st.n(2)
                        pe.wait_ge(vb.sem, vb.at(n, "y"))
                        pe.wait_ge(xT_done, st.n(0) if st.has(0) else B)
                        wait(pe, vb.sem, vb.at(n - 1, "z"))
                        for tb in range(TB):
                            ins = pe.matmul(g.ps[:, T_BANK, tb * P:(tb + 1) * P], yT[:, tb * P:(tb + 1) * P], w_out[:],
                                            start=True, stop=True)
                        ins.then_inc(tb_.sem, 1)
                    if st.has(1):
                        n = st.n(1)
                        for i, (m, c) in enumerate(scans):
                            pe.wait_ge(pa.sem, pa.at(n, f"p{i}"))
                            if i == 0 and st.has(2):
                                pe.wait_ge(ab.sem, ab.at(st.n(2), "cb1"))
                            if i == 2 and st.has(2):
                                pe.wait_ge(vb.sem, vb.at(st.n(2), "y1"))
                            if c is None:
                                pe.matmul(g.ps[0:HM, DEN_BANK, :], to_m[:, m, :], prod[:, i, :], start=(m == 0),
                                          stop=(m == 1)).then_inc(ta.sem, 1)
                            else:
                                pe.matmul(g.ps[:, NUM_BANK + m, :], to_c[:, c, :], prod[:, i, :], start=(c == 0),
                                          stop=(c == 3)).then_inc(ta.sem, 1)

                run_steps(pe, B, 3, step, U=2)

            @block.scalar
            def _(act):
                act.wait_ge(loaded, 16 * 8)

                def bank(m):
                    return g.ps[0:HM if m in (ZA, ZB) else P, R_BANK + m % 4, :]

                def step(st):
                    if st.has(1):
                        n = st.n(1)
                        for k in range(2):
                            act.wait_ge(va.sem, va.at(n, ("lq", "lk")[k]))
                            act.activation(low[:, k, :], low[:, k, :], ACT.Exp).then_inc(aa.sem, 1)
                    if st.has(0):
                        n = st.n(0)
                        act.wait_ge(xp_ready, n)
                        wait(act, proj_ready, NP * (n - 2))
                        act.activation(xT[st.slot(0, 2)][:], g.ps[:, T_BANK, :], ACT.Copy).then_inc(xT_done, 1)
                    if st.has(2):
                        act.wait_ge(tb_.sem, tb_.at(st.n(2), "cb0"))
                        wait(act, vb.sem, vb.at(st.n(2) - 1, "y0"))
                        act.activation(cb[:, 0, :], g.ps[:, DEN_BANK, :], ACT.Copy).then_inc(ab.sem, 1)
                    if st.has(1):
                        n = st.n(1)
                        wait(act, va.sem, va.at(n - 1, "s9"))
                        for k in range(2):
                            act.wait_ge(proj_ready, NP * (n - 1) + B0 + k + 1)
                            act.activation(beta[:, k, :], bank(B0 + k), ACT.Sigmoid, bias=bias[:, k:k + 1]
                                           ).then_inc(aa.sem, 1)
                    if st.has(2):
                        act.wait_ge(tb_.sem, tb_.at(st.n(2), "cb1"))
                        wait(act, vb.sem, vb.at(st.n(2) - 1, "y1"))
                        act.activation(cb[:, 1, :], g.ps[:, DEN_BANK, :], ACT.Copy).then_inc(ab.sem, 1)
                    if st.has(1):
                        n = st.n(1)
                        for k in range(2):
                            act.wait_ge(proj_ready, NP * (n - 1) + ZA + k + 1)
                            if k == 0:
                                wait(act, aa.sem, aa.at(n - 1, "zexp"))
                            act.activation(z[:, k, :], bank(ZA + k), ACT.Identity, bias=bias[0:HM, 2 + k:3 + k]
                                           ).then_inc(aa.sem, 1)
                        act.wait_ge(pa.sem, pa.at(n, "zsub"))
                        if st.has(3):
                            act.wait_ge(vb.sem, vb.at(st.n(3), "coef"))
                        act.activation(zexp[st.slot(1, 2)][:], z[:], ACT.Exp).then_inc(aa.sem, 1)

                run_steps(act, B, 3, step, U=2)

            @block.gpsimd
            def _(pool):
                pool.wait_ge(loaded, 16 * 8)

                def step(st):
                    if st.has(1):
                        n, r = st.n(1), st.slot(1, 2)
                        pool.wait_ge(va.sem, va.at(n, "zmax"))
                        pool.tensor_tensor(z[:], z[:], zmax[:, None, :].to_broadcast([HM, 2, S]), ALU.subtract
                                           ).then_inc(pa.sem, 1)
                        for i in range(10):
                            if i == 2:
                                pool.wait_ge(aa.sem, aa.at(n, "zexp"))
                                if st.has(3):
                                    pool.wait_ge(vb.sem, vb.at(st.n(3), "den"))
                                pool.tensor_tensor(zsum[r][:], zexp[r][:, 0, :], zexp[r][:, 1, :], ALU.add
                                                   ).then_inc(pa.sem, 1)
                            pool.wait_ge(va.sem, va.at(n, f"s{i}"))
                            wait(pool, ta.sem, ta.at(n - 1, f"m{i}"))
                            pool.tensor_tensor(prod[:, i, :], state[:, i, :], phi[:, 0, :], ALU.mult
                                               ).then_inc(pa.sem, 1)
                    if st.has(2):
                        n = st.n(2)
                        pool.wait_ge(xn2_done, TB * n)
                        wait(pool, vb.sem, vb.at(n - 1, "z"))
                        pool.tensor_tensor(xnb[:], xn2[:], bout[:, None, :].to_broadcast([P, TB, DM]), ALU.add
                                           ).then_inc(pool_xnb, 1)

                run_steps(pool, B, 3, step, U=2)

            @block.vector
            def _(dve):
                dve.memset(coef[:], 0.0).then_inc(zeroed, 1)
                dve.wait_ge(loaded, 16 * 8)
                dve.wait_ge(zeroed, 1)

                def bank(m):
                    return g.ps[:, R_BANK + m % 4, :]

                def done(ins, marks):
                    ins.then_inc(marks.sem, 1)

                def step(st):
                    if st.has(0):
                        wait(dve, xp_ready, st.n(0) - 1)
                        normalise(dve, g.x_all, g.mean_var, g.rstd, st.n(0), xn, xn_done)
                    if st.has(1):
                        n = st.n(1)
                        wait(dve, va.sem, va.at(n - 1, "s9"))
                        for k in range(2):
                            for t in range(2):
                                dve.wait_ge(proj_ready, NP * (n - 1) + 2 * k + t + 1)
                                dve.tensor_tensor(u[:, k, t, :], bank(2 * k + t), rope[:, t, :], ALU.mult
                                                  ).then_inc(va.sem, 1)
                        for k in range(2):
                            dve.wait_ge(va.sem, va.at(n, ("sq", "sk")[k]))
                            dve.tensor_tensor(rot[:, k, :], u[:, k, 0, :], u[:, k, 1, :], ALU.add).then_inc(va.sem, 1)
                        for k in range(2):
                            dve.wait_ge(va.sem, va.at(n, ("rq", "rk")[k]))
                            dve.tensor_scalar(low[:, k, :], rot[:, k, :], 0.0, None, ALU.min).then_inc(va.sem, 1)
                    if st.has(2):
                        n, r = st.n(2), st.slot(2, 2)
                        dve.wait_ge(ta.sem, ta.at(n, "m1"))
                        dve.wait_ge(pa.sem, pa.at(n, "zsum"))
                        wait(dve, tb_.sem, tb_.at(n - 1, "cb1"))
                        dve.scalar_tensor_tensor(den[:], g.ps[0:HM, DEN_BANK, :], 1e-6, zsum[r][:], ALU.add, ALU.mult
                                                 ).then_inc(vb.sem, 1)
                        dve.wait_ge(vb.sem, vb.at(n, "den"))
                        dve.reciprocal(den[:], den[:]).then_inc(vb.sem, 1)
                        dve.wait_ge(vb.sem, vb.at(n, "recip"))
                        dve.tensor_tensor(coef[0:HM, :], den[:], zexp[r][:, 0, :], ALU.mult).then_inc(vb.sem, 1)
                    if st.has(1):
                        n = st.n(1)
                        for k in range(2):
                            dve.wait_ge(aa.sem, aa.at(n, ("eq", "ek")[k]))
                            dve.tensor_scalar(low[:, k, :], low[:, k, :], -1.0, 1.0, ALU.add, ALU.add
                                              ).then_inc(va.sem, 1)
                        wait(dve, pa.sem, pa.at(n - 1, "p9"))
                        for k in range(2):
                            dve.wait_ge(va.sem, va.at(n, ("tq", "tk")[k]))
                            dve.scalar_tensor_tensor(phi[:, k, :], rot[:, k, :], 0.0, low[:, k, :], ALU.max, ALU.add
                                                     ).then_inc(va.sem, 1)
                        dve.wait_ge(va.sem, va.at(n, "phi_k"))
                        for c in range(4):
                            dve.wait_ge(proj_ready, NP * (n - 1) + V0 + c + 1)
                            dve.tensor_tensor(kv[:, c, :], bank(V0 + c), phi[:, 1, :], ALU.mult).then_inc(va.sem, 1)
                        for m in range(2):
                            dve.wait_ge(aa.sem, aa.at(n, ("beta0", "beta1")[m]))
                            dve.tensor_scalar(beta[:, m, :], beta[:, m, :], 0.85, 0.9995, ALU.max, ALU.min
                                              ).then_inc(va.sem, 1)
                        dve.wait_ge(aa.sem, aa.at(n, "zb"))
                        wait(dve, pa.sem, pa.at(n - 1, "zsub"))
                        dve.tensor_tensor(zmax[:], z[:, 0, :], z[:, 1, :], ALU.max).then_inc(va.sem, 1)
                    if st.has(2):
                        n = st.n(2)
                        dve.wait_ge(ta.sem, ta.at(n, "m9"))
                        wait(dve, tb_.sem, tb_.at(n - 1, "out"))
                        for m in range(2):
                            dve.wait_ge(ab.sem, ab.at(n, ("cb0", "cb1")[m]))
                            dve.tensor_tensor(y2[:, m, :], g.ps[:, NUM_BANK + m, :], cb[:, m, :], ALU.mult
                                              ).then_inc(vb.sem, 1)
                        dve.wait_ge(vb.sem, vb.at(n, "y1"))
                        dve.tensor_tensor(yT[:], y2[:, 0, :], y2[:, 1, :], ALU.add).then_inc(vb.sem, 1)
                        wait(dve, pool_xnb, n - 1)
                        normalise(dve, g.x_all, g.mean_var, g.rstd, n, xn2, xn2_done)
                    if st.has(1):
                        n = st.n(1)
                        dve.wait_ge(va.sem, va.at(n, "beta1"))
                        for i, (m, c) in enumerate(scans):
                            dve.tensor_tensor_scan(state[:, i, :], beta[:, m, :],
                                                   phi[:, 1, :] if c is None else kv[:, c, :], 0.0, ALU.mult, ALU.add
                                                   ).then_inc(va.sem, 1)
                    if st.has(2):
                        n = st.n(2)
                        dve.wait_ge(tb_.sem, tb_.at(n, "out"))
                        dve.wait_ge(pool_xnb, n)
                        dve.tensor_tensor(batch_of(g.y_all, n), g.ps[:, T_BANK, :].rearrange("p (t d) -> p t d", t=TB),
                                          xnb[:], ALU.add).then_inc(vb.sem, 1)

                run_steps(dve, B, 3, step, U=2)


def project_out(nc, g, name, wide):
    G = 8 if wide else 1
    src = g.o32 if wide else g.o8
    with Phase(nc, name) as ph:
        w = ph.sb("w", [P, G, DM])
        bias = ph.sb("bias", [P, 3, DM])
        o = [ph.sb(f"o{r}", [P, TB, G * P]) for r in range(2)]
        oT = ph.sb("oT", [P, 2, S])
        yT = ph.sb("yT", [P, S])
        w_loaded = ph.sem("w_loaded")
        loaded = [ph.sem(f"loaded{r}") for r in range(2)]
        t_ready, t_read, mm_done, y_copied, yt_ready, added = (
            ph.sem(k) for k in ("t_ready", "t_read", "mm_done", "y_copied", "yt_ready", "added"))
        T_BANK, Y_BANK, YT_BANK = 0, 2, 4
        pieces = 8 if wide else 4
        width = G * P // pieces
        dest = g.y_all if wide else g.x_all

        with nc.Block() as block:
            @block.sync
            def _(sp):
                for k, part in enumerate(g.w_out32 if wide else (g.w_out8[name],)):
                    sp.dma_start(w[:, k, :], part).then_inc(w_loaded, 16)
                if wide:
                    sp.dma_start(bias[:, 0, :], g.b_out[None, :].to_broadcast([P, DM])).then_inc(w_loaded, 16)

                def step(st):
                    n, r = st.n(0), st.slot(0, 2)
                    wait(sp, t_ready, G * (n - 2))
                    for k in range(pieces):
                        sp.dma_start(o[r][:, :, k * width:(k + 1) * width],
                                     src[bass.ds((n - 1) * pieces + k, 1)].rearrange("a t p c -> p (a t) c")
                                     ).then_inc(loaded[r], 16)

                run_steps(sp, B, 0, step, U=2)

            @block.tensor
            def _(pe):
                pe.wait_ge(w_loaded, 16 * (G + wide))

                def step(st):
                    n, r = st.n(0), st.slot(0, 2)
                    pe.wait_ge(loaded[r], 16 * pieces * st.use(0, 2))

                    def turn(k):
                        m = G * (n - 1) + k + 1
                        wait(pe, t_read, m - 2)
                        slot = k % 2 if wide else r
                        for tb in range(TB):
                            ins = pe.transpose(g.ps[:, T_BANK + slot, tb * P:(tb + 1) * P],
                                               o[r][:, tb, k * P:(k + 1) * P], g.ident[:])
                        ins.then_inc(t_ready, 1)

                    turn(0)
                    wait(pe, y_copied, n - 2)
                    for k in range(G):
                        if k + 1 < G:
                            turn(k + 1)
                        pe.wait_ge(t_read, G * (n - 1) + k + 1)
                        slot = k % 2 if wide else r
                        pe.matmul(g.ps[:, Y_BANK + r, :], w[:, k, :], oT[:, slot, :],
                                  start=(k == 0), stop=(k == G - 1)).then_inc(mm_done, 1)
                    pe.wait_ge(y_copied, n)
                    wait(pe, added, n - 2)
                    for tb in range(TB):
                        ins = pe.transpose(g.ps[:, YT_BANK + r, tb * P:(tb + 1) * P], yT[:, tb * P:(tb + 1) * P],
                                           g.ident[:])
                    ins.then_inc(yt_ready, 1)

                run_steps(pe, B, 0, step, U=2)

            @block.scalar
            def _(act):
                def step(st):
                    n, r = st.n(0), st.slot(0, 2)
                    for k in range(G):
                        m = G * (n - 1) + k + 1
                        slot = k % 2 if wide else r
                        act.wait_ge(t_ready, m)
                        wait(act, mm_done, m - 2)
                        act.activation(oT[:, slot, :], g.ps[:, T_BANK + slot, :], ACT.Copy).then_inc(t_read, 1)
                    act.wait_ge(mm_done, G * n)
                    wait(act, yt_ready, n - 1)
                    act.activation(yT[:], g.ps[:, Y_BANK + r, :], ACT.Copy).then_inc(y_copied, 1)

                run_steps(act, B, 0, step, U=2)

            @block.vector
            def _(dve):
                if wide:
                    dve.wait_ge(w_loaded, 16 * (G + 1))

                def step(st):
                    n, r = st.n(0), st.slot(0, 2)
                    dve.wait_ge(yt_ready, n)
                    y = g.ps[:, YT_BANK + r, :].rearrange("p (t d) -> p t d", t=TB)
                    other = (bias[:, 0:1, :].to_broadcast([P, TB, DM]) if wide else batch_of(g.x_all, n))
                    dve.tensor_tensor(batch_of(dest, n), y, other, ALU.add).then_inc(added, 1)

                run_steps(dve, B, 0, step, U=2)


def add_normalised(nc, g, name, source, gamma, beta):
    with Phase(nc, name) as ph:
        gb = ph.sb("gb", [P, 2, DM])
        yn = ph.sb("yn", [P, TB, DM])
        loaded, done, chain = ph.sem("loaded"), ph.sem("done"), ph.sem("chain")
        with nc.Block() as block:
            @block.sync
            def _(sp):
                for k, src in enumerate((gamma, beta)):
                    sp.dma_start(gb[:, k, :], src[None, :].to_broadcast([P, DM])).then_inc(loaded, 16)

            @block.vector
            def _(dve):
                dve.wait_ge(loaded, 32)
                with dve.Fori(1, B + 1) as n:
                    normalise(dve, source, g.mean_var, g.rstd, n, yn, done)
                    dve.wait_ge(done, TB * n)
                    link = Link(dve, chain, n, 3)
                    link(dve.tensor_tensor(yn[:], yn[:], gb[:, 0:1, :].to_broadcast([P, TB, DM]), ALU.mult))
                    link(dve.tensor_tensor(yn[:], yn[:], gb[:, 1:2, :].to_broadcast([P, TB, DM]), ALU.add))
                    link(dve.tensor_tensor(batch_of(g.x_all, n), batch_of(g.x_all, n), yn[:], ALU.add))


def swiglu(nc, g, name, packed, E, C, router=None):
    EC = E * C
    W = 3 * C * P
    quant = packed.dtype == I32
    routed = E - 1
    OUT_LAG, OUT_AT = (2, 5) if E > 1 else (3, 0)
    DOWN_LAG = 3 if routed else 2
    X_AT = EC // 3
    with Phase(nc, name) as ph:
        stage = ph.sb("stage", [P, 2, W], I32 if quant else F32)
        stage_f = ph.sb("stage_f", [P, 2, W]) if quant else stage
        w_hi = ph.sb("w_hi", [P, E, W], F32R)
        w_lo = ph.sb("w_lo", [P, E, W], F32R)
        xn = ph.sb("xn", [P, TB, DM])
        xT = ph.sb("xT", [P, S])
        x_hi = [ph.sb(f"x_hi{r}", [P, S], F32R) for r in range(2)]
        x_lo = [ph.sb(f"x_lo{r}", [P, S], F32R) for r in range(2)]
        gate = ph.sb("gate", [P, 2, S])
        h = ph.sb("h", [P, C, S])
        h_hi = ph.sb("h_hi", [P, C, S], F32R)
        h_lo = ph.sb("h_lo", [P, C, S], F32R)
        acc = ph.sb("acc", [P, S])
        stage_loaded = [ph.sem(f"stage_loaded{k}") for k in range(2)]
        dequant_done, w_hi_done, w_done = ph.sem("dequant_done"), ph.sem("w_hi_done"), ph.sem("w_done")
        xn_done, xp_ready, xT_done, x_hi_done, x_lo_done = (
            ph.sem(k) for k in ("xn_done", "xp_ready", "xT_done", "x_hi_done", "x_lo_done"))
        gu_ready, gate_done, h_done, h_hi_done, h_lo_done, down_done, d_ready, d_read, acc_done = (
            ph.sem(k) for k in ("gu_ready", "gate_done", "h_done", "h_hi_done", "h_lo_done", "down_done", "d_ready",
                                "d_read", "acc_done"))
        out_ready, out_added = ph.sem("out_ready"), ph.sem("out_added")
        if routed:
            rw = ph.sb("rw", [P, routed])
            lower = ph.sb("lower", [P, routed, routed])
            comb = [ph.sb(f"comb{r}", [P, TB, routed]) for r in range(2)]
            mx, sm = ph.sb("mx", [P, TB]), ph.sb("sm", [P, TB])
            pr, sel = ph.sb("pr", [P, TB, routed]), ph.sb("sel", [P, TB, routed])
            gt, eq = (ph.sb(k, [P, TB, routed, routed]) for k in ("gt", "eq"))
            cw = ph.sb("cw", [P, 2, S])
            part = ph.sb("part", [P, S])
            small_loaded, lg_ready, shifted, p_exp, comb_done, cw_ready, cw_done, chain = (
                ph.sem(k) for k in ("small_loaded", "lg_ready", "shifted", "p_exp", "comb_done", "cw_ready",
                                    "cw_done", "chain"))
            recip_done = ph.sem("recip_done")
        T_BANK, R_BANK, G_BANK, U_BANK, D_BANK = 0, 1, 2, 4, 6
        LG_AT, COMB_AT = X_AT + 3, X_AT + 4

        def position(st, k, q):
            return EC * (st.n(k) - 1) + q + 1, (EC * (st.c - k - 1) + q) % 2

        with nc.Block() as block:
            @block.sync
            def _(sp):
                if routed:
                    sp.dma_start(rw[:], router[0]).then_inc(small_loaded, 16)
                    sp.dma_start(lower[:], router[1][None, :, :].to_broadcast([P, routed, routed])
                                 ).then_inc(small_loaded, 16)
                for e in range(E):
                    wait(sp, w_done, e - 1)
                    sp.dma_start(stage[:, e % 2, :], packed[e]).then_inc(stage_loaded[e % 2], 16)

            @block.tensor
            def _(pe):
                def three(bank, w0, cols, hi, lo, start, stop):
                    pe.matmul(bank, w_hi[:, w0, cols], hi, start=start, stop=False)
                    pe.matmul(bank, w_lo[:, w0, cols], hi, start=False, stop=False)
                    return pe.matmul(bank, w_hi[:, w0, cols], lo, start=False, stop=stop)

                def gate_up(st, q):
                    e, c = divmod(q, C)
                    m, par = position(st, 1, q)
                    r = st.slot(1, 2)
                    wait(pe, gate_done, m - 2)
                    wait(pe, h_done, m - 2)
                    three(g.ps[:, G_BANK + par, :], e, slice(c * P, (c + 1) * P), x_hi[r][:], x_lo[r][:], True, True)
                    three(g.ps[:, U_BANK + par, :], e, slice((C + c) * P, (C + c + 1) * P), x_hi[r][:], x_lo[r][:],
                          True, True).then_inc(gu_ready, 1)

                def down(st, k, q):
                    e, c = divmod(q, C)
                    m, _ = position(st, k, q)
                    bank = g.ps[:, D_BANK + (E * (st.c - k - 1) + e) % 2, :]
                    pe.wait_ge(h_lo_done, m)
                    if c == 0:
                        wait(pe, d_read, E * (st.n(k) - 1) + e - 1)
                    ins = three(bank, e, slice((2 * C + c) * P, (2 * C + c + 1) * P), h_hi[:, c, :], h_lo[:, c, :],
                                c == 0, c == C - 1)
                    ins.then_inc(down_done, 1)
                    if c == C - 1:
                        pe.wait_ge(down_done, m)
                        pe.sem_inc(d_ready, 1)

                def step(st):
                    if st.has(1):
                        pe.wait_ge(x_lo_done, st.n(1))
                    if routed and st.has(1):
                        pe.wait_ge(comb_done, st.n(1))
                    for q in range(EC):
                        e, c = divmod(q, C)
                        if st.has(1):
                            if isinstance(st.i, int) and st.n(1) == 1 and c == 0:
                                pe.wait_ge(w_done, e + 1)
                            if routed and e and c == 0:
                                k = routed * (st.n(1) - 1) + e
                                wait(pe, cw_done, k - 1)
                                if st.has(0):
                                    wait(pe, shifted, st.n(0) - (0 if q > LG_AT else 1))
                                else:
                                    wait(pe, shifted, st.n(1))
                                for tb in range(TB):
                                    ins = pe.matmul(g.ps[:, R_BANK, tb * P:(tb + 1) * P],
                                                    comb[st.slot(1, 2)][:, tb, e - 1:e].to_broadcast([P, P]),
                                                    g.ident[:], start=True, stop=True)
                                ins.then_inc(cw_ready, 1)
                            gate_up(st, q)
                        if q >= DOWN_LAG and st.has(1):
                            down(st, 1, q - DOWN_LAG)
                        if q < DOWN_LAG and st.has(2):
                            down(st, 2, EC - DOWN_LAG + q)
                        if q == X_AT and st.has(0):
                            pe.wait_ge(xn_done, TB * st.n(0))
                            if st.has(OUT_LAG) or (st.has(OUT_LAG + 1) and OUT_AT >= X_AT):
                                wait(pe, out_added, st.n(OUT_LAG))
                            for tb in range(TB):
                                ins = pe.transpose(g.ps[:, T_BANK, tb * P:(tb + 1) * P], xn[:, tb, :], g.ident[:])
                            ins.then_inc(xp_ready, 1)
                        if routed and q == LG_AT and st.has(0):
                            if st.n(0) == 1 if isinstance(st.i, int) else False:
                                pe.wait_ge(small_loaded, 32)
                            pe.wait_ge(xT_done, st.n(0))
                            if st.has(1):
                                pe.wait_ge(cw_done, routed * (st.n(1) - 1) + q // C)
                            for tb in range(TB):
                                ins = pe.matmul(g.ps[:, R_BANK, tb * 8:tb * 8 + routed], xT[:, tb * P:(tb + 1) * P],
                                                rw[:], start=True, stop=True)
                            ins.then_inc(lg_ready, 1)
                        if q == OUT_AT and st.has(OUT_LAG):
                            if routed:
                                pe.wait_ge(acc_done, routed * st.n(OUT_LAG))
                            else:
                                pe.wait_ge(d_read, st.n(OUT_LAG))
                            if st.has(1):
                                pe.wait_ge(x_lo_done, st.n(1))
                            for tb in range(TB):
                                ins = pe.transpose(g.ps[:, T_BANK, tb * P:(tb + 1) * P], acc[:, tb * P:(tb + 1) * P],
                                                   g.ident[:])
                            ins.then_inc(out_ready, 1)

                run_steps(pe, B, OUT_LAG, step, U=2)

            @block.scalar
            def _(act):
                def step(st):
                    for q in range(EC):
                        e, c = divmod(q, C)
                        if isinstance(st.i, int) and st.c + 2 * st.i == 2 and c == 0:
                            if quant:
                                act.wait_ge(dequant_done, e + 1)
                            else:
                                act.wait_ge(stage_loaded[e % 2], 16 * (e // 2 + 1))
                            act.activation(w_hi[:, e, :], stage_f[:, e % 2, :], ACT.Copy).then_inc(w_hi_done, 1)
                        if st.has(1):
                            m, par = position(st, 1, q)
                            if routed and e and c == 0:
                                k = routed * (st.n(1) - 1) + e
                                act.wait_ge(cw_ready, k)
                                wait(act, d_read, E * (st.n(1) - 1) + (e - 1 if e > 2 else 0))
                                act.activation(cw[:, e % 2, :], g.ps[:, R_BANK, :], ACT.Copy).then_inc(cw_done, 1)
                            act.wait_ge(gu_ready, m)
                            wait(act, h_done, m - 2)
                            act.activation(gate[:, par, :], g.ps[:, G_BANK + par, :], ACT.Silu).then_inc(gate_done, 1)
                        for k, qq in (((1, q - 1),) if q else ((2, EC - 1),)):
                            if st.has(k):
                                m, _ = position(st, k, qq)
                                act.wait_ge(h_done, m)
                                wait(act, down_done, m - C)
                                act.activation(h_hi[:, qq % C, :], h[:, qq % C, :], ACT.Copy).then_inc(h_hi_done, 1)
                        if q == X_AT and st.has(0):
                            act.wait_ge(xp_ready, st.n(0))
                            if routed:
                                wait(act, lg_ready, st.n(0) - 1)
                                act.activation(xT[:], g.ps[:, T_BANK, :], ACT.Copy).then_inc(xT_done, 1)
                            wait(act, gu_ready, EC * (st.n(0) - 2))
                            act.activation(x_hi[st.slot(0, 2)][:], g.ps[:, T_BANK, :], ACT.Copy).then_inc(x_hi_done, 1)
                        if routed and q == COMB_AT and st.has(0):
                            act.wait_ge(shifted, st.n(0))
                            act.activation(pr[:], pr[:], ACT.Exp).then_inc(p_exp, 1)

                run_steps(act, B, OUT_LAG, step, U=2)

            @block.vector
            def _(dve):
                def softmax_top2(st, part):
                    n, r = st.n(0), st.slot(0, 2)
                    logits = g.ps[:, R_BANK, 0:TB * 8].rearrange("p (t e) -> p t e", t=TB)[:, :, 0:routed]
                    wide = [P, TB, routed]
                    cube = [P, TB, routed, routed]
                    p_e = pr[:, :, :, None].to_broadcast(cube)
                    p_j = pr[:, :, None, :].to_broadcast(cube)
                    link = Link(dve, chain, n, 12, done=(0, 1, 3, 6, 8, 10, 12)[part])
                    if part == 0:
                        if isinstance(st.i, int) and n == 1:
                            dve.wait_ge(small_loaded, 32)
                        dve.wait_ge(lg_ready, n)
                        link(dve.tensor_reduce(mx[:], logits, AX_X, ALU.max))
                        dve.tensor_tensor(pr[:], logits, mx[:, :, None].to_broadcast(wide), ALU.subtract
                                          ).then_inc(shifted, 1)
                    elif part == 1:
                        dve.wait_ge(p_exp, n)
                        link(dve.tensor_reduce(sm[:], pr[:], AX_X, ALU.add))
                        link(dve.reciprocal(sm[:], sm[:]))
                    elif part == 2:
                        link(dve.tensor_tensor(pr[:], pr[:], sm[:, :, None].to_broadcast(wide), ALU.mult))
                        link(dve.tensor_tensor(eq[:], p_j, p_e, ALU.is_equal))
                        link(dve.tensor_tensor(eq[:], eq[:], lower[:, None, :, :].to_broadcast(cube), ALU.mult))
                    elif part == 3:
                        link(dve.tensor_tensor(gt[:], p_j, p_e, ALU.is_gt))
                        link(dve.tensor_tensor(gt[:], gt[:], eq[:], ALU.add))
                    elif part == 4:
                        link(dve.tensor_reduce(sel[:], gt[:], AX_X, ALU.add))
                        link(dve.scalar_tensor_tensor(pr[:], sel[:], 2.0, pr[:], ALU.is_lt, ALU.mult))
                    elif part == 5:
                        link(dve.tensor_reduce(sm[:], pr[:], AX_X, ALU.add))
                        link(dve.tensor_scalar(sm[:], sm[:], 1e-9, None, ALU.add))
                        dve.reciprocal(mx[:], sm[:]).then_inc(recip_done, 1)
                    else:
                        dve.wait_ge(recip_done, n)
                        wait(dve, cw_ready, routed * (n - 2))
                        dve.tensor_tensor(comb[r][:], pr[:], mx[:, :, None].to_broadcast(wide), ALU.mult
                                          ).then_inc(comb_done, 1)

                def add_up(st, k, e):
                    n = st.n(k)
                    bank = g.ps[:, D_BANK + (E * (st.c - k - 1) + e) % 2, :]
                    dve.wait_ge(d_ready, E * (n - 1) + e + 1)
                    if e == 0:
                        wait(dve, out_ready, n - 1)
                        dve.tensor_copy(acc[:], bank).then_inc(d_read, 1)
                        return
                    dve.wait_ge(cw_done, routed * (n - 1) + e)
                    wait(dve, acc_done, routed * (n - 1) + e - 1)
                    dve.tensor_tensor(part[:], bank, cw[:, e % 2, :], ALU.mult).then_inc(d_read, 1)
                    dve.wait_ge(d_read, E * (n - 1) + e + 1)
                    dve.tensor_tensor(acc[:], acc[:], part[:], ALU.add).then_inc(acc_done, 1)

                def step(st):
                    if isinstance(st.i, int) and st.i == 0 and st.c == 1 and quant:
                        dve.wait_ge(stage_loaded[0], 16)
                        dve.tensor_scalar(stage_f[:, 0, :], stage[:, 0, :], float(np.float32(1.0 / 127.0)), None,
                                          ALU.mult).then_inc(dequant_done, 1)
                    for q in range(EC):
                        e, c = divmod(q, C)
                        if isinstance(st.i, int) and st.c + 2 * st.i == 2 and c == 0:
                            dve.wait_ge(w_hi_done, e + 1)
                            dve.tensor_tensor(w_lo[:, e, :], stage_f[:, e % 2, :], w_hi[:, e, :].bitcast(F32),
                                              ALU.subtract).then_inc(w_done, 1)
                        if st.has(1):
                            m, par = position(st, 1, q)
                            dve.wait_ge(gate_done, m)
                            wait(dve, h_lo_done, m - C)
                            dve.tensor_tensor(h[:, c, :], gate[:, par, :], g.ps[:, U_BANK + par, :], ALU.mult
                                              ).then_inc(h_done, 1)
                        for k, qq in (((1, q - 1),) if q else ((2, EC - 1),)):
                            if st.has(k):
                                m, _ = position(st, k, qq)
                                dve.wait_ge(h_hi_done, m)
                                dve.tensor_tensor(h_lo[:, qq % C, :], h[:, qq % C, :],
                                                  h_hi[:, qq % C, :].bitcast(F32), ALU.subtract).then_inc(h_lo_done, 1)
                        for e2 in range(E):
                            at = C * e2 + C + DOWN_LAG
                            if at == q and st.has(1):
                                add_up(st, 1, e2)
                            if at - EC == q and st.has(2):
                                add_up(st, 2, e2)
                        if q == OUT_AT + 1 and st.has(OUT_LAG):
                            dve.wait_ge(out_ready, st.n(OUT_LAG))
                            dst = batch_of(g.x_all, st.n(OUT_LAG))
                            dve.tensor_tensor(dst, g.ps[:, T_BANK, :].rearrange("p (t d) -> p t d", t=TB), dst,
                                              ALU.add).then_inc(out_added, 1)
                        if q == X_AT - 1 and st.has(0):
                            wait(dve, xp_ready, st.n(0) - 1)
                            normalise(dve, g.x_all, g.mean_var, g.rstd, st.n(0), xn, xn_done)
                        if q == X_AT and st.has(0):
                            dve.wait_ge(x_hi_done, st.n(0))
                            dve.tensor_tensor(x_lo[st.slot(0, 2)][:], g.ps[:, T_BANK, :],
                                              x_hi[st.slot(0, 2)][:].bitcast(F32), ALU.subtract).then_inc(x_lo_done, 1)
                        if routed and COMB_AT <= q < COMB_AT + 7 and st.has(0):
                            softmax_top2(st, q - COMB_AT)

                run_steps(dve, B, OUT_LAG, step, U=2)


class Memory:
    pass


def build(nc, a, out, layers=range(8)):
    g = Memory()
    dram = lambda name, shape: nc.dram_tensor(name, shape, F32).ap()
    g.q_hi8, g.q_lo8, g.k_hi8, g.k_lo8 = (dram(k, [B * P, S]) for k in ("q_hi8", "q_lo8", "k_hi8", "k_lo8"))
    g.v8 = dram("v8", [B * 4, S, P])
    g.o8 = dram("o8", [B * 4, TB, P, 32])
    g.o32 = dram("o32", [B * 8, TB, P, P])
    g.lines = dram("lines", [16, 1024])
    g.strips = dram("strips", [16, P, STRIP])
    g.decay = a["decay_strip"]
    g.pick, g.w_qkv, g.b_out = a["pick"], a["b0_wqkv"], a["b0_bout"]
    g.w_out32 = [a["b0_wout"][k * P:(k + 1) * P, :] for k in range(8)]
    with ExitStack() as stack:
        sb = lambda name, shape, dt=F32: stack.enter_context(nc.sbuf_tensor(name, shape, dt))
        g.ps = stack.enter_context(nc.psum_tensor("ps", [P, 8, 512], F32))
        g.x_all = sb("x_all", [P, TILES, DM])
        g.mean_var = sb("mean_var", [P, TILES, 2])
        g.rstd = sb("rstd", [P, TILES])
        g.ident = sb("ident", [P, P])
        x_tiles = a["x"].rearrange("(t p) d -> p t d", p=P)
        g.w_out8 = {"out_a0": a["a0_wo"], "out_a1": a["a1_wo"]}
        with Phase(nc, "begin") as ph:
            loaded = ph.sem("loaded")
            with nc.Block() as block:
                @block.sync
                def _(sp):
                    sp.dma_start(g.x_all[:], x_tiles).then_inc(loaded, 16)
                    sp.dma_start(g.ident[:], a["ident"]).then_inc(loaded, 16)
                    sp.wait_ge(loaded, 32)

        if 0 in layers:
            row_stats(nc, "st_a0", g.x_all, g.mean_var, g.rstd, 1e-5)
            scale = float(np.float32(1.0) / (np.sqrt(np.float32(DM)) + np.float32(1e-8)))
            project_small(nc, g, "in_a0", scale, (a["a0_wdown"], a["a0_wupk"], a["a0_wupv"]),
                          (a["a0_wq"], a["a0_wk"], a["a0_wv"]))
            attend_small(nc, g, "at_a0", True)
            project_out(nc, g, "out_a0", False)
        def mixture(k):
            row_stats(nc, f"st_moe{k}", g.x_all, g.mean_var, g.rstd, 1e-5)
            swiglu(nc, g, f"moe{k}", a["moe_w"], EXPERTS, DFF // P, (a["router"], a["lower"]))

        def quantised(k):
            row_stats(nc, f"st_ffn{k}", g.x_all, g.mean_var, g.rstd, 1e-5)
            swiglu(nc, g, f"ffn{k}", a["ffn_w"], 1, HID // P)

        if 1 in layers:
            mixture(1)
        if 2 in layers:
            row_stats(nc, "st_b0", g.x_all, g.mean_var, g.rstd, 1e-5)
            attend_wide(nc, g, "at_b0", 32 ** -0.5)
            with nc.sbuf_tensor("y_all", [P, TILES, DM], F32) as g.y_all:
                project_out(nc, g, "out_b0", True)
                row_stats(nc, "st_y", g.y_all, g.mean_var, g.rstd, 1e-6)
                add_normalised(nc, g, "ln_b0", g.y_all, a["b0_gamma"], a["b0_beta"])
        if 3 in layers:
            mixture(3)
        if 4 in layers:
            bias_strips(nc, g, "bias_a1", a["taps"], a["line_table"], a["wpos"], a["flip"])
            row_stats(nc, "st_a1", g.x_all, g.mean_var, g.rstd, 1e-5)
            project_small(nc, g, "in_a1", 8 ** -0.5, None, [a["a1_wqkv"][:, k * P:(k + 1) * P] for k in range(3)])
            attend_small(nc, g, "at_a1", False)
            project_out(nc, g, "out_a1", False)
        if 5 in layers:
            quantised(5)
        if 6 in layers:
            row_stats(nc, "st_lin", g.x_all, g.mean_var, g.rstd, 1e-5)
            with nc.sbuf_tensor("z_all", [P, TILES, DM], F32) as g.y_all:
                linear_attention(nc, g, "lin", {k[4:]: v for k, v in a.items() if k.startswith("lin_")})
                row_stats(nc, "st_z", g.y_all, g.mean_var, g.rstd, 1e-5)
                add_normalised(nc, g, "ln_lin", g.y_all, a["ln_gamma"], a["ln_beta"])
        if 7 in layers:
            quantised(7)
        with Phase(nc, "end") as ph:
            stored = ph.sem("stored")
            with nc.Block() as block:
                @block.sync
                def _(sp):
                    sp.dma_start(out.rearrange("(t p) d -> p t d", p=P), g.x_all[:]).then_inc(stored, 16)
                    sp.wait_ge(stored, 16)


def pack(gate, up, down):
    import numpy as np
    chunks = down.T.reshape(-1, 128, 128)
    return np.concatenate([gate.T, up.T, *chunks], axis=1)


def line_table():
    import numpy as np
    ramp = np.linspace(0.0, 1.0, 64, dtype=np.float32)
    rel = np.abs(np.arange(1024) - 511).astype(np.float32) / np.float32(511)
    point = np.clip(np.round(rel * np.float32(63)).astype(np.int64), 0, 63)
    at = point[None, :] - np.arange(101)[:, None]
    return np.where(at >= 0, ramp[np.maximum(at, 0)], np.float32(0)).astype(np.float32)


def wide_columns(w):
    import numpy as np
    qk = w[:, :2048].reshape(128, 16, 4, 32).transpose(0, 1, 3, 2).reshape(128, 2048)
    return np.concatenate([qk, w[:, 2048:]], axis=1)


def linear_layouts(f):
    import numpy as np
    row = np.arange(128)
    h, d = row // 4, row % 4
    m, hm = np.arange(64) // 32, np.arange(64) % 32
    pad = lambda t: np.concatenate([t, np.zeros_like(t)], axis=0)
    wq, wk, wv, wb, wm = (f[f"L1_attn_b_{k}"] for k in ("Wq", "Wk", "Wv", "Wbeta", "Wmix"))
    bb, bm = f["L1_attn_b_bbeta"], f["L1_attn_b_bmix"]
    swap = 4 * h + (d + 2) % 4
    w = [wq, wq[swap], wk, wk[swap], wb[2 * h], wb[2 * h + 1], pad(wm[2 * hm + m]), pad(wm[2 * hm + 1 - m])]
    w += [wv[4 * h + c] for c in range(4)]
    freq = np.where(d % 2 == 0, np.float32(1.0), np.float32(1.0) / np.float32(10000.0) ** np.float32(0.5))
    angle = np.arange(512, dtype=np.float32)[None, :] * freq.astype(np.float32)[:, None]
    sign = np.where(d < 2, np.float32(-1), np.float32(1))[:, None]
    one = np.float32(1)
    return {
        "lin_w": np.stack(w).transpose(2, 0, 1),
        "lin_w_out": f["L1_attn_b_Wout"].T, "lin_bout": f["L1_attn_b_bout"],
        "lin_bias": np.stack([bb[2 * h], bb[2 * h + 1], pad(bm[2 * hm + m]), pad(bm[2 * hm + 1 - m])], axis=1),
        "lin_rope": np.stack([np.cos(angle), np.sin(angle) * sign], axis=1).astype(np.float32),
        "lin_to_c": ((h[:, None, None] == h) & (np.arange(4)[:, None] == d)) * one,
        "lin_to_m": ((h[:, None, None] == hm) & (np.arange(2)[:, None] == m)) * one,
        "lin_from_m": np.stack([pad(((hm[:, None] == h) & (m[:, None] == k)) * one) for k in range(2)], axis=1),
        "ln_gamma": f["L1_attn_b_ln_g"], "ln_beta": f["L1_attn_b_ln_b"],
    }


def laid_out(i):
    import numpy as np
    f = {k: np.asarray(v) for k, v in i.items()}
    p = np.arange(128)[:, None]
    strip_delta = np.abs(np.arange(896)[None, :] - p - 384).astype(np.float32)
    d = {
        "x": f["L0_attn_a_x"].reshape(-1, 128),
        "ident": np.eye(128, dtype=np.float32),
        "decay_strip": np.exp(np.float32(-0.01 * 0.01) * strip_delta).astype(np.float32),
        "a0_wq": f["L0_attn_a_Wq"], "a0_wk": f["L0_attn_a_Wk"], "a0_wv": f["L0_attn_a_Wv"],
        "a0_wo": f["L0_attn_a_Wo"], "a0_wdown": f["L0_attn_a_W_down_kv"],
        "a0_wupk": f["L0_attn_a_W_up_k"], "a0_wupv": f["L0_attn_a_W_up_v"],
        "a1_wo": f["L1_attn_a_Wout"].T, "a1_wqkv": f["L1_attn_a_Wqkv"].T,
        "taps": f["L1_attn_a_coeffs"].T, "wpos": f["L1_attn_a_Wpos"].T,
        "line_table": line_table(), "flip": np.eye(128, dtype=np.float32)[::-1],
        "pick": np.eye(128, dtype=np.float32)[:, ::32],
        "b0_wqkv": wide_columns(f["L0_attn_b_w_qkv"]), "b0_wout": f["L0_attn_b_w_out"], "b0_bout": f["L0_attn_b_b_out"],
        "b0_gamma": f["L0_attn_b_ln_gamma"], "b0_beta": f["L0_attn_b_ln_beta"],
        "moe_w": np.stack([pack(*w) for w in [
            (f["L0_ffn_shared_gate"], f["L0_ffn_shared_up"], f["L0_ffn_shared_down"]),
            *zip(f["L0_ffn_routed_gate"], f["L0_ffn_routed_up"], f["L0_ffn_routed_down"])]]),
        "router": f["L0_ffn_router_w"].T,
        "lower": np.tril(np.ones((7, 7), np.float32), -1),
        "ffn_w": pack(f["L1_ffn_w_gate"], f["L1_ffn_w_up"], f["L1_ffn_w_down"])[None],
    }
    d.update(linear_layouts(f))
    return {k: np.ascontiguousarray(v) for k, v in d.items()}


def kernel(**inputs):
    import concourse.bacc as _bacc
    from concourse import mybir as _mybir
    from concourse.bass_utils import run_bass_kernel_spmd as _run

    nc = _bacc.Bacc("TRN2", target_bir_lowering=False, num_devices=1)
    arrays = laid_out(inputs)
    a = {k: nc.dram_tensor(f"in_{k}", v.shape, _mybir.dt.from_np(v.dtype), kind="ExternalInput").ap()
         for k, v in arrays.items()}
    out = nc.dram_tensor("out", (8 * 512, 128), _mybir.dt.float32, kind="ExternalOutput").ap()
    build(nc, a, out)
    r = _run(nc, [{f"in_{k}": v for k, v in arrays.items()}], core_ids=[0])
    return r.results[0]["out"].reshape(8, 512, 128)
```

```python
from contextlib import ExitStack

import concourse.bass as bass
import numpy as np
from concourse import mybir

ALU = mybir.AluOpType
ACT = mybir.ActivationFunctionType
F32 = mybir.dt.float32
F32R = mybir.dt.float32r
I32 = mybir.dt.int32
AX_X = mybir.AxisListType.X

P = 128
B, S, DM = 8, 512, 128
TB = S // P
TILES = B * TB
HG = 4
KROWS = 96
CLAMP = 10000.0
STRIP = S + (TB - 1) * P
STRIP0 = (TB - 1) * P
EXPERTS, DFF = 8, 512
HID = 384


class Phase:

    def __init__(self, nc, name):
        self.nc, self.name = nc, name

    def __enter__(self):
        self.stack = ExitStack().__enter__()
        self.sems = []
        return self

    def sb(self, name, shape, dt=F32):
        return self.stack.enter_context(self.nc.sbuf_tensor(f"{self.name}_{name}", shape, dt))

    def sem(self, name):
        s = self.stack.enter_context(self.nc.semaphore(f"{self.name}_{name}"))
        self.sems.append(s)
        return s

    def __exit__(self, *exc):
        if exc[0] is None:
            for s in self.sems:
                self.nc.sync.sem_clear(s)
            self.nc.all_engine_barrier()
        return self.stack.__exit__(*exc)


def wait(eng, sem, value):
    if isinstance(value, int) and value <= 0:
        return
    eng.wait_ge(sem, value)


def settle(eng, sem):
    eng.sem_inc(sem, 1)


class Link:

    def __init__(self, eng, sem, n, k, done=0):
        self.eng, self.sem, self.n, self.k, self.done = eng, sem, n, k, done

    def __call__(self, ins):
        self.done += 1
        assert self.done <= self.k
        ins.then_inc(self.sem, 1)
        self.eng.wait_ge(self.sem, self.k * (self.n - 1) + self.done)


class Step:

    def __init__(self, i, c, count, U=4):
        self.i, self.c, self.count, self.U = i, c, count, U

    def has(self, k):
        return not isinstance(self.i, int) or 1 <= self.U * self.i + self.c - k <= self.count

    def n(self, k):
        return self.U * self.i + (self.c - k)

    def slot(self, k, ring):
        return (self.c - k) % ring

    def use(self, k, ring):
        return self.U // ring * self.i + (self.c - k + ring - 1) // ring


def run_steps(eng, count, extra, step, U=4):
    peeled = max(1, -(-extra // U))
    for i in range(peeled):
        for c in range(1, U + 1):
            step(Step(i, c, count, U))
    with eng.Fori(peeled, count // U) as i:
        for c in range(1, U + 1):
            step(Step(i, c, count, U))
    for c in range(1, extra + 1):
        step(Step(count // U, c, count, U))


RSQRT_LINKS = 12


def rsqrt(dve, link, var, eps, y, t):
    y_bits, t_bits = y.bitcast(I32), t.bitcast(I32)
    link(dve.tensor_scalar(var, var, eps, None, ALU.add))
    link(dve.tensor_scalar(t_bits, var.bitcast(I32), 1, None, ALU.logical_shift_right))
    link(dve.tensor_scalar(y_bits, t_bits, -1.0, float(0x5F3759DF), ALU.mult, ALU.add))
    for _ in range(3):
        link(dve.tensor_tensor(t, y, y, ALU.mult))
        link(dve.scalar_tensor_tensor(t, t, -0.5, var, ALU.mult, ALU.mult))
        link(dve.scalar_tensor_tensor(y, t, 1.5, y, ALU.add, ALU.mult))


def row_stats(nc, name, x_all, mean_var, rstd, eps, stats=None):
    with Phase(nc, name) as ph:
        taken = stats is not None
        stats = stats if taken else ph.sb("stats", [P, TILES, 6])
        t = ph.sb("t", [P, TILES])
        var = ph.sb("var", [P, TILES])
        stats_done, aggr_done, chain = ph.sem("stats_done"), ph.sem("aggr_done"), ph.sem("chain")
        with nc.Block() as block:
            @block.vector
            def _(dve):
                if not taken:
                    for tile in range(TILES):
                        dve.bn_stats(stats[:, tile, :], x_all[:, tile, :]).then_inc(stats_done, 1)
                    dve.wait_ge(stats_done, TILES)
                for tile in range(TILES):
                    dve.bn_aggr(mean_var[:, tile, :], stats[:, tile, :]).then_inc(aggr_done, 1)
                dve.wait_ge(aggr_done, TILES)
                link = Link(dve, chain, 1, RSQRT_LINKS + 1)
                link(dve.tensor_copy(var[:], mean_var[:, :, 1]))
                rsqrt(dve, link, var[:], eps, rstd[:], t[:])


def normalise(dve, x_all, mean_var, rstd, n, xn, done):
    for tb in range(TB):
        tile = (n - 1) * TB + tb
        if isinstance(tile, int):
            x, m, r = x_all[:, tile, :], mean_var[:, tile, 0:1], rstd[:, tile:tile + 1]
        else:
            x = x_all[:, bass.ds(tile, 1), :].rearrange("p a n -> p (a n)")
            m = mean_var[:, bass.ds(tile, 1), 0:1].rearrange("p a n -> p (a n)")
            r = rstd[:, bass.ds(tile, 1)]
        dve.tensor_scalar(xn[:, tb, :], x, m, r, ALU.subtract, ALU.mult).then_inc(done, 1)


def batch_of(x_all, n):
    return x_all[:, bass.ds((n - 1) * TB, TB), :]


def item(dram, n):
    return dram[bass.ds(n - 1, 1)]


def project_small(nc, g, name, scale, latent, weights):
    with Phase(nc, name) as ph:
        n_w = len(weights)
        w = ph.sb("w", [P, n_w, DM])
        wd, wu = (ph.sb("wd", [P, 32]), ph.sb("wu", [32, 2, DM])) if latent else (None, None)
        xn = ph.sb("xn", [P, TB, DM])
        xT = [ph.sb(f"xT{r}", [P, S]) for r in range(2)]
        xT_rev = [ph.sb(f"xT_rev{r}", [P, S]) for r in range(2)]
        kv = ph.sb("kv", [P, S])
        lat = ph.sb("lat", [32, S])
        hi = [ph.sb(f"hi{r}", [P, 2, S], F32R) for r in range(2)]
        lo = [ph.sb(f"lo{r}", [P, 2, S], F32R) for r in range(2)]
        va = [ph.sb(f"va{r}", [P, TB, 16, 32]) for r in range(2)]
        w_loaded = ph.sem("w_loaded")
        ones_set = ph.sem("ones_set")
        xn_done, xp_ready, xT_done = (ph.sem(k) for k in ("xn_done", "xp_ready", "xT_done"))
        proj_done, hi_done, lo_done, v_done = (ph.sem(k) for k in ("proj_done", "hi_done", "lo_done", "v_done"))
        kv_ready, kv_done, lat_ready, lat_done = (ph.sem(k) for k in ("kv_ready", "kv_done", "lat_ready", "lat_done"))
        stored = [ph.sem(f"stored{r}") for r in range(2)]
        sp_settled = ph.sem("sp_settled")
        bank_x, bank_q, bank_k, bank_kv, bank_lat, bank_v = (g.ps[:, k, :] for k in range(6))
        bank_rev = bank_kv
        n_loads = n_w + (3 if latent else 0)
        q_w = w[:, 0, :]

        with nc.Block() as block:
            @block.sync
            def _(sp):
                for k, src in enumerate(weights):
                    sp.dma_start(w[:, k, :], src).then_inc(w_loaded, 16)
                if latent:
                    for dst, src in zip((wd[:], wu[:, 0, :], wu[:, 1, :]), latent):
                        sp.dma_start(dst, src).then_inc(w_loaded, 16)

                def step(st):
                    if st.has(1):
                        n, r = st.n(1), st.slot(1, 2)
                        sp.wait_ge(lo_done, 2 * n)
                        settle(sp, sp_settled)
                        for k, (dh, dl) in enumerate(((g.q_hi8, g.q_lo8), (g.k_hi8, g.k_lo8))):
                            for dst, src in ((dh, hi[r]), (dl, lo[r])):
                                sp.dma_start(dst[bass.ds((n - 1) * P, P), :], src[:, k, :].bitcast(F32)
                                             ).then_inc(stored[r], 16)
                        sp.wait_ge(v_done, n)
                        settle(sp, sp_settled)
                        for hg in range(4):
                            sp.dma_start(g.v8[bass.ds((n - 1) * 4 + hg, 1)].rearrange("a (t p) n -> p (a t) n", p=P),
                                         va[r][:, :, hg * HG:(hg + 1) * HG, :].rearrange("p t h d -> p t (h d)")
                                         ).then_inc(stored[r], 16)

                run_steps(sp, B, 2, step, U=2)
                for r in range(2):
                    sp.wait_ge(stored[r], 16 * 8 * B // 2)

            @block.vector
            def _(dve):
                for r in range(2):
                    dve.memset(va[r][:], 0.0).then_inc(ones_set, 1)
                dve.wait_ge(ones_set, 2)
                for r in range(2):
                    dve.memset(va[r][:, :, :, 8:9], 1.0).then_inc(ones_set, 1)
                dve.wait_ge(ones_set, 4)

                def step(st):
                    if st.has(0):
                        wait(dve, xp_ready, st.n(0) - 1)
                        normalise(dve, g.x_all, g.mean_var, g.rstd, st.n(0), xn, xn_done)
                    if st.has(1):
                        n, r = st.n(1), st.slot(1, 2)
                        for k, bank in enumerate((bank_q, bank_k)):
                            dve.wait_ge(hi_done, 2 * (n - 1) + k + 1)
                            wait(dve, stored[r], 16 * 8 * (st.use(1, 2) - 1))
                            dve.scalar_tensor_tensor(lo[r][:, k, :], bank, scale if k == 0 else 1.0,
                                                     hi[r][:, k, :].bitcast(F32), ALU.mult, ALU.subtract
                                                     ).then_inc(lo_done, 1)
                        dve.wait_ge(proj_done, 3 * n)
                        dve.tensor_copy(va[r][:, :, :, 0:8], bank_v.rearrange("p (t h d) -> p t h d", t=TB, d=8)
                                        ).then_inc(v_done, 1)

                run_steps(dve, B, 2, step, U=2)

            @block.scalar
            def _(act):
                def step(st):
                    if latent and st.has(1):
                        act.wait_ge(kv_ready, st.n(1))
                        wait(act, lat_ready, st.n(1) - 1)
                        act.activation(kv[:], bank_kv, ACT.Copy).then_inc(kv_done, 1)
                    if st.has(0):
                        act.wait_ge(xp_ready, st.n(0))
                        wait(act, proj_done, 3 * (st.n(0) - 2))
                        ins = act.activation(xT[st.slot(0, 2)][:], bank_x, ACT.Copy)
                        if not latent:
                            ins = act.activation(xT_rev[st.slot(0, 2)][:], bank_rev, ACT.Copy)
                        ins.then_inc(xT_done, 1)
                    if latent and st.has(1):
                        act.wait_ge(lat_ready, st.n(1))
                        wait(act, proj_done, 3 * (st.n(1) - 1))
                        act.activation(lat[:], bank_lat[0:32, :], ACT.Copy).then_inc(lat_done, 1)
                    if st.has(1):
                        n, r = st.n(1), st.slot(1, 2)
                        wait(act, stored[r], 16 * 8 * (st.use(1, 2) - 1))
                        for k, bank in enumerate((bank_q, bank_k)):
                            act.wait_ge(proj_done, 3 * (n - 1) + k + 1)
                            act.activation(hi[r][:, k, :], bank, ACT.Copy,
                                           scale=scale if k == 0 else 1.0).then_inc(hi_done, 1)

                run_steps(act, B, 2, step, U=2)

            @block.tensor
            def _(pe):
                pe.wait_ge(w_loaded, 16 * n_loads)

                def step(st):
                    x = xT[st.slot(1, 2)]
                    if latent and st.has(1):
                        n = st.n(1)
                        pe.wait_ge(xT_done, n)
                        wait(pe, kv_done, n - 1)
                        pe.matmul(bank_kv, w[:, 1, :], x[:], start=True, stop=False)
                        pe.matmul(bank_kv, w[:, 2, :], x[:], start=False, stop=True).then_inc(kv_ready, 1)
                    if st.has(0):
                        pe.wait_ge(xn_done, TB * st.n(0))
                        wait(pe, xT_done, st.n(0) - 1)
                        for tb in range(TB):
                            ins = pe.transpose(bank_x[:, tb * P:(tb + 1) * P], xn[:, tb, :], g.ident[:])
                        if not latent:
                            for tb in range(TB):
                                ins = pe.matmul(bank_rev[:, tb * P:(tb + 1) * P], xn[:, tb, :], g.flip[:],
                                                start=True, stop=True)
                        ins.then_inc(xp_ready, 1)
                    if st.has(1):
                        n = st.n(1)
                        pe.wait_ge(xT_done, n)
                        wait(pe, lo_done, 2 * (n - 1))
                        wait(pe, v_done, n - 1)
                        if latent:
                            pe.wait_ge(kv_done, n)
                            wait(pe, lat_done, n - 1)
                            pe.matmul(bank_lat[0:32, :], wd[:], kv[:], start=True, stop=True).then_inc(lat_ready, 1)
                        x_q = x if latent else xT_rev[st.slot(1, 2)]
                        pe.matmul(bank_q, q_w, x_q[:], start=True, stop=True).then_inc(proj_done, 1)
                        if latent:
                            pe.wait_ge(lat_done, n)
                            pe.matmul(bank_k, wu[:, 0, :], lat[:], start=True, stop=True).then_inc(proj_done, 1)
                        else:
                            pe.matmul(bank_k, w[:, 1, :], x[:], start=True, stop=True).then_inc(proj_done, 1)
                        for tb in range(TB):
                            cols = slice(tb * P, (tb + 1) * P)
                            ins = pe.matmul(bank_v[:, cols], lat[:, cols] if latent else x[:, cols],
                                            wu[:, 1, :] if latent else w[:, 2, :], start=True, stop=True)
                        ins.then_inc(proj_done, 1)

                run_steps(pe, B, 2, step, U=2)


def attend_small(nc, g, name, decay):
    NG = 4 * B

    def place(st, k):
        later, batch = divmod(st.c - k - 1, B)
        return batch, st.i + later

    with Phase(nc, name) as ph:
        q4 = [ph.sb(f"q4_{r}", [P, HG, S], F32R) for r in range(2)]
        k4 = [ph.sb(f"k4_{r}", [P, HG, S], F32R) for r in range(2)]
        v4 = [ph.sb(f"v4_{r}", [P, TB, P]) for r in range(4)]
        decay_strip = ph.sb("decay_strip", [P, STRIP]) if decay else None
        strip = None if decay else ph.sb("strip", [P, HG, STRIP])
        clipped = ph.sb("clipped", [P, TB, S]) if decay else None
        logits = ph.sb("logits", [P, 2, TB, S])
        top = ph.sb("top", [P, 2, TB])
        neg_top = ph.sb("neg_top", [P, 2, TB])
        e = ph.sb("e", [P, HG, TB, S])
        eT = [ph.sb(f"eT_{r}", [P, HG, TB, S]) for r in range(2)]
        o_sb = ph.sb("o_sb", [P, S])
        r16 = ph.sb("r16", [P, TB, HG])
        o_tok = [ph.sb(f"o_tok{r}", [P, TB, HG, 8]) for r in range(2)]
        zeroed, decay_loaded = ph.sem("zeroed"), ph.sem("decay_loaded")
        loaded = [ph.sem(f"loaded{r}") for r in range(2)]
        v_loaded = [ph.sem(f"v_loaded{r}") for r in range(4)]
        s_ready, logits_done, top_done = ph.sem("s_ready"), ph.sem("logits_done"), ph.sem("top_done")
        clip_done = ph.sem("clip_done")
        dve_settled, sp_settled = ph.sem("dve_settled"), ph.sem("sp_settled")
        s_read = clip_done if decay else logits_done
        exp_done, tr_ready = ph.sem("exp_done"), ph.sem("tr_ready")
        tr_read = [ph.sem(f"tr_read{kb}") for kb in range(TB)]
        pv_done, o_copied, oT_ready, recip_done, o_done = (
            ph.sem(k) for k in ("pv_done", "o_copied", "oT_ready", "recip_done", "o_done"))
        stored = [ph.sem(f"stored{r}") for r in range(2)]
        S_BANK, TR_BANK, PV_BANK, OT_BANK = 0, 2, 6, 7
        on_dve = () if decay else (3,)
        strip_loaded = [] if decay else [ph.sem(f"strip_loaded{j}") for j in range(HG)]

        with nc.Block() as block:
            @block.gpsimd
            def _(pool):
                for r in range(2):
                    pool.memset(q4[r][:].bitcast(F32), 0.0).then_inc(zeroed, 1)
                    pool.memset(k4[r][:].bitcast(F32), 0.0).then_inc(zeroed, 1)

            @block.sync
            def _(sp):
                if decay:
                    sp.dma_start(decay_strip[:], g.decay).then_inc(decay_loaded, 16)
                sp.wait_ge(zeroed, 4)

                def step(st):
                    if st.has(0):
                        n, r, rv = st.n(0), st.slot(0, 2), st.slot(0, 4)
                        batch, heads = place(st, 0)
                        wait(sp, s_ready, 16 * (n - 2))
                        settle(sp, sp_settled)
                        for row, dq, dk in ((0, g.q_hi8, g.k_hi8), (32, g.q_hi8, g.k_lo8), (64, g.q_lo8, g.k_hi8)):
                            for dst, src in ((q4[r], dq), (k4[r], dk)):
                                sp.dma_start(dst[row:row + 8].bitcast(F32),
                                             src[bass.ds(batch * P + heads * 32, 32), :].rearrange("(j d) n -> d j n", d=8)
                                             ).then_inc(loaded[r], 16)
                        wait(sp, pv_done, n - 4)
                        settle(sp, sp_settled)
                        sp.dma_start(v4[rv][:], item(g.v8, batch * 4 + heads + 1).rearrange("a (t p) n -> p (a t) n", p=P)
                                     ).then_inc(v_loaded[rv], 16)
                        if not decay and st.c == 1:
                            for j in range(HG):
                                wait(sp, logits_done, 16 * (n - 2) + 4 * j + 4)
                                settle(sp, sp_settled)
                                rows = bass.AP(g.lines.tensor, j * BIAS_LINE,
                                               [[HG * BIAS_LINE, 4], [1, P], [1, STRIP]])
                                sp.dma_start(strip[:, j, :], rows[bass.ds(heads, 1)].rearrange("a p x -> p (a x)")
                                             ).then_inc(strip_loaded[j], 16)
                    if st.has(4):
                        sp.wait_ge(o_done, st.n(4))
                        settle(sp, sp_settled)
                        r = st.slot(4, 2)
                        batch, heads = place(st, 4)
                        sp.dma_start(item(g.o8, batch * 4 + heads + 1).rearrange("a t p c -> p (a t) c"),
                                     o_tok[r][:].rearrange("p t j d -> p t (j d)")).then_inc(stored[r], 16)

                run_steps(sp, NG, 4, step, U=B)
                for r in range(2):
                    sp.wait_ge(stored[r], 16 * NG // 2)

            @block.tensor
            def _(pe):
                def scores(n, r, j, blocks):
                    for qb in blocks:
                        wait(pe, s_read, 16 * (n - 1) + 4 * j + qb - 1)
                        pe.matmul(g.ps[:, S_BANK + qb % 2, :], q4[r][0:KROWS, j, qb * P:(qb + 1) * P],
                                  k4[r][0:KROWS, j, :], start=True, stop=True).then_inc(s_ready, 1)

                def transposes(n, j, blocks):
                    pe.wait_ge(exp_done, 16 * (n - 1) + 4 * j + 4)
                    for kb in blocks:
                        wait(pe, tr_read[kb], 4 * (n - 1) + j)
                        for qb in range(TB):
                            bank = g.ps[:, TR_BANK + kb, qb * P:(qb + 1) * P]
                            block = e[:, j, qb, kb * P:(kb + 1) * P]
                            ins = pe.transpose(bank, block, g.ident[:] if decay else g.flip[:])
                        ins.then_inc(tr_ready, 1)

                def product(n, r, rv, kb):
                    if kb == 0:
                        for k in range(TB):
                            pe.wait_ge(tr_read[k], 4 * n)
                        wait(pe, o_copied, n - 1)
                    for j in range(HG):
                        ins = pe.matmul(g.ps[32 * j:32 * j + 32, PV_BANK, :], v4[rv][:, kb, 32 * j:32 * j + 32],
                                        eT[r][:, j, kb, :], start=(kb == 0), stop=(kb == TB - 1))
                    if kb == TB - 1:
                        ins.then_inc(pv_done, 1)

                def turn(n):
                    pe.wait_ge(o_copied, n)
                    wait(pe, o_done, n - 1)
                    for tb in range(TB):
                        ins = pe.transpose(g.ps[:, OT_BANK, tb * P:(tb + 1) * P], o_sb[:, tb * P:(tb + 1) * P],
                                           g.ident[:])
                    ins.then_inc(oT_ready, 1)

                def step(st):
                    now, before = st.has(0), st.has(1)
                    if now:
                        pe.wait_ge(loaded[st.slot(0, 2)], 16 * 6 * st.use(0, 2))
                    for j in range(HG):
                        k, jt = (0, j - 2) if j >= 2 else (1, j + 2)
                        for blocks, turned in (((0, 1), (0, 1)), ((2,), (2,)), ((3,), (3,))):
                            if now:
                                scores(st.n(0), st.slot(0, 2), j, blocks)
                            if st.has(k):
                                transposes(st.n(k), jt, turned)
                        if before and j >= 2:
                            if j == 2:
                                pe.wait_ge(v_loaded[st.slot(1, 4)], 16 * st.use(1, 4))
                            for kb in (2 * j - 4, 2 * j - 3):
                                product(st.n(1), st.slot(1, 2), st.slot(1, 4), kb)
                        if j == 1 and st.has(2):
                            turn(st.n(2))

                run_steps(pe, NG, 2, step, U=B)

            @block.scalar
            def _(act):
                def copies(n, r, j):
                    for kb in range(TB):
                        if kb in on_dve:
                            continue
                        act.wait_ge(tr_ready, 16 * (n - 1) + 4 * j + kb + 1)
                        if kb == 0 and j == 0:
                            wait(act, pv_done, n - 2)
                        act.activation(eT[r][:, j, kb, :], g.ps[:, TR_BANK + kb, :], ACT.Copy).then_inc(tr_read[kb], 1)

                def exps(n, j):
                    act.wait_ge(top_done, 4 * (n - 1) + j + 1)
                    wait(act, tr_ready, 16 * (n - 1) + 4 * j - 12)
                    for qb in range(TB):
                        act.activation(e[:, j, qb, :], logits[:, j % 2, qb, :], ACT.Exp,
                                       bias=neg_top[:, j % 2, qb:qb + 1]).then_inc(exp_done, 1)

                def copy_out(n):
                    act.wait_ge(pv_done, n)
                    wait(act, oT_ready, n - 1)
                    act.activation(o_sb[:], g.ps[:, PV_BANK, :], ACT.Copy).then_inc(o_copied, 1)

                def step(st):
                    for j in range(HG):
                        k, jt = (0, j - 2) if j >= 2 else (1, j + 2)
                        if st.has(k):
                            copies(st.n(k), st.slot(k, 2), jt)
                        if j == 0 and st.has(2):
                            copy_out(st.n(2))
                        if st.has(0):
                            exps(st.n(0), j)

                run_steps(act, NG, 2, step, U=B)

            @block.vector
            def _(dve):
                if decay:
                    dve.wait_ge(decay_loaded, 16)

                def clip(n, j, qb):
                    dve.wait_ge(s_ready, 16 * (n - 1) + 4 * j + qb + 1)
                    dve.tensor_scalar(clipped[:, qb, :], g.ps[:, S_BANK + qb % 2, :], -CLAMP, CLAMP,
                                      ALU.max, ALU.min).then_inc(clip_done, 1)

                def head(n, r, j):
                    wait(dve, exp_done, 16 * (n - 1) + 4 * j - 4)
                    if decay and j == 0:
                        clip(n, j, 0)
                    for qb in range(TB):
                        k = 16 * (n - 1) + 4 * j + qb + 1
                        cols = slice(STRIP0 - qb * P, STRIP0 - qb * P + S)
                        if decay:
                            dve.wait_ge(clip_done, k)
                            if qb + 1 < TB:
                                clip(n, j, qb + 1)
                            elif j + 1 < HG:
                                dve.wait_ge(logits_done, k - 3)
                                clip(n, j + 1, 0)
                            else:
                                settle(dve, dve_settled)
                            dve.tensor_tensor_reduce(logits[:, j % 2, qb, :], clipped[:, qb, :], decay_strip[:, cols],
                                                     1.0, -3e38, ALU.mult, ALU.max, top[:, j % 2, qb:qb + 1]
                                                     ).then_inc(logits_done, 1)
                        else:
                            dve.wait_ge(s_ready, k)
                            settle(dve, dve_settled)
                            dve.tensor_tensor_reduce(logits[:, j % 2, qb, :], g.ps[:, S_BANK + qb % 2, :],
                                                     strip[:, j, cols], 1.0, -3e38, ALU.add, ALU.max,
                                                     top[:, j % 2, qb:qb + 1]).then_inc(logits_done, 1)
                    dve.wait_ge(logits_done, 16 * (n - 1) + 4 * j + 4)
                    dve.tensor_scalar(neg_top[:, j % 2, :], top[:, j % 2, :], -1.0, None, ALU.mult).then_inc(top_done, 1)

                def copies(n, r, j):
                    for kb in on_dve:
                        dve.wait_ge(tr_ready, 16 * (n - 1) + 4 * j + kb + 1)
                        if j == 0:
                            wait(dve, pv_done, n - 2)
                        dve.tensor_copy(eT[r][:, j, kb, :], g.ps[:, TR_BANK + kb, :]).then_inc(tr_read[kb], 1)

                def finish(st):
                    n, r = st.n(2), st.slot(2, 2)
                    o = g.ps[:, OT_BANK, :].rearrange("p (t j d) -> p t j d", t=TB, j=HG)
                    dve.wait_ge(oT_ready, n)
                    dve.reciprocal(r16[:], o[:, :, :, 8]).then_inc(recip_done, 1)
                    dve.wait_ge(recip_done, n)
                    wait(dve, stored[r], 16 * (st.use(2, 2) - 1))
                    dve.tensor_tensor(o_tok[r][:], o[:, :, :, 0:8], r16[:, :, :, None].to_broadcast([P, TB, HG, 8]),
                                      ALU.mult).then_inc(o_done, 1)

                def step(st):
                    for j in range(HG):
                        if st.has(0):
                            if not decay and st.c == 1:
                                dve.wait_ge(strip_loaded[j], 16 * (st.i + 1))
                            head(st.n(0), st.slot(0, 2), j)
                        k, jt = (0, j - 2) if j >= 2 else (1, j + 2)
                        if st.has(k):
                            copies(st.n(k), st.slot(k, 2), jt)
                        if j == 2 and st.has(2):
                            finish(st)

                run_steps(dve, NG, 2, step, U=B)


def attend_wide(nc, g, name, scale):
    U = 8
    NG = B * U
    RQ = 4
    W = U * P
    with Phase(nc, name) as ph:
        w = ph.sb("w", [P, 3 * W])
        xn = ph.sb("xn", [P, TB, DM])
        xT, xT_v = ph.sb("xT", [P, S]), ph.sb("xT_v", [P, S])
        q_hi, q_lo, k_hi, k_lo = (ph.sb(k, [P, S], F32R) for k in ("q_hi", "q_lo", "k_hi", "k_lo"))
        q4 = [ph.sb(f"q4_{r}", [P, HG, S], F32R) for r in range(RQ)]
        k4 = [ph.sb(f"k4_{r}", [P, HG, S], F32R) for r in range(RQ)]
        v4 = [ph.sb(f"v4_{r}", [P, TB, P]) for r in range(2)]
        top = ph.sb("top", [P, 2, TB, HG])
        top_hi, top_lo = (ph.sb(k, [HG, S], F32R) for k in ("top_hi", "top_lo"))
        e = [ph.sb(f"e{r}", [P, HG, TB, S]) for r in range(2)]
        e_pair = ph.sb("e_pair", [P, HG, 2, S])
        ones = ph.sb("ones", [P, 32])
        o_sb, l_sb, o_norm = (ph.sb(k, [P, S]) for k in ("o_sb", "l_sb", "o_norm"))
        w_out = ph.sb("w_out", [P, U, DM])
        bias = ph.sb("bias", [P, DM])
        y_sb = ph.sb("y_sb", [P, S])
        sp_settled = ph.sem("sp_settled")
        set_up, w_loaded = ph.sem("set_up"), ph.sem("w_loaded")
        xn_done, xp_ready, xT_done, xT_v_done = (ph.sem(k) for k in ("xn_done", "xp_ready", "xT_done", "xT_v_done"))
        q_ready, q_hi_done, q_lo_done, k_ready, k_hi_done, k_lo_done, v_ready, v_done = (
            ph.sem(k) for k in ("q_ready", "q_hi_done", "q_lo_done", "k_ready", "k_hi_done", "k_lo_done", "v_ready",
                                "v_done"))
        loaded = [ph.sem(f"loaded{r}") for r in range(RQ)]
        row_loaded = [ph.sem(f"row_loaded{r}") for r in range(RQ)]
        s_ready, max_done, tt_ready, hi_done, lo_done, st_ready, exp_done, pair_done, pv_done, o_copied, \
            recip_done, o_done, y_ready, y_copied, yT_ready, y_added, y_stored = (ph.sem(k) for k in (
                "s_ready", "max_done", "tt_ready", "hi_done", "lo_done", "st_ready", "exp_done", "pair_done",
                "pv_done", "o_copied", "recip_done", "o_done", "y_ready", "y_copied", "yT_ready", "y_added",
                "y_stored"))
        S_BANK, ST_BANK, PV_BANK, TURN_BANK, PROJ_BANK, Y_BANK = 0, 2, 4, 5, 6, 7
        RECIP_SLOTS = ((0, 1), (0, 2), (0, 3), (1, 0), (1, 1), (2, 0), (2, 2), (2, 3))
        PART = S // len(RECIP_SLOTS)

        with nc.Block() as block:
            @block.gpsimd
            def _(pool):
                for r in range(RQ):
                    pool.memset(k4[r][KROWS:KROWS + 2].bitcast(F32), 1.0).then_inc(set_up, 1)

                def step(st):
                    if st.has(4):
                        n, r = st.n(4), st.slot(4, 2)
                        for j in range(HG):
                            pool.wait_ge(exp_done, 16 * (n - 1) + 4 * j + 4)
                            if j == 0:
                                wait(pool, pv_done, n - 1)
                            pool.tensor_tensor(e_pair[:, j, :, :], e[r][:, j, 0:2, :], e[r][:, j, 2:4, :], ALU.add
                                               ).then_inc(pair_done, 1)
                    if st.has(5):
                        n = st.n(5)
                        pool.wait_ge(recip_done, len(RECIP_SLOTS) * n)
                        wait(pool, y_ready, n - 1)
                        pool.tensor_tensor(o_norm[:], o_sb[:], l_sb[:], ALU.mult).then_inc(o_done, 1)

                run_steps(pool, NG, 6, step, U=U)

            @block.sync
            def _(sp):
                sp.dma_start(w[:], g.w_qkv).then_inc(w_loaded, 16)
                for k, part in enumerate(g.w_out32):
                    sp.dma_start(w_out[:, k, :], part).then_inc(w_loaded, 16)
                sp.dma_start(bias[:], g.b_out[None, :].to_broadcast([P, DM])).then_inc(w_loaded, 16)

                def step(st):
                    if st.has(0):
                        n, r = st.n(0), st.slot(0, RQ)
                        wait(sp, st_ready, 16 * (n - 4))
                        settle(sp, sp_settled)
                        sp.wait_ge(q_lo_done, n)
                        for row, src in ((0, q_hi), (32, q_hi), (64, q_lo)):
                            sp.dma_start(q4[r][row:row + 32].bitcast(F32), src[:].bitcast(F32)).then_inc(loaded[r], 16)
                    if st.has(2):
                        k = st.slot(2, RQ)
                        sp.wait_ge(lo_done, st.n(2))
                        for row, part in ((KROWS, top_hi), (KROWS + 1, top_lo)):
                            sp.dma_start(q4[k][row:row + 1].bitcast(F32), part[:].bitcast(F32)
                                         ).then_inc(row_loaded[k], 16)
                    if st.has(0):
                        n, r = st.n(0), st.slot(0, RQ)
                        sp.wait_ge(k_lo_done, n)
                        for row, src in ((0, k_hi), (32, k_lo), (64, k_hi)):
                            sp.dma_start(k4[r][row:row + 32].bitcast(F32), src[:].bitcast(F32)).then_inc(loaded[r], 16)

                    if st.has(6) and st.c == 6:
                        sp.wait_ge(y_added, st.i)
                        settle(sp, sp_settled)
                        sp.dma_start(item(g.y_dram, st.i).rearrange("b p n -> p (b n)"),
                                     xn[:].rearrange("p t d -> p (t d)")).then_inc(y_stored, 16)

                run_steps(sp, NG, 6, step, U=U)
                sp.wait_ge(y_stored, 16 * B)

            @block.tensor
            def _(pe):
                pe.wait_ge(set_up, RQ + 1)
                pe.wait_ge(w_loaded, 16 * (U + 2))

                def turn_x(st):
                    pe.wait_ge(xn_done, TB * (st.i + 1))
                    if st.has(4):
                        wait(pe, v_done, st.n(4))
                    for tb in range(TB):
                        ins = pe.transpose(g.ps[:, PROJ_BANK, tb * P:(tb + 1) * P], xn[:, tb, :], g.ident[:])
                    ins.then_inc(xp_ready, 1)

                def project_q(st):
                    if st.c == 1:
                        pe.wait_ge(xT_done, st.i + 1)
                    if st.has(4):
                        wait(pe, v_done, st.n(4))
                    if st.c == 7 and st.has(7):
                        pe.wait_ge(y_added, st.i)
                    pe.matmul(g.ps[:, PROJ_BANK, :], w[:, (st.c - 1) * P:st.c * P], xT[:], start=True, stop=True
                              ).then_inc(q_ready, 1)

                def project_k(st):
                    pe.wait_ge(q_lo_done, st.n(0))
                    pe.matmul(g.ps[:, PROJ_BANK, :], w[:, W + (st.c - 1) * P:W + st.c * P], xT[:], start=True, stop=True
                              ).then_inc(k_ready, 1)

                def project_v(st):
                    group = (st.c - 4) % U
                    if group == 0:
                        pe.wait_ge(xT_v_done, st.i + 1)
                    if st.has(0):
                        pe.wait_ge(k_lo_done, st.n(0))
                    wait(pe, v_done, st.n(4))
                    for tb in range(TB):
                        ins = pe.matmul(g.ps[:, PROJ_BANK, tb * P:(tb + 1) * P], xT_v[:, tb * P:(tb + 1) * P],
                                        w[:, 2 * W + group * P:2 * W + (group + 1) * P], start=True, stop=True)
                    ins.then_inc(v_ready, 1)

                def scores(n, r, j, qb):
                    wait(pe, max_done, 16 * (n - 1) + 4 * j + qb - 1)
                    pe.matmul(g.ps[:, S_BANK + qb % 2, :], q4[r][0:KROWS, j, qb * P:(qb + 1) * P],
                              k4[r][0:KROWS, j, :], start=True, stop=True).then_inc(s_ready, 1)

                def turn_tops(n, t):
                    pe.wait_ge(max_done, 16 * n)
                    wait(pe, o_copied, n - 3)
                    for qb in range(TB):
                        ins = pe.transpose(g.ps[0:HG, TURN_BANK, qb * P:(qb + 1) * P], top[:, t, qb, :], g.ident[:])
                    ins.then_inc(tt_ready, 1)

                def shifted_scores(n, r, j, kb):
                    wait(pe, exp_done, 16 * (n - 1) + 4 * j + kb - 1)
                    pe.matmul(g.ps[:, ST_BANK + kb % 2, :], k4[r][0:KROWS + 2, j, kb * P:(kb + 1) * P],
                              q4[r][0:KROWS + 2, j, :], start=True, stop=True).then_inc(st_ready, 1)

                def product(n, r, kb):
                    if kb == 0:
                        pe.wait_ge(exp_done, 16 * n)
                        pe.wait_ge(v_done, n)
                        wait(pe, o_copied, n - 1)
                    for j in range(HG):
                        pe.matmul(g.ps[32 * j:32 * j + 32, PV_BANK, :], v4[r][:, kb, 32 * j:32 * j + 32],
                                  e[r][:, j, kb, :], start=(kb == 0), stop=(kb == TB - 1))

                def sums(st):
                    pe.wait_ge(pair_done, HG * st.n(4))
                    if st.has(2):
                        pe.wait_ge(lo_done, st.n(2))
                    wait(pe, o_copied, st.n(5))
                    for pair in range(2):
                        for j in range(HG):
                            ins = pe.matmul(g.ps[32 * j:32 * j + 32, TURN_BANK, :], ones[:], e_pair[:, j, pair, :],
                                            start=(pair == 0), stop=(pair == 1))
                    ins.then_inc(pv_done, 1)

                def project_out(st):
                    group = (st.c - 7) % U
                    pe.wait_ge(o_done, st.n(6))
                    if group == 0:
                        wait(pe, y_copied, st.i)
                    pe.matmul(g.ps[:, Y_BANK, :], w_out[:, group, :], o_norm[:], start=(group == 0),
                              stop=(group == U - 1)).then_inc(y_ready, 1)

                def turn_y(st):
                    pe.wait_ge(y_copied, st.i)
                    if st.has(3):
                        pe.wait_ge(v_done, st.n(3))
                    for tb in range(TB):
                        ins = pe.transpose(g.ps[:, PROJ_BANK, tb * P:(tb + 1) * P], y_sb[:, tb * P:(tb + 1) * P],
                                           g.ident[:])
                    ins.then_inc(yT_ready, 1)

                def step(st):
                    if st.has(1):
                        pe.wait_ge(loaded[st.slot(1, RQ)], 16 * 6 * st.use(1, RQ))
                    if st.has(3):
                        pe.wait_ge(row_loaded[st.slot(3, RQ)], 16 * 2 * st.use(3, RQ))
                    for j in range(HG):
                        for b in range(TB):
                            if st.has(1):
                                scores(st.n(1), st.slot(1, RQ), j, b)
                            if st.has(3):
                                shifted_scores(st.n(3), st.slot(3, RQ), j, b)
                            if (j, b) == (0, 1) and st.has(0) and st.c == 1:
                                turn_x(st)
                            if (j, b) == (0, 2) and st.has(6):
                                project_out(st)
                            if (j, b) == (1, 0) and st.has(0):
                                project_q(st)
                            if (j, b) == (1, 1) and st.has(2):
                                turn_tops(st.n(2), st.slot(2, 2))
                            if (j, b) == (1, 3) and st.has(0):
                                project_k(st)
                            if (j, b) == (2, 3) and st.has(3):
                                project_v(st)
                            if (j, b) == (3, 1) and st.has(6) and st.c == 6:
                                turn_y(st)
                            if j + b == 3 and st.has(4):
                                product(st.n(4), st.slot(4, 2), j)
                            if (j, b) == (3, 3) and st.has(4):
                                sums(st)

                run_steps(pe, NG, 6, step, U=U)

            @block.scalar
            def _(act):
                def copy_out(n):
                    act.wait_ge(pv_done, n)
                    wait(act, o_done, n - 1)
                    act.activation(l_sb[:], g.ps[:, TURN_BANK, :], ACT.Copy)
                    act.activation(o_sb[:], g.ps[:, PV_BANK, :], ACT.Copy).then_inc(o_copied, 1)

                def copy_y(st):
                    act.wait_ge(y_ready, U * st.i)
                    wait(act, yT_ready, st.i - 1)
                    act.activation(y_sb[:], g.ps[:, Y_BANK, :], ACT.Copy).then_inc(y_copied, 1)

                def copy_x(st):
                    act.wait_ge(xp_ready, st.i + 1)
                    wait(act, k_ready, st.n(0) - 1)
                    wait(act, xT_v_done, st.i)
                    act.activation(xT[:], g.ps[:, PROJ_BANK, :], ACT.Copy).then_inc(xT_done, 1)

                def copy_x_for_v(st):
                    act.wait_ge(xT_done, st.i + 1)
                    wait(act, v_ready, st.n(4))
                    act.activation(xT_v[:], xT[:], ACT.Copy).then_inc(xT_v_done, 1)

                def high(st, bank, ready, hi, factor, done):
                    act.wait_ge(ready, st.n(0))
                    if st.has(1):
                        act.wait_ge(loaded[st.slot(1, RQ)], 16 * 6 * st.use(1, RQ))
                    act.activation(hi[:], g.ps[:, bank, :], ACT.Copy, scale=factor).then_inc(done, 1)

                def copy_v(st):
                    n, r = st.n(3), st.slot(3, 2)
                    act.wait_ge(v_ready, n)
                    wait(act, pv_done, n - 2)
                    act.activation(v4[r][:], g.ps[:, PROJ_BANK, :].rearrange("p (t c) -> p t c", t=TB), ACT.Copy
                                   ).then_inc(v_done, 1)

                def top_row(st):
                    act.wait_ge(tt_ready, st.n(2))
                    if st.has(3):
                        act.wait_ge(row_loaded[st.slot(3, RQ)], 16 * 2 * st.use(3, RQ))
                    act.activation(top_hi[:], g.ps[0:HG, TURN_BANK, :], ACT.Copy, scale=-1.0).then_inc(hi_done, 1)

                def step(st):
                    for j in range(HG):
                        for b in range(TB):
                            if st.has(3):
                                n, r = st.n(3), st.slot(3, 2)
                                act.wait_ge(st_ready, 16 * (n - 1) + 4 * j + b + 1)
                                if j == 0 and b == 0:
                                    wait(act, pv_done, n - 2)
                                act.activation(e[r][:, j, b, :], g.ps[:, ST_BANK + b % 2, :], ACT.Exp
                                               ).then_inc(exp_done, 1)
                            if (j, b) == (0, 0) and st.has(5):
                                copy_out(st.n(5))
                            if (j, b) == (0, 2) and st.has(0) and st.c == 1:
                                copy_x(st)
                            if (j, b) == (0, 2) and st.has(3) and st.c == 4:
                                copy_x_for_v(st)
                            if (j, b) == (1, 0) and st.has(6) and st.c == 6:
                                copy_y(st)
                            if (j, b) == (1, 1) and st.has(0):
                                high(st, PROJ_BANK, q_ready, q_hi, scale, q_hi_done)
                            if (j, b) == (1, 2) and st.has(2):
                                top_row(st)
                            if (j, b) == (2, 0) and st.has(0):
                                high(st, PROJ_BANK, k_ready, k_hi, 1.0, k_hi_done)
                            if (j, b) == (3, 0) and st.has(3):
                                copy_v(st)

                run_steps(act, NG, 6, step, U=U)

            @block.vector
            def _(dve):
                def recip(n, k):
                    dve.wait_ge(o_copied, n)
                    part = l_sb[:, k * PART:(k + 1) * PART]
                    dve.reciprocal(part, part).then_inc(recip_done, 1)

                def add_bias(st):
                    dve.wait_ge(yT_ready, st.i)
                    dve.wait_ge(xp_ready, st.i + 1 if st.has(0) else B)
                    dve.tensor_tensor(xn[:], g.ps[:, PROJ_BANK, :].rearrange("p (t d) -> p t d", t=TB),
                                      bias[:, None, :].to_broadcast([P, TB, DM]), ALU.add).then_inc(y_added, 1)

                def low(st, bank, hi_done, hi, lo, factor, done):
                    dve.wait_ge(hi_done, st.n(0))
                    if st.has(1):
                        dve.wait_ge(loaded[st.slot(1, RQ)], 16 * 6 * st.use(1, RQ))
                    dve.scalar_tensor_tensor(lo[:], g.ps[:, bank, :], factor, hi[:].bitcast(F32), ALU.mult,
                                             ALU.subtract).then_inc(done, 1)

                def low_top(st):
                    dve.wait_ge(hi_done, st.n(2))
                    if st.has(3):
                        dve.wait_ge(row_loaded[st.slot(3, RQ)], 16 * 2 * st.use(3, RQ))
                    dve.scalar_tensor_tensor(top_lo[:], g.ps[0:HG, TURN_BANK, :], -1.0, top_hi[:].bitcast(F32),
                                             ALU.mult, ALU.subtract).then_inc(lo_done, 1)

                dve.memset(ones[:], 1.0).then_inc(set_up, 1)
                dve.wait_ge(w_loaded, 16 * (U + 2))

                def step(st):
                    if st.has(0) and st.c == 1:
                        wait(dve, xp_ready, st.i)
                        wait(dve, y_stored, 16 * (st.i - 1))
                        normalise(dve, g.x_all, g.mean_var, g.rstd, st.i + 1, xn, xn_done)
                    for j in range(HG):
                        for qb in range(TB):
                            if st.has(1):
                                n, t = st.n(1), st.slot(1, 2)
                                if j == 0 and qb == 0:
                                    wait(dve, tt_ready, n - 2)
                                dve.wait_ge(s_ready, 16 * (n - 1) + 4 * j + qb + 1)
                                dve.tensor_reduce(top[:, t, qb, j:j + 1], g.ps[:, S_BANK + qb % 2, :], AX_X, ALU.max
                                                  ).then_inc(max_done, 1)
                            if (j, qb) in RECIP_SLOTS and st.has(5):
                                recip(st.n(5), RECIP_SLOTS.index((j, qb)))
                            if (j, qb) == (3, 2) and st.has(6) and st.c == 6:
                                add_bias(st)
                            if (j, qb) == (1, 2) and st.has(0):
                                low(st, PROJ_BANK, q_hi_done, q_hi, q_lo, scale, q_lo_done)
                            if (j, qb) == (1, 3) and st.has(2):
                                low_top(st)
                            if (j, qb) == (2, 1) and st.has(0):
                                low(st, PROJ_BANK, k_hi_done, k_hi, k_lo, 1.0, k_lo_done)

                run_steps(dve, NG, 6, step, U=U)


BIAS_LINE = 1024


def bias_lines(nc, g, name, coeffs_t, line_table, wpos_t, flip):
    with Phase(nc, name) as ph:
        taps = ph.sb("taps", [101, 4])
        table = ph.sb("table", [101, BIAS_LINE])
        wp = ph.sb("wp", [4, 16])
        resp = ph.sb("resp", [4, BIAS_LINE])
        lines = ph.sb("lines", [16, BIAS_LINE])
        loaded, mm, copied, line_stored = (ph.sem(k) for k in ("loaded", "mm", "copied", "line_stored"))
        with nc.Block() as block:
            @block.sync
            def _(sp):
                for dst, src in ((taps, coeffs_t), (table, line_table), (wp, wpos_t)):
                    sp.dma_start(dst[:], src).then_inc(loaded, 16)
                sp.dma_start(g.flip[:], flip).then_inc(line_stored, 16)
                sp.wait_ge(copied, 4)
                sp.dma_start(g.lines, lines[:]).then_inc(line_stored, 16)
                sp.wait_ge(line_stored, 32)

            @block.tensor
            def _(pe):
                pe.wait_ge(loaded, 48)
                for k in range(2):
                    pe.matmul(g.ps[0:4, k, :], taps[:], table[:, k * 512:(k + 1) * 512], start=True, stop=True
                              ).then_inc(mm, 1)
                for k in range(2):
                    pe.wait_ge(copied, k + 1)
                    pe.matmul(g.ps[0:16, 2 + k, :], wp[:], resp[:, k * 512:(k + 1) * 512], start=True, stop=True
                              ).then_inc(mm, 1)

            @block.vector
            def _(dve):
                for k in range(2):
                    dve.wait_ge(mm, k + 1)
                    dve.tensor_copy(resp[:, k * 512:(k + 1) * 512], g.ps[0:4, k, :]).then_inc(copied, 1)
                for k in range(2):
                    dve.wait_ge(mm, 2 + k + 1)
                    dve.tensor_copy(lines[:, k * 512:(k + 1) * 512], g.ps[0:16, 2 + k, :]).then_inc(copied, 1)


class Marks:

    def __init__(self, ph, name, steps):
        self.sem, self.steps = ph.sem(name), steps.split()

    def at(self, n, step):
        return len(self.steps) * (n - 1) + self.steps.index(step) + 1


def linear_attention(nc, g, name, d):
    NP = 12
    Q, QS, K, KS, B0, B1, ZA, ZB, V0 = range(9)
    HM = 64
    with Phase(nc, name) as ph:
        w = ph.sb("w", [P, NP, P])
        w_out = ph.sb("w_out", [P, DM])
        bout = ph.sb("bout", [P, DM])
        bias = ph.sb("bias", [P, 4])
        rope = ph.sb("rope", [P, 2, S])
        to_c = ph.sb("to_c", [P, 4, P])
        to_m = ph.sb("to_m", [P, 2, HM])
        from_m = ph.sb("from_m", [P, 2, P])
        xn, xn2, xnb = (ph.sb(k, [P, TB, DM]) for k in ("xn", "xn2", "xnb"))
        xT = [ph.sb(f"xT{r}", [P, S]) for r in range(2)]
        u = ph.sb("u", [P, 2, 2, S])
        rot = ph.sb("rot", [P, 2, S])
        low = ph.sb("low", [P, 2, S])
        phi = ph.sb("phi", [P, 2, S])
        beta = ph.sb("beta", [P, 2, S])
        kv = ph.sb("kv", [P, 4, S])
        z = ph.sb("z", [HM, 2, S])
        zmax = ph.sb("zmax", [HM, S])
        zexp = [ph.sb(f"zexp{r}", [HM, 2, S]) for r in range(2)]
        zsum = [ph.sb(f"zsum{r}", [HM, S]) for r in range(2)]
        state = ph.sb("state", [P, 10, S])
        prod = ph.sb("prod", [P, 10, S])
        den = ph.sb("den", [HM, S])
        coef = ph.sb("coef", [P, S])
        cb = ph.sb("cb", [P, 2, S])
        y2 = ph.sb("y2", [P, 2, S])
        yT = ph.sb("yT", [P, S])
        y_tok = [ph.sb(f"y_tok{r}", [P, TB, DM]) for r in range(2)]
        y_stored = [ph.sem(f"y_stored{r}") for r in range(2)]
        loaded, zeroed, sp_settled = ph.sem("loaded"), ph.sem("zeroed"), ph.sem("sp_settled")
        xn_done, xp_ready, xT_done = ph.sem("xn_done"), ph.sem("xp_ready"), ph.sem("xT_done")
        proj_ready = ph.sem("proj_ready")
        va = Marks(ph, "vec_rotate_scan", "cq sq ck sk rq rk lq lk tq tk phi_q phi_k kv0 kv1 kv2 kv3 beta0 beta1 zmax "
                                          "s0 s1 s2 s3 s4 s5 s6 s7 s8 s9 p7 p8 p9")
        vb = Marks(ph, "vec_finish", "den recip coef y0 y1 y z")
        xn2_done = ph.sem("xn2_done")
        aa = Marks(ph, "act_features", "eq ek beta0 beta1 za zb zexp")
        ab = Marks(ph, "act_coef", "cb0 cb1")
        pa = Marks(ph, "pool_products", "zsub p0 p1 zsum p2 p3 p4 p5 p6")
        pool_xnb = ph.sem("pool_xnb")
        ta = Marks(ph, "pe_sums", "m0 m1 m2 m3 m4 m5 m6 m7 m8 m9")
        tb_ = Marks(ph, "pe_finish", "cb0 cb1 out")
        T_BANK, R_BANK, NUM_BANK, DEN_BANK = 0, 1, 5, 7
        ON_POOL = 7
        scans = [(0, None), (1, None)] + [(m, c) for m in range(2) for c in range(4)]

        with nc.Block() as block:
            @block.sync
            def _(sp):
                for dst, src in ((w[:], d["w"]), (w_out[:], d["w_out"]), (bias[:], d["bias"]),
                                 (rope[:], d["rope"]), (to_c[:], d["to_c"]), (to_m[:], d["to_m"]),
                                 (from_m[:], d["from_m"]), (bout[:], d["bout"][None, :].to_broadcast([P, DM]))):
                    sp.dma_start(dst, src).then_inc(loaded, 16)

                def step(st):
                    if st.has(2):
                        r = st.slot(2, 2)
                        sp.wait_ge(vb.sem, vb.at(st.n(2), "z"))
                        settle(sp, sp_settled)
                        sp.dma_start(item(g.y_dram, st.n(2)).rearrange("b p n -> p (b n)"),
                                     y_tok[r][:].rearrange("p t d -> p (t d)")).then_inc(y_stored[r], 16)

                run_steps(sp, B, 3, step, U=2)
                for r in range(2):
                    sp.wait_ge(y_stored[r], 16 * B // 2)

            @block.tensor
            def _(pe):
                pe.wait_ge(loaded, 16 * 8)
                pe.wait_ge(zeroed, 1)

                def project(st, k, pieces):
                    n, r = st.n(k), st.slot(k, 2)
                    for m in pieces:
                        if m < 4:
                            wait(pe, va.sem, va.at(n - 1, f"kv{m}"))
                        elif m < 8:
                            pe.wait_ge(va.sem, va.at(n, ("cq", "sq", "ck", "sk")[m - 4]))
                        else:
                            pe.wait_ge(aa.sem, aa.at(n, ("beta0", "beta1", "za", "zb")[m - 8]))
                        rows = HM if m in (ZA, ZB) else P
                        pe.matmul(g.ps[0:rows, R_BANK + m % 4, :], w[:, m, 0:rows], xT[r][:], start=True, stop=True
                                  ).then_inc(proj_ready, 1)

                def step(st):
                    if st.has(0):
                        n = st.n(0)
                        pe.wait_ge(xn_done, TB * n)
                        if st.has(3):
                            wait(pe, vb.sem, vb.at(st.n(3), "z"))
                        for tb in range(TB):
                            ins = pe.transpose(g.ps[:, T_BANK, tb * P:(tb + 1) * P], xn[:, tb, :], g.ident[:])
                        ins.then_inc(xp_ready, 1)
                    if st.has(2):
                        pe.wait_ge(vb.sem, vb.at(st.n(2), "coef"))
                        pe.matmul(g.ps[:, DEN_BANK, :], from_m[:, 0, :], coef[:], start=True, stop=True
                                  ).then_inc(tb_.sem, 1)
                    if st.has(1):
                        project(st, 1, (B0, B1))
                    if st.has(2):
                        pe.wait_ge(ab.sem, ab.at(st.n(2), "cb0"))
                        pe.matmul(g.ps[:, DEN_BANK, :], from_m[:, 1, :], coef[:], start=True, stop=True
                                  ).then_inc(tb_.sem, 1)
                    if st.has(1):
                        project(st, 1, range(ZA, NP))
                    if st.has(2):
                        n = st.n(2)
                        pe.wait_ge(vb.sem, vb.at(n, "y"))
                        pe.wait_ge(xT_done, st.n(0) if st.has(0) else B)
                        wait(pe, vb.sem, vb.at(n - 1, "z"))
                        for tb in range(TB):
                            ins = pe.matmul(g.ps[:, T_BANK, tb * P:(tb + 1) * P], yT[:, tb * P:(tb + 1) * P], w_out[:],
                                            start=True, stop=True)
                        ins.then_inc(tb_.sem, 1)
                    if st.has(0):
                        pe.wait_ge(xT_done, st.n(0))
                        project(st, 0, range(Q, KS + 1))
                    if st.has(1):
                        n = st.n(1)
                        for i, (m, c) in enumerate(scans):
                            marks = pa if i < ON_POOL else va
                            pe.wait_ge(marks.sem, marks.at(n, f"p{i}"))
                            if i == 0 and st.has(2):
                                pe.wait_ge(ab.sem, ab.at(st.n(2), "cb1"))
                            if i == 2 and st.has(2):
                                pe.wait_ge(vb.sem, vb.at(st.n(2), "y1"))
                            if c is None:
                                pe.matmul(g.ps[0:HM, DEN_BANK, :], to_m[:, m, :], prod[:, i, :], start=(m == 0),
                                          stop=(m == 1)).then_inc(ta.sem, 1)
                            else:
                                pe.matmul(g.ps[:, NUM_BANK + m, :], to_c[:, c, :], prod[:, i, :], start=(c == 0),
                                          stop=(c == 3)).then_inc(ta.sem, 1)

                run_steps(pe, B, 3, step, U=2)

            @block.scalar
            def _(act):
                act.wait_ge(loaded, 16 * 8)

                def bank(m):
                    return g.ps[0:HM if m in (ZA, ZB) else P, R_BANK + m % 4, :]

                def step(st):
                    if st.has(0):
                        n = st.n(0)
                        act.wait_ge(xp_ready, n)
                        wait(act, proj_ready, NP * (n - 2))
                        act.activation(xT[st.slot(0, 2)][:], g.ps[:, T_BANK, :], ACT.Copy).then_inc(xT_done, 1)
                    if st.has(2):
                        act.wait_ge(tb_.sem, tb_.at(st.n(2), "cb0"))
                        wait(act, vb.sem, vb.at(st.n(2) - 1, "y0"))
                        act.activation(cb[:, 0, :], g.ps[:, DEN_BANK, :], ACT.Copy).then_inc(ab.sem, 1)
                    if st.has(1):
                        n = st.n(1)
                        for k in range(2):
                            act.wait_ge(va.sem, va.at(n, ("lq", "lk")[k]))
                            act.activation(low[:, k, :], low[:, k, :], ACT.Exp).then_inc(aa.sem, 1)
                    if st.has(1):
                        n = st.n(1)
                        wait(act, va.sem, va.at(n - 1, "s9"))
                        for k in range(2):
                            act.wait_ge(proj_ready, NP * (n - 1) + B0 + k + 1)
                            act.activation(beta[:, k, :], bank(B0 + k), ACT.Sigmoid, bias=bias[:, k:k + 1]
                                           ).then_inc(aa.sem, 1)
                    if st.has(2):
                        act.wait_ge(tb_.sem, tb_.at(st.n(2), "cb1"))
                        wait(act, vb.sem, vb.at(st.n(2) - 1, "y1"))
                        act.activation(cb[:, 1, :], g.ps[:, DEN_BANK, :], ACT.Copy).then_inc(ab.sem, 1)
                    if st.has(1):
                        n = st.n(1)
                        for k in range(2):
                            act.wait_ge(proj_ready, NP * (n - 1) + ZA + k + 1)
                            if k == 0:
                                wait(act, aa.sem, aa.at(n - 1, "zexp"))
                            act.activation(z[:, k, :], bank(ZA + k), ACT.Identity, bias=bias[0:HM, 2 + k:3 + k]
                                           ).then_inc(aa.sem, 1)
                        act.wait_ge(pa.sem, pa.at(n, "zsub"))
                        if st.has(3):
                            act.wait_ge(vb.sem, vb.at(st.n(3), "coef"))
                        act.activation(zexp[st.slot(1, 2)][:], z[:], ACT.Exp).then_inc(aa.sem, 1)

                run_steps(act, B, 3, step, U=2)

            @block.gpsimd
            def _(pool):
                pool.wait_ge(loaded, 16 * 8)

                def step(st):
                    if st.has(1):
                        n, r = st.n(1), st.slot(1, 2)
                        pool.wait_ge(va.sem, va.at(n, "zmax"))
                        pool.tensor_tensor(z[:], z[:], zmax[:, None, :].to_broadcast([HM, 2, S]), ALU.subtract
                                           ).then_inc(pa.sem, 1)
                        if st.has(2):
                            pool.wait_ge(xn2_done, TB * st.n(2))
                            wait(pool, vb.sem, vb.at(st.n(2) - 1, "z"))
                            pool.tensor_tensor(xnb[:], xn2[:], bout[:, None, :].to_broadcast([P, TB, DM]), ALU.add
                                               ).then_inc(pool_xnb, 1)
                        for i in range(ON_POOL):
                            if i == 2:
                                pool.wait_ge(aa.sem, aa.at(n, "zexp"))
                                if st.has(3):
                                    pool.wait_ge(vb.sem, vb.at(st.n(3), "den"))
                                pool.tensor_tensor(zsum[r][:], zexp[r][:, 0, :], zexp[r][:, 1, :], ALU.add
                                                   ).then_inc(pa.sem, 1)
                            pool.wait_ge(va.sem, va.at(n, f"s{i}"))
                            wait(pool, ta.sem, ta.at(n - 1, f"m{i}"))
                            pool.tensor_tensor(prod[:, i, :], state[:, i, :], phi[:, 0, :], ALU.mult
                                               ).then_inc(pa.sem, 1)
                    if st.has(2) and not st.has(1):
                        n = st.n(2)
                        pool.wait_ge(xn2_done, TB * n)
                        wait(pool, vb.sem, vb.at(n - 1, "z"))
                        pool.tensor_tensor(xnb[:], xn2[:], bout[:, None, :].to_broadcast([P, TB, DM]), ALU.add
                                           ).then_inc(pool_xnb, 1)

                run_steps(pool, B, 3, step, U=2)

            @block.vector
            def _(dve):
                dve.memset(coef[:], 0.0).then_inc(zeroed, 1)
                dve.wait_ge(loaded, 16 * 8)
                dve.wait_ge(zeroed, 1)

                def bank(m):
                    return g.ps[:, R_BANK + m % 4, :]

                def done(ins, marks):
                    ins.then_inc(marks.sem, 1)

                def step(st):
                    if st.has(0):
                        wait(dve, xp_ready, st.n(0) - 1)
                        normalise(dve, g.x_all, g.mean_var, g.rstd, st.n(0), xn, xn_done)
                    if st.has(2):
                        n, r = st.n(2), st.slot(2, 2)
                        dve.wait_ge(ta.sem, ta.at(n, "m1"))
                        dve.wait_ge(pa.sem, pa.at(n, "zsum"))
                        wait(dve, tb_.sem, tb_.at(n - 1, "cb1"))
                        dve.scalar_tensor_tensor(den[:], g.ps[0:HM, DEN_BANK, :], 1e-6, zsum[r][:], ALU.add, ALU.mult
                                                 ).then_inc(vb.sem, 1)
                        dve.wait_ge(vb.sem, vb.at(n, "den"))
                        dve.reciprocal(den[:], den[:]).then_inc(vb.sem, 1)
                        dve.wait_ge(vb.sem, vb.at(n, "recip"))
                        dve.tensor_tensor(coef[0:HM, :], den[:], zexp[r][:, 0, :], ALU.mult).then_inc(vb.sem, 1)
                    if st.has(1):
                        n = st.n(1)
                        wait(dve, va.sem, va.at(n - 1, "s9"))
                        for k in range(2):
                            for t in range(2):
                                dve.wait_ge(proj_ready, NP * (n - 1) + 2 * k + t + 1)
                                dve.tensor_tensor(u[:, k, t, :], bank(2 * k + t), rope[:, t, :], ALU.mult
                                                  ).then_inc(va.sem, 1)
                        for k in range(2):
                            dve.wait_ge(va.sem, va.at(n, ("sq", "sk")[k]))
                            dve.tensor_tensor(rot[:, k, :], u[:, k, 0, :], u[:, k, 1, :], ALU.add).then_inc(va.sem, 1)
                        for k in range(2):
                            dve.wait_ge(va.sem, va.at(n, ("rq", "rk")[k]))
                            dve.tensor_scalar(low[:, k, :], rot[:, k, :], 0.0, None, ALU.min).then_inc(va.sem, 1)
                    if st.has(1):
                        n = st.n(1)
                        for k in range(2):
                            dve.wait_ge(aa.sem, aa.at(n, ("eq", "ek")[k]))
                            dve.tensor_scalar(low[:, k, :], low[:, k, :], -1.0, 1.0, ALU.add, ALU.add
                                              ).then_inc(va.sem, 1)
                        wait(dve, pa.sem, pa.at(n - 1, "p6"))
                        wait(dve, va.sem, va.at(n - 1, "p9"))
                        for k in range(2):
                            dve.wait_ge(va.sem, va.at(n, ("tq", "tk")[k]))
                            dve.scalar_tensor_tensor(phi[:, k, :], rot[:, k, :], 0.0, low[:, k, :], ALU.max, ALU.add
                                                     ).then_inc(va.sem, 1)
                        dve.wait_ge(va.sem, va.at(n, "phi_k"))
                        for c in range(4):
                            dve.wait_ge(proj_ready, NP * (n - 1) + V0 + c + 1)
                            dve.tensor_tensor(kv[:, c, :], bank(V0 + c), phi[:, 1, :], ALU.mult).then_inc(va.sem, 1)
                        for m in range(2):
                            dve.wait_ge(aa.sem, aa.at(n, ("beta0", "beta1")[m]))
                            dve.tensor_scalar(beta[:, m, :], beta[:, m, :], 0.85, 0.9995, ALU.max, ALU.min
                                              ).then_inc(va.sem, 1)
                        dve.wait_ge(aa.sem, aa.at(n, "zb"))
                        wait(dve, pa.sem, pa.at(n - 1, "zsub"))
                        dve.tensor_tensor(zmax[:], z[:, 0, :], z[:, 1, :], ALU.max).then_inc(va.sem, 1)
                    if st.has(2):
                        n = st.n(2)
                        dve.wait_ge(ta.sem, ta.at(n, "m9"))
                        wait(dve, tb_.sem, tb_.at(n - 1, "out"))
                        for m in range(2):
                            dve.wait_ge(ab.sem, ab.at(n, ("cb0", "cb1")[m]))
                            dve.tensor_tensor(y2[:, m, :], g.ps[:, NUM_BANK + m, :], cb[:, m, :], ALU.mult
                                              ).then_inc(vb.sem, 1)
                        dve.wait_ge(vb.sem, vb.at(n, "y1"))
                        dve.tensor_tensor(yT[:], y2[:, 0, :], y2[:, 1, :], ALU.add).then_inc(vb.sem, 1)
                        wait(dve, pool_xnb, n - 1)
                        normalise(dve, g.x_all, g.mean_var, g.rstd, n, xn2, xn2_done)
                    if st.has(1):
                        n = st.n(1)
                        dve.wait_ge(va.sem, va.at(n, "beta1"))
                        for i, (m, c) in enumerate(scans):
                            dve.tensor_tensor_scan(state[:, i, :], beta[:, m, :],
                                                   phi[:, 1, :] if c is None else kv[:, c, :], 0.0, ALU.mult, ALU.add
                                                   ).then_inc(va.sem, 1)
                        for i in range(ON_POOL, 10):
                            dve.wait_ge(va.sem, va.at(n, f"s{i}"))
                            wait(dve, ta.sem, ta.at(n - 1, f"m{i}"))
                            dve.tensor_tensor(prod[:, i, :], state[:, i, :], phi[:, 0, :], ALU.mult
                                              ).then_inc(va.sem, 1)
                    if st.has(2):
                        n = st.n(2)
                        dve.wait_ge(tb_.sem, tb_.at(n, "out"))
                        dve.wait_ge(pool_xnb, n)
                        wait(dve, y_stored[st.slot(2, 2)], 16 * (st.use(2, 2) - 1))
                        dve.tensor_tensor(y_tok[st.slot(2, 2)][:], g.ps[:, T_BANK, :].rearrange("p (t d) -> p t d", t=TB),
                                          xnb[:], ALU.add).then_inc(vb.sem, 1)

                run_steps(dve, B, 3, step, U=2)


def project_out(nc, g, name, w_out):
    with Phase(nc, name) as ph:
        w = ph.sb("w", [P, DM])
        o = [ph.sb(f"o{r}", [P, TB, P]) for r in range(2)]
        oT = [ph.sb(f"oT{r}", [P, S]) for r in range(2)]
        yT = [ph.sb(f"yT{r}", [P, S]) for r in range(2)]
        w_loaded = ph.sem("w_loaded")
        loaded = [ph.sem(f"loaded{r}") for r in range(2)]
        t_ready, t_read, mm_done, y_copied, yt_ready, added = (
            ph.sem(k) for k in ("t_ready", "t_read", "mm_done", "y_copied", "yt_ready", "added"))
        T_BANK, Y_BANK, YT_BANK = 0, 2, 4
        PIECES = 4
        width = P // PIECES

        with nc.Block() as block:
            @block.sync
            def _(sp):
                sp.dma_start(w[:], w_out).then_inc(w_loaded, 16)

                def step(st):
                    n, r = st.n(0), st.slot(0, 2)
                    wait(sp, t_ready, n - 2)
                    for k in range(PIECES):
                        sp.dma_start(o[r][:, :, k * width:(k + 1) * width],
                                     g.o8[bass.ds((n - 1) * PIECES + k, 1)].rearrange("a t p c -> p (a t) c")
                                     ).then_inc(loaded[r], 16)

                run_steps(sp, B, 0, step, U=2)

            @block.tensor
            def _(pe):
                pe.wait_ge(w_loaded, 16)

                def step(st):
                    if st.has(0):
                        n, r = st.n(0), st.slot(0, 2)
                        pe.wait_ge(loaded[r], 16 * PIECES * st.use(0, 2))
                        wait(pe, t_read, n - 2)
                        for tb in range(TB):
                            ins = pe.transpose(g.ps[:, T_BANK + r, tb * P:(tb + 1) * P], o[r][:, tb, :], g.ident[:])
                        ins.then_inc(t_ready, 1)
                    if st.has(1):
                        n, r = st.n(1), st.slot(1, 2)
                        pe.wait_ge(t_read, n)
                        wait(pe, y_copied, n - 2)
                        pe.matmul(g.ps[:, Y_BANK + r, :], w[:], oT[r][:], start=True, stop=True).then_inc(mm_done, 1)
                    if st.has(2):
                        n, r = st.n(2), st.slot(2, 2)
                        pe.wait_ge(y_copied, n)
                        wait(pe, added, n - 2)
                        for tb in range(TB):
                            ins = pe.transpose(g.ps[:, YT_BANK + r, tb * P:(tb + 1) * P],
                                               yT[r][:, tb * P:(tb + 1) * P], g.ident[:])
                        ins.then_inc(yt_ready, 1)

                run_steps(pe, B, 3, step, U=2)

            @block.scalar
            def _(act):
                def step(st):
                    if st.has(0):
                        n, r = st.n(0), st.slot(0, 2)
                        act.wait_ge(t_ready, n)
                        wait(act, mm_done, n - 2)
                        act.activation(oT[r][:], g.ps[:, T_BANK + r, :], ACT.Copy).then_inc(t_read, 1)
                    if st.has(1):
                        n, r = st.n(1), st.slot(1, 2)
                        act.wait_ge(mm_done, n)
                        wait(act, yt_ready, n - 2)
                        act.activation(yT[r][:], g.ps[:, Y_BANK + r, :], ACT.Copy).then_inc(y_copied, 1)

                run_steps(act, B, 3, step, U=2)

            @block.vector
            def _(dve):
                def step(st):
                    n, r = st.n(0), st.slot(0, 2)
                    dve.wait_ge(yt_ready, n)
                    x = batch_of(g.x_all, n)
                    dve.tensor_tensor(x, g.ps[:, YT_BANK + r, :].rearrange("p (t d) -> p t d", t=TB), x, ALU.add
                                      ).then_inc(added, 1)

                run_steps(dve, B, 0, step, U=2)


def add_normalised(nc, g, name, source, gamma, beta, eps):
    with Phase(nc, name) as ph:
        gb = ph.sb("gb", [P, 2, DM])
        y = ph.sb("y", [P, TILES, DM])
        yn = ph.sb("yn", [P, 2, TB, DM])
        stats = ph.sb("stats", [P, TILES, 6])
        t = ph.sb("t", [P, TILES])
        var = ph.sb("var", [P, TILES])
        y_loaded = [ph.sem(f"y_loaded{b}") for b in range(B)]
        loaded, stats_done, aggr_done, chain = (ph.sem(k) for k in ("loaded", "stats_done", "aggr_done", "chain"))
        scaled, shifted, added = (ph.sem(k) for k in ("scaled", "shifted", "added"))
        with nc.Block() as block:
            @block.sync
            def _(sp):
                for b in range(B):
                    sp.dma_start(y[:, b * TB:(b + 1) * TB, :].rearrange("p t d -> p (t d)"), source[b]
                                 ).then_inc(y_loaded[b], 16)
                for k, src in enumerate((gamma, beta)):
                    sp.dma_start(gb[:, k, :], src[None, :].to_broadcast([P, DM])).then_inc(loaded, 16)

            @block.vector
            def _(dve):
                for tile in range(TILES):
                    if tile % TB == 0:
                        dve.wait_ge(y_loaded[tile // TB], 16)
                    dve.bn_stats(stats[:, tile, :], y[:, tile, :]).then_inc(stats_done, 1)
                dve.wait_ge(stats_done, TILES)
                for tile in range(TILES):
                    dve.bn_aggr(g.mean_var[:, tile, :], stats[:, tile, :]).then_inc(aggr_done, 1)
                dve.wait_ge(aggr_done, TILES)
                link = Link(dve, chain, 1, RSQRT_LINKS + 1)
                link(dve.tensor_copy(var[:], g.mean_var[:, :, 1]))
                rsqrt(dve, link, var[:], eps, g.rstd[:], t[:])
                dve.wait_ge(loaded, 32)
                for b in range(B + 1):
                    if b < B:
                        for tile in range(b * TB, (b + 1) * TB):
                            if tile % TB == 0:
                                wait(dve, added, b - 1)
                            dve.scalar_tensor_tensor(yn[:, b % 2, tile % TB, :], y[:, tile, :],
                                                     g.mean_var[:, tile, 0:1], gb[:, 0, :], ALU.subtract, ALU.mult
                                                     ).then_inc(scaled, 1)
                    if 1 <= b <= B:
                        dve.wait_ge(scaled, TB * b)
                        for tile in range((b - 1) * TB, b * TB):
                            v = yn[:, (b - 1) % 2, tile % TB, :]
                            dve.scalar_tensor_tensor(v, v, g.rstd[:, tile:tile + 1], gb[:, 1, :], ALU.mult, ALU.add
                                                     ).then_inc(shifted, 1)
                        dve.wait_ge(shifted, TB * b)
                        x = g.x_all[:, (b - 1) * TB:b * TB, :]
                        dve.tensor_tensor(x, x, yn[:, (b - 1) % 2, :, :], ALU.add).then_inc(added, 1)


def swiglu(nc, g, name, packed, E, C, stats, router=None):
    EC = E * C
    W = 3 * C * P
    quant = packed.dtype == I32
    routed = E - 1
    OUT_LAG, OUT_AT = (2, 5) if E > 1 else (3, 0)
    DOWN_LAG = 3 if routed else 2
    X_AT = EC // 3
    with Phase(nc, name) as ph:
        stage = ph.sb("stage", [P, 2, W], I32 if quant else F32)
        stage_f = ph.sb("stage_f", [P, 2, W]) if quant else stage
        w_hi = ph.sb("w_hi", [P, E, W], F32R)
        w_lo = ph.sb("w_lo", [P, E, W], F32R)
        xn = ph.sb("xn", [P, TB, DM])
        xT = ph.sb("xT", [P, S])
        x_hi = [ph.sb(f"x_hi{r}", [P, S], F32R) for r in range(2)]
        x_lo = [ph.sb(f"x_lo{r}", [P, S], F32R) for r in range(2)]
        gate = ph.sb("gate", [P, 2, S])
        h = ph.sb("h", [P, C, S])
        h_hi = ph.sb("h_hi", [P, C, S], F32R)
        h_lo = ph.sb("h_lo", [P, C, S], F32R)
        acc = ph.sb("acc", [P, S])
        stage_loaded = [ph.sem(f"stage_loaded{k}") for k in range(2)]
        dequant_done, w_hi_done, w_done = ph.sem("dequant_done"), ph.sem("w_hi_done"), ph.sem("w_done")
        xn_done, xp_ready, xT_done, x_hi_done, x_lo_done = (
            ph.sem(k) for k in ("xn_done", "xp_ready", "xT_done", "x_hi_done", "x_lo_done"))
        gu_ready, gate_done, h_done, h_hi_done, h_lo_done, down_done, d_ready, d_read, acc_done = (
            ph.sem(k) for k in ("gu_ready", "gate_done", "h_done", "h_hi_done", "h_lo_done", "down_done", "d_ready",
                                "d_read", "acc_done"))
        out_ready, out_added = ph.sem("out_ready"), ph.sem("out_added")
        stats_done, stats_settled = ph.sem("stats_done"), ph.sem("stats_settled")
        if routed:
            rw = ph.sb("rw", [P, routed])
            lower = ph.sb("lower", [P, routed, routed])
            comb = [ph.sb(f"comb{r}", [P, TB, routed]) for r in range(2)]
            mx, sm = ph.sb("mx", [P, TB]), ph.sb("sm", [P, TB])
            pr, sel = ph.sb("pr", [P, TB, routed]), ph.sb("sel", [P, TB, routed])
            gt, eq = (ph.sb(k, [P, TB, routed, routed]) for k in ("gt", "eq"))
            cw = ph.sb("cw", [P, 2, S])
            part = ph.sb("part", [P, S])
            small_loaded, lg_ready, shifted, p_exp, comb_done, cw_ready, cw_done, chain = (
                ph.sem(k) for k in ("small_loaded", "lg_ready", "shifted", "p_exp", "comb_done", "cw_ready",
                                    "cw_done", "chain"))
            recip_done = ph.sem("recip_done")
        T_BANK, R_BANK, G_BANK, U_BANK, D_BANK = 0, 1, 2, 4, 6
        LG_AT, COMB_AT = X_AT + 3, X_AT + 4

        def position(st, k, q):
            return EC * (st.n(k) - 1) + q + 1, (EC * (st.c - k - 1) + q) % 2

        with nc.Block() as block:
            @block.sync
            def _(sp):
                if routed:
                    sp.dma_start(rw[:], router[0]).then_inc(small_loaded, 16)
                    sp.dma_start(lower[:], router[1][None, :, :].to_broadcast([P, routed, routed])
                                 ).then_inc(small_loaded, 16)
                for e in range(E):
                    wait(sp, w_done, e - 1)
                    sp.dma_start(stage[:, e % 2, :], packed[e]).then_inc(stage_loaded[e % 2], 16)

            @block.tensor
            def _(pe):
                def three(bank, w0, cols, hi, lo, start, stop):
                    pe.matmul(bank, w_hi[:, w0, cols], hi, start=start, stop=False)
                    pe.matmul(bank, w_lo[:, w0, cols], hi, start=False, stop=False)
                    return pe.matmul(bank, w_hi[:, w0, cols], lo, start=False, stop=stop)

                def gate_up(st, q):
                    e, c = divmod(q, C)
                    m, par = position(st, 1, q)
                    r = st.slot(1, 2)
                    wait(pe, gate_done, m - 2)
                    wait(pe, h_done, m - 2)
                    three(g.ps[:, G_BANK + par, :], e, slice(c * P, (c + 1) * P), x_hi[r][:], x_lo[r][:], True, True)
                    three(g.ps[:, U_BANK + par, :], e, slice((C + c) * P, (C + c + 1) * P), x_hi[r][:], x_lo[r][:],
                          True, True).then_inc(gu_ready, 1)

                def down(st, k, q):
                    e, c = divmod(q, C)
                    m, _ = position(st, k, q)
                    bank = g.ps[:, D_BANK + (E * (st.c - k - 1) + e) % 2, :]
                    pe.wait_ge(h_lo_done, m)
                    if c == 0:
                        wait(pe, d_read, E * (st.n(k) - 1) + e - 1)
                    ins = three(bank, e, slice((2 * C + c) * P, (2 * C + c + 1) * P), h_hi[:, c, :], h_lo[:, c, :],
                                c == 0, c == C - 1)
                    ins.then_inc(down_done, 1)
                    if c == C - 1:
                        pe.wait_ge(down_done, m)
                        pe.sem_inc(d_ready, 1)

                def step(st):
                    if st.has(1):
                        pe.wait_ge(x_lo_done, st.n(1))
                    if routed and st.has(1):
                        pe.wait_ge(comb_done, st.n(1))
                    for q in range(EC):
                        e, c = divmod(q, C)
                        if st.has(1):
                            if isinstance(st.i, int) and st.n(1) == 1 and c == 0:
                                pe.wait_ge(w_done, e + 1)
                            if routed and e and c == 0:
                                k = routed * (st.n(1) - 1) + e
                                wait(pe, cw_done, k - 1)
                                if st.has(0):
                                    wait(pe, shifted, st.n(0) - (0 if q > LG_AT else 1))
                                else:
                                    wait(pe, shifted, st.n(1))
                                for tb in range(TB):
                                    ins = pe.matmul(g.ps[:, R_BANK, tb * P:(tb + 1) * P],
                                                    comb[st.slot(1, 2)][:, tb, e - 1:e].to_broadcast([P, P]),
                                                    g.ident[:], start=True, stop=True)
                                ins.then_inc(cw_ready, 1)
                            gate_up(st, q)
                        if q >= DOWN_LAG and st.has(1):
                            down(st, 1, q - DOWN_LAG)
                        if q < DOWN_LAG and st.has(2):
                            down(st, 2, EC - DOWN_LAG + q)
                        if q == X_AT and st.has(0):
                            pe.wait_ge(xn_done, TB * st.n(0))
                            if st.has(OUT_LAG) or (st.has(OUT_LAG + 1) and OUT_AT >= X_AT):
                                wait(pe, out_added, st.n(OUT_LAG))
                            for tb in range(TB):
                                ins = pe.transpose(g.ps[:, T_BANK, tb * P:(tb + 1) * P], xn[:, tb, :], g.ident[:])
                            ins.then_inc(xp_ready, 1)
                        if routed and q == LG_AT and st.has(0):
                            if st.n(0) == 1 if isinstance(st.i, int) else False:
                                pe.wait_ge(small_loaded, 32)
                            pe.wait_ge(xT_done, st.n(0))
                            if st.has(1):
                                pe.wait_ge(cw_done, routed * (st.n(1) - 1) + q // C)
                            for tb in range(TB):
                                ins = pe.matmul(g.ps[:, R_BANK, tb * 8:tb * 8 + routed], xT[:, tb * P:(tb + 1) * P],
                                                rw[:], start=True, stop=True)
                            ins.then_inc(lg_ready, 1)
                        if q == OUT_AT and st.has(OUT_LAG):
                            if routed:
                                pe.wait_ge(acc_done, routed * st.n(OUT_LAG))
                            else:
                                pe.wait_ge(d_read, st.n(OUT_LAG))
                            if st.has(1):
                                pe.wait_ge(x_lo_done, st.n(1))
                            for tb in range(TB):
                                ins = pe.transpose(g.ps[:, T_BANK, tb * P:(tb + 1) * P], acc[:, tb * P:(tb + 1) * P],
                                                   g.ident[:])
                            ins.then_inc(out_ready, 1)

                run_steps(pe, B, 3, step, U=2)

            @block.scalar
            def _(act):
                def step(st):
                    for q in range(EC):
                        e, c = divmod(q, C)
                        if isinstance(st.i, int) and st.c + 2 * st.i == 2 and c == 0:
                            if quant:
                                act.wait_ge(dequant_done, e + 1)
                            else:
                                act.wait_ge(stage_loaded[e % 2], 16 * (e // 2 + 1))
                            act.activation(w_hi[:, e, :], stage_f[:, e % 2, :], ACT.Copy).then_inc(w_hi_done, 1)
                        if st.has(1):
                            m, par = position(st, 1, q)
                            if routed and e and c == 0:
                                k = routed * (st.n(1) - 1) + e
                                act.wait_ge(cw_ready, k)
                                wait(act, d_read, E * (st.n(1) - 1) + (e - 1 if e > 2 else 0))
                                act.activation(cw[:, e % 2, :], g.ps[:, R_BANK, :], ACT.Copy).then_inc(cw_done, 1)
                            act.wait_ge(gu_ready, m)
                            wait(act, h_done, m - 2)
                            act.activation(gate[:, par, :], g.ps[:, G_BANK + par, :], ACT.Silu).then_inc(gate_done, 1)
                        for k, qq in (((1, q - 1),) if q else ((2, EC - 1),)):
                            if st.has(k):
                                m, _ = position(st, k, qq)
                                act.wait_ge(h_done, m)
                                wait(act, down_done, m - C)
                                act.activation(h_hi[:, qq % C, :], h[:, qq % C, :], ACT.Copy).then_inc(h_hi_done, 1)
                        if q == X_AT and st.has(0):
                            act.wait_ge(xp_ready, st.n(0))
                            if routed:
                                wait(act, lg_ready, st.n(0) - 1)
                                act.activation(xT[:], g.ps[:, T_BANK, :], ACT.Copy).then_inc(xT_done, 1)
                            wait(act, gu_ready, EC * (st.n(0) - 2))
                            act.activation(x_hi[st.slot(0, 2)][:], g.ps[:, T_BANK, :], ACT.Copy).then_inc(x_hi_done, 1)
                        if routed and q == COMB_AT and st.has(0):
                            act.wait_ge(shifted, st.n(0))
                            act.activation(pr[:], pr[:], ACT.Exp).then_inc(p_exp, 1)

                run_steps(act, B, 3, step, U=2)

            @block.vector
            def _(dve):
                def softmax_top2(st, part):
                    n, r = st.n(0), st.slot(0, 2)
                    logits = g.ps[:, R_BANK, 0:TB * 8].rearrange("p (t e) -> p t e", t=TB)[:, :, 0:routed]
                    wide = [P, TB, routed]
                    cube = [P, TB, routed, routed]
                    p_e = pr[:, :, :, None].to_broadcast(cube)
                    p_j = pr[:, :, None, :].to_broadcast(cube)
                    link = Link(dve, chain, n, 12, done=(0, 1, 3, 6, 8, 10, 12)[part])
                    if part == 0:
                        if isinstance(st.i, int) and n == 1:
                            dve.wait_ge(small_loaded, 32)
                        dve.wait_ge(lg_ready, n)
                        link(dve.tensor_reduce(mx[:], logits, AX_X, ALU.max))
                        dve.tensor_tensor(pr[:], logits, mx[:, :, None].to_broadcast(wide), ALU.subtract
                                          ).then_inc(shifted, 1)
                    elif part == 1:
                        dve.wait_ge(p_exp, n)
                        link(dve.tensor_reduce(sm[:], pr[:], AX_X, ALU.add))
                        link(dve.reciprocal(sm[:], sm[:]))
                    elif part == 2:
                        link(dve.tensor_tensor(pr[:], pr[:], sm[:, :, None].to_broadcast(wide), ALU.mult))
                        link(dve.tensor_tensor(eq[:], p_j, p_e, ALU.is_equal))
                        link(dve.tensor_tensor(eq[:], eq[:], lower[:, None, :, :].to_broadcast(cube), ALU.mult))
                    elif part == 3:
                        link(dve.tensor_tensor(gt[:], p_j, p_e, ALU.is_gt))
                        link(dve.tensor_tensor(gt[:], gt[:], eq[:], ALU.add))
                    elif part == 4:
                        link(dve.tensor_reduce(sel[:], gt[:], AX_X, ALU.add))
                        link(dve.scalar_tensor_tensor(pr[:], sel[:], 2.0, pr[:], ALU.is_lt, ALU.mult))
                    elif part == 5:
                        link(dve.tensor_reduce(sm[:], pr[:], AX_X, ALU.add))
                        link(dve.tensor_scalar(sm[:], sm[:], 1e-9, None, ALU.add))
                        dve.reciprocal(mx[:], sm[:]).then_inc(recip_done, 1)
                    else:
                        dve.wait_ge(recip_done, n)
                        wait(dve, cw_ready, routed * (n - 2))
                        dve.tensor_tensor(comb[r][:], pr[:], mx[:, :, None].to_broadcast(wide), ALU.mult
                                          ).then_inc(comb_done, 1)

                def add_up(st, k, e):
                    n = st.n(k)
                    bank = g.ps[:, D_BANK + (E * (st.c - k - 1) + e) % 2, :]
                    dve.wait_ge(d_ready, E * (n - 1) + e + 1)
                    if e == 0:
                        wait(dve, out_ready, n - 1)
                        dve.tensor_copy(acc[:], bank).then_inc(d_read, 1)
                        return
                    dve.wait_ge(cw_done, routed * (n - 1) + e)
                    wait(dve, acc_done, routed * (n - 1) + e - 1)
                    dve.tensor_tensor(part[:], bank, cw[:, e % 2, :], ALU.mult).then_inc(d_read, 1)
                    dve.wait_ge(d_read, E * (n - 1) + e + 1)
                    dve.tensor_tensor(acc[:], acc[:], part[:], ALU.add).then_inc(acc_done, 1)

                def step(st):
                    if isinstance(st.i, int) and st.i == 0 and st.c == 1 and quant:
                        dve.wait_ge(stage_loaded[0], 16)
                        dve.tensor_scalar(stage_f[:, 0, :], stage[:, 0, :], float(np.float32(1.0 / 127.0)), None,
                                          ALU.mult).then_inc(dequant_done, 1)
                    for q in range(EC):
                        e, c = divmod(q, C)
                        if isinstance(st.i, int) and st.c + 2 * st.i == 2 and c == 0:
                            dve.wait_ge(w_hi_done, e + 1)
                            dve.tensor_tensor(w_lo[:, e, :], stage_f[:, e % 2, :], w_hi[:, e, :].bitcast(F32),
                                              ALU.subtract).then_inc(w_done, 1)
                        if st.has(1):
                            m, par = position(st, 1, q)
                            dve.wait_ge(gate_done, m)
                            wait(dve, h_lo_done, m - C)
                            dve.tensor_tensor(h[:, c, :], gate[:, par, :], g.ps[:, U_BANK + par, :], ALU.mult
                                              ).then_inc(h_done, 1)
                        for k, qq in (((1, q - 1),) if q else ((2, EC - 1),)):
                            if st.has(k):
                                m, _ = position(st, k, qq)
                                dve.wait_ge(h_hi_done, m)
                                dve.tensor_tensor(h_lo[:, qq % C, :], h[:, qq % C, :],
                                                  h_hi[:, qq % C, :].bitcast(F32), ALU.subtract).then_inc(h_lo_done, 1)
                        for e2 in range(E):
                            at = C * e2 + C + DOWN_LAG
                            if at == q and st.has(1):
                                add_up(st, 1, e2)
                            if at - EC == q and st.has(2):
                                add_up(st, 2, e2)
                        if q == OUT_AT + 1 and st.has(OUT_LAG):
                            dve.wait_ge(out_ready, st.n(OUT_LAG))
                            dst = batch_of(g.x_all, st.n(OUT_LAG))
                            dve.tensor_tensor(dst, g.ps[:, T_BANK, :].rearrange("p (t d) -> p t d", t=TB), dst,
                                              ALU.add).then_inc(out_added, 1)
                        if q == OUT_AT + 2 and st.has(OUT_LAG):
                            dve.wait_ge(out_added, st.n(OUT_LAG))
                            settle(dve, stats_settled)
                            for tb in range(TB):
                                tile = (st.n(OUT_LAG) - 1) * TB + tb
                                dve.bn_stats(stats[:, bass.ds(tile, 1), :].rearrange("p a n -> p (a n)"),
                                             g.x_all[:, bass.ds(tile, 1), :].rearrange("p a n -> p (a n)")
                                             ).then_inc(stats_done, 1)
                        if q == X_AT - 1 and st.has(0):
                            wait(dve, xp_ready, st.n(0) - 1)
                            normalise(dve, g.x_all, g.mean_var, g.rstd, st.n(0), xn, xn_done)
                        if q == X_AT and st.has(0):
                            dve.wait_ge(x_hi_done, st.n(0))
                            dve.tensor_tensor(x_lo[st.slot(0, 2)][:], g.ps[:, T_BANK, :],
                                              x_hi[st.slot(0, 2)][:].bitcast(F32), ALU.subtract).then_inc(x_lo_done, 1)
                        if routed and COMB_AT <= q < COMB_AT + 7 and st.has(0):
                            softmax_top2(st, q - COMB_AT)

                run_steps(dve, B, 3, step, U=2)
                dve.wait_ge(stats_done, TILES)


class Memory:
    pass


def build(nc, a, out, layers=range(8)):
    g = Memory()
    dram = lambda name, shape: nc.dram_tensor(name, shape, F32).ap()
    g.q_hi8, g.q_lo8, g.k_hi8, g.k_lo8 = (dram(k, [B * P, S]) for k in ("q_hi8", "q_lo8", "k_hi8", "k_lo8"))
    g.v8 = dram("v8", [B * 4, S, P])
    g.o8 = dram("o8", [B * 4, TB, P, 32])
    g.y_dram = dram("y_dram", [B, P, S])
    g.lines = dram("lines", [16, BIAS_LINE])
    g.decay = a["decay_strip"]
    g.w_qkv, g.b_out = a["b0_wqkv"], a["b0_bout"]
    g.w_out32 = [a["b0_wout"][k * P:(k + 1) * P, :] for k in range(8)]
    with ExitStack() as stack:
        sb = lambda name, shape, dt=F32: stack.enter_context(nc.sbuf_tensor(name, shape, dt))
        g.ps = stack.enter_context(nc.psum_tensor("ps", [P, 8, 512], F32))
        g.x_all = sb("x_all", [P, TILES, DM])
        g.mean_var = sb("mean_var", [P, TILES, 2])
        g.rstd = sb("rstd", [P, TILES])
        g.ident = sb("ident", [P, P])
        x_tiles = a["x"].rearrange("(t p) d -> p t d", p=P)
        with Phase(nc, "begin") as ph:
            loaded = ph.sem("loaded")
            with nc.Block() as block:
                @block.sync
                def _(sp):
                    sp.dma_start(g.x_all[:], x_tiles).then_inc(loaded, 16)
                    sp.dma_start(g.ident[:], a["ident"]).then_inc(loaded, 16)
                    sp.wait_ge(loaded, 32)

        g.stats_ready = False
        if 0 in layers:
            row_stats(nc, "st_a0", g.x_all, g.mean_var, g.rstd, 1e-5)
            scale = float(np.float32(1.0) / (np.sqrt(np.float32(DM)) + np.float32(1e-8)))
            project_small(nc, g, "in_a0", scale, (a["a0_wdown"], a["a0_wupk"], a["a0_wupv"]),
                          (a["a0_wq"], a["a0_wk"], a["a0_wv"]))
            attend_small(nc, g, "at_a0", True)
            project_out(nc, g, "out_a0", a["a0_wo"])

        def row_stats_of(name):
            if not g.stats_ready:
                row_stats(nc, f"st_{name}", g.x_all, g.mean_var, g.rstd, 1e-5)
            g.stats_ready = False

        def swiglu_layer(name, *args):
            row_stats_of(name)
            with nc.sbuf_tensor(f"stats_{name}", [P, TILES, 6], F32) as stats:
                swiglu(nc, g, name, *args[:3], stats, *args[3:])
                if name != "ffn7":
                    row_stats(nc, f"st_after_{name}", g.x_all, g.mean_var, g.rstd, 1e-5, stats)
                    g.stats_ready = True

        def mixture(k):
            swiglu_layer(f"moe{k}", a["moe_w"], EXPERTS, DFF // P, (a["router"], a["lower"]))

        def quantised(k):
            swiglu_layer(f"ffn{k}", a["ffn_w"], 1, HID // P)

        if 1 in layers:
            mixture(1)
        if 2 in layers:
            row_stats_of("b0")
            attend_wide(nc, g, "at_b0", 32 ** -0.5)
            add_normalised(nc, g, "ln_b0", g.y_dram, a["b0_gamma"], a["b0_beta"], 1e-6)
        if 3 in layers:
            mixture(3)
        if 4 in layers:
            with nc.sbuf_tensor("flip", [P, P], F32) as g.flip:
                bias_lines(nc, g, "bias_a1", a["taps"], a["line_table"], a["wpos"], a["flip"])
                row_stats_of("a1")
                project_small(nc, g, "in_a1", 8 ** -0.5, None, [a["a1_wqkv"][:, k * P:(k + 1) * P] for k in range(3)])
                attend_small(nc, g, "at_a1", False)
                project_out(nc, g, "out_a1", a["a1_wo"])
        if 5 in layers:
            quantised(5)
        if 6 in layers:
            row_stats_of("lin")
            linear_attention(nc, g, "lin", {k[4:]: v for k, v in a.items() if k.startswith("lin_")})
            add_normalised(nc, g, "ln_lin", g.y_dram, a["ln_gamma"], a["ln_beta"], 1e-5)
        if 7 in layers:
            quantised(7)
        with Phase(nc, "end") as ph:
            stored = ph.sem("stored")
            with nc.Block() as block:
                @block.sync
                def _(sp):
                    sp.dma_start(out.rearrange("(t p) d -> p t d", p=P), g.x_all[:]).then_inc(stored, 16)
                    sp.wait_ge(stored, 16)


def pack(gate, up, down):
    import numpy as np
    chunks = down.T.reshape(-1, 128, 128)
    return np.concatenate([gate.T, up.T, *chunks], axis=1)


def line_table():
    import numpy as np
    ramp = np.linspace(0.0, 1.0, 64, dtype=np.float32)
    rel = np.abs(np.arange(1024) - 511).astype(np.float32) / np.float32(511)
    point = np.clip(np.round(rel * np.float32(63)).astype(np.int64), 0, 63)
    at = point[None, :] - np.arange(101)[:, None]
    return np.where(at >= 0, ramp[np.maximum(at, 0)], np.float32(0)).astype(np.float32)


def wide_columns(w):
    import numpy as np
    qk = w[:, :2048].reshape(128, 16, 4, 32).transpose(0, 1, 3, 2).reshape(128, 2048)
    return np.concatenate([qk, w[:, 2048:]], axis=1)


def linear_layouts(f):
    import numpy as np
    row = np.arange(128)
    h, d = row // 4, row % 4
    m, hm = np.arange(64) // 32, np.arange(64) % 32
    pad = lambda t: np.concatenate([t, np.zeros_like(t)], axis=0)
    wq, wk, wv, wb, wm = (f[f"L1_attn_b_{k}"] for k in ("Wq", "Wk", "Wv", "Wbeta", "Wmix"))
    bb, bm = f["L1_attn_b_bbeta"], f["L1_attn_b_bmix"]
    swap = 4 * h + (d + 2) % 4
    w = [wq, wq[swap], wk, wk[swap], wb[2 * h], wb[2 * h + 1], pad(wm[2 * hm + m]), pad(wm[2 * hm + 1 - m])]
    w += [wv[4 * h + c] for c in range(4)]
    freq = np.where(d % 2 == 0, np.float32(1.0), np.float32(1.0) / np.float32(10000.0) ** np.float32(0.5))
    angle = np.arange(512, dtype=np.float32)[None, :] * freq.astype(np.float32)[:, None]
    sign = np.where(d < 2, np.float32(-1), np.float32(1))[:, None]
    one = np.float32(1)
    return {
        "lin_w": np.stack(w).transpose(2, 0, 1),
        "lin_w_out": f["L1_attn_b_Wout"].T, "lin_bout": f["L1_attn_b_bout"],
        "lin_bias": np.stack([bb[2 * h], bb[2 * h + 1], pad(bm[2 * hm + m]), pad(bm[2 * hm + 1 - m])], axis=1),
        "lin_rope": np.stack([np.cos(angle), np.sin(angle) * sign], axis=1).astype(np.float32),
        "lin_to_c": ((h[:, None, None] == h) & (np.arange(4)[:, None] == d)) * one,
        "lin_to_m": ((h[:, None, None] == hm) & (np.arange(2)[:, None] == m)) * one,
        "lin_from_m": np.stack([pad(((hm[:, None] == h) & (m[:, None] == k)) * one) for k in range(2)], axis=1),
        "ln_gamma": f["L1_attn_b_ln_g"], "ln_beta": f["L1_attn_b_ln_b"],
    }


def laid_out(i):
    import numpy as np
    f = {k: np.asarray(v) for k, v in i.items()}
    p = np.arange(128)[:, None]
    strip_delta = np.abs(np.arange(896)[None, :] - p - 384).astype(np.float32)
    d = {
        "x": f["L0_attn_a_x"].reshape(-1, 128),
        "ident": np.eye(128, dtype=np.float32), "flip": np.eye(128, dtype=np.float32)[::-1],
        "decay_strip": np.exp(np.float32(-0.01 * 0.01) * strip_delta).astype(np.float32),
        "a0_wq": f["L0_attn_a_Wq"], "a0_wk": f["L0_attn_a_Wk"], "a0_wv": f["L0_attn_a_Wv"],
        "a0_wo": f["L0_attn_a_Wo"], "a0_wdown": f["L0_attn_a_W_down_kv"],
        "a0_wupk": f["L0_attn_a_W_up_k"], "a0_wupv": f["L0_attn_a_W_up_v"],
        "a1_wo": f["L1_attn_a_Wout"].T, "a1_wqkv": f["L1_attn_a_Wqkv"].T,
        "taps": f["L1_attn_a_coeffs"].T, "wpos": f["L1_attn_a_Wpos"].T,
        "line_table": line_table(),
        "b0_wqkv": wide_columns(f["L0_attn_b_w_qkv"]), "b0_wout": f["L0_attn_b_w_out"], "b0_bout": f["L0_attn_b_b_out"],
        "b0_gamma": f["L0_attn_b_ln_gamma"], "b0_beta": f["L0_attn_b_ln_beta"],
        "moe_w": np.stack([pack(*w) for w in [
            (f["L0_ffn_shared_gate"], f["L0_ffn_shared_up"], f["L0_ffn_shared_down"]),
            *zip(f["L0_ffn_routed_gate"], f["L0_ffn_routed_up"], f["L0_ffn_routed_down"])]]),
        "router": f["L0_ffn_router_w"].T,
        "lower": np.tril(np.ones((7, 7), np.float32), -1),
        "ffn_w": pack(f["L1_ffn_w_gate"], f["L1_ffn_w_up"], f["L1_ffn_w_down"])[None],
    }
    d.update(linear_layouts(f))
    return {k: np.ascontiguousarray(v) for k, v in d.items()}


def kernel(**inputs):
    import concourse.bacc as _bacc
    from concourse import mybir as _mybir
    from concourse.bass_utils import run_bass_kernel_spmd as _run

    nc = _bacc.Bacc("TRN2", target_bir_lowering=False, num_devices=1)
    arrays = laid_out(inputs)
    a = {k: nc.dram_tensor(f"in_{k}", v.shape, _mybir.dt.from_np(v.dtype), kind="ExternalInput").ap()
         for k, v in arrays.items()}
    out = nc.dram_tensor("out", (8 * 512, 128), _mybir.dt.float32, kind="ExternalOutput").ap()
    build(nc, a, out)
    r = _run(nc, [{f"in_{k}": v for k, v in arrays.items()}], core_ids=[0])
    return r.results[0]["out"].reshape(8, 512, 128)
```
